# Optimizing a Trainium2 kernel written in Bass

```python
import numpy as np
import jax
import jax.numpy as jnp

def _softmax(x, axis=-1):
    return jax.nn.softmax(x, axis=axis)

def _gelu(x):
    return jax.nn.gelu(x, approximate=True)

def _silu(x):
    return jax.nn.silu(x)

def _sigmoid(x):
    return jax.nn.sigmoid(x)

def _layernorm(x, axis=-1, eps=1e-05):
    m = jnp.mean(x, axis=axis, keepdims=True)
    v = jnp.var(x, axis=axis, keepdims=True)
    return (x - m) / jnp.sqrt(v + eps)

def _scatter_add(tgt, idx, src, axis=0):
    return tgt.at[idx].add(src)

def _segment_sum(src, seg, n):
    return jax.ops.segment_sum(src, seg, n)
kernel_name = 'mk_cond_seq_d4_seqx_r2_e51ad2'

def setup_inputs(seed: int=0):
    np.random.seed(seed)
    _w = jnp.asarray

    def _rec_inputs():
        import jax
        import jax.numpy as jnp
        _rk = jax.random.key(seed)
        x = -0.0005207 + 1.001 * jax.random.normal(jax.random.fold_in(_rk, 1), (2, 2048, 512), jnp.float32)
        _lenS = 2048 - jax.random.randint(jax.random.fold_in(_rk, 7), (2,), 0, max(1, 2048 // 4) + 1, jnp.int32)
        _lenS2 = 2048 - jax.random.randint(jax.random.fold_in(_rk, 8), (2,), 0, max(1, 2048 // 4) + 1, jnp.int32)
        itok_B_34_63 = jax.random.randint(jax.random.fold_in(_rk, 12), (2,), 34, 64, jnp.int32)
        fside_Bx16xSxS_0 = -1.47943e-05 + 1.00017 * jax.random.normal(jax.random.fold_in(_rk, 13), (2, 16, 2048, 2048), jnp.float32)
        itok_B_0_15 = jax.random.randint(jax.random.fold_in(_rk, 14), (2,), 0, 16, jnp.int32)
        condB_theta = jax.random.uniform(jax.random.fold_in(_rk, 15), (2,), jnp.float32, 0.0, 0.983423)
        condB_phi = jax.random.uniform(jax.random.fold_in(_rk, 16), (2,), jnp.float32, 0.0, 0.961312)
        itok_B_0_2 = jax.random.randint(jax.random.fold_in(_rk, 17), (2,), 0, 3, jnp.int32)
        _validS = jnp.arange(2048)[None, :] < _lenS[:, None]
        _validS2 = jnp.arange(2048)[None, :] < _lenS2[:, None]
        _causal = jnp.tril(jnp.ones((2048, 2048), dtype=bool))
        mask_Bx1xSxS_bk0 = jnp.logical_not(jnp.broadcast_to(_validS[:, None, None, :], (2, 1, 2048, 2048)))
        return (x, itok_B_34_63, fside_Bx16xSxS_0, itok_B_0_15, condB_theta, condB_phi, itok_B_0_2, mask_Bx1xSxS_bk0)
    x, itok_B_34_63, fside_Bx16xSxS_0, itok_B_0_15, condB_theta, condB_phi, itok_B_0_2, mask_Bx1xSxS_bk0 = _rec_inputs()

    def _L0_cond_setup():
        import jax, jax.numpy as jnp
        import numpy as np
        import math
        D_MODEL = 512
        N_HEAD = 16
        HEAD_DIM = D_MODEL // N_HEAD
        D_FF = 2048
        NUM_STEPS = 100.0
        RESCALE = 4000.0
        EPS = 1e-05

        def _sin_emb(t):
            half = D_MODEL // 2
            x = t.astype(jnp.float32) / NUM_STEPS * RESCALE
            freqs = jnp.exp(jnp.arange(half, dtype=jnp.float32) * (-math.log(10000.0) / (half - 1)))
            e = x[:, None] * freqs[None, :]
            return jnp.concatenate([jnp.sin(e), jnp.cos(e)], axis=-1)

        def _ln(x):
            m = jnp.mean(x, axis=-1, keepdims=True)
            v = jnp.var(x, axis=-1, keepdims=True)
            return (x - m) / jnp.sqrt(v + EPS)

        def _gelu2(x):
            return x * jax.nn.sigmoid(1.702 * x)
        key = jax.random.key(seed)
        ks = jax.random.split(key, 24)
        B, S, D, F = (4, 256, D_MODEL, D_FF)
        std = 0.02
        inp = {'src': jax.random.normal(ks[0], (B, S, D), dtype=jnp.float32), 'src_mask': jax.random.randint(ks[1], (B, 1, S, S), 0, 2).astype(bool), 'timestep': jax.random.randint(ks[2], (B,), 0, 100, dtype=jnp.int32), 'attention_bias': jax.random.normal(ks[3], (B, N_HEAD, S, S), dtype=jnp.float32), 'W_ada': jax.random.normal(ks[4], (D, 2 * D), dtype=jnp.float32) * std, 'b_ada': jnp.zeros((2 * D,), dtype=jnp.float32), 'Wq': jax.random.normal(ks[5], (D, D), dtype=jnp.float32) * std, 'bq': jnp.zeros((D,), dtype=jnp.float32), 'Wk': jax.random.normal(ks[6], (D, D), dtype=jnp.float32) * std, 'bk': jnp.zeros((D,), dtype=jnp.float32), 'Wv': jax.random.normal(ks[7], (D, D), dtype=jnp.float32) * std, 'bv': jnp.zeros((D,), dtype=jnp.float32), 'Wo': jax.random.normal(ks[8], (D, D), dtype=jnp.float32) * std, 'bo': jnp.zeros((D,), dtype=jnp.float32), 'W1': jax.random.normal(ks[9], (D, F), dtype=jnp.float32) * std, 'b1': jnp.zeros((F,), dtype=jnp.float32), 'W2': jax.random.normal(ks[10], (F, D), dtype=jnp.float32) * std, 'b2': jnp.zeros((D,), dtype=jnp.float32), 'g2': jnp.ones((D,), dtype=jnp.float32), 'beta2': jnp.zeros((D,), dtype=jnp.float32)}
        return inp
    _L0_cond_all = _L0_cond_setup()
    _L0_cond_in = {k: v for k, v in _L0_cond_all.items() if k in ('W_ada', 'b_ada', 'Wq', 'bq', 'Wk', 'bk', 'Wv', 'bv', 'Wo', 'bo', 'W1', 'b1', 'W2', 'b2', 'g2', 'beta2')}
    del _L0_cond_all

    def _L1_cond_setup():
        import jax, jax.numpy as jnp
        import numpy as np
        B, S, D = (32, 512, 512)
        A = 128
        E = 16
        LN_EPS = 1e-05
        key = jax.random.key(seed)
        ks = jax.random.split(key, 10)
        s = lambda fan_in: 1.0 / np.sqrt(fan_in)
        return {'hidden_states': jax.random.normal(ks[0], (B, S, D), dtype=jnp.float32), 'domain_id': jax.random.randint(ks[1], (B,), 0, E, dtype=jnp.int64), 'down_W': jax.random.uniform(ks[2], (A, D), jnp.float32, -s(D), s(D)), 'down_b': jax.random.uniform(ks[3], (A,), jnp.float32, -s(D), s(D)), 'up_W': jax.random.uniform(ks[4], (D, A), jnp.float32, -s(A), s(A)), 'up_b': jax.random.uniform(ks[5], (D,), jnp.float32, -s(A), s(A)), 'expert_W': jax.random.uniform(ks[6], (E, A, A), jnp.float32, -s(A), s(A)), 'expert_b': jax.random.uniform(ks[7], (E, A), jnp.float32, -s(A), s(A)), 'domain_emb': jax.random.normal(ks[8], (E, A), dtype=jnp.float32), 'ln_gamma': jnp.ones((D,), jnp.float32), 'ln_beta': jnp.zeros((D,), jnp.float32)}
    _L1_cond_all = _L1_cond_setup()
    _L1_cond_in = {k: v for k, v in _L1_cond_all.items() if k in ('down_W', 'down_b', 'up_W', 'up_b', 'expert_W', 'expert_b', 'domain_emb', 'ln_gamma', 'ln_beta')}
    del _L1_cond_all

    def _L2_cond_setup():
        import jax, jax.numpy as jnp
        import numpy as np
        key = jax.random.key(seed)
        k1, k2, k3 = jax.random.split(key, 3)
        B, N, D = (16, 2048, 512)
        embeddings = jax.random.normal(k1, (B, N, D), dtype=jnp.float32)
        theta = jax.random.uniform(k2, (B,), dtype=jnp.float32)
        phi = jax.random.uniform(k3, (B,), dtype=jnp.float32)
        return {'embeddings': embeddings, 'theta': theta, 'phi': phi}
    _L2_cond_all = _L2_cond_setup()
    _L2_cond_in = {k: v for k, v in _L2_cond_all.items() if k in ()}
    del _L2_cond_all

    def _L3_cond_setup():
        import jax, jax.numpy as jnp
        import numpy as np
        H = 512
        EPS = 1e-05

        def _gelu(x):
            return jax.nn.gelu(x, approximate=False)
        key = jax.random.key(seed)
        ks = jax.random.split(key, 16)
        s = 1.0 / np.sqrt(H)
        inp = {'x': jax.random.normal(ks[0], (64, 512, H), dtype=jnp.float32), 'condition': jax.random.randint(ks[1], (64,), 0, 3), 'w1_nr': jax.random.normal(ks[2], (H, H), dtype=jnp.float32) * s, 'b1_nr': jnp.zeros((H,), dtype=jnp.float32), 'w2_nr': jax.random.normal(ks[3], (H, H), dtype=jnp.float32) * s, 'b2_nr': jnp.zeros((H,), dtype=jnp.float32), 'w1_tsr': jax.random.normal(ks[4], (H, H), dtype=jnp.float32) * s, 'b1_tsr': jnp.zeros((H,), dtype=jnp.float32), 'w2_tsr': jax.random.normal(ks[5], (H, H), dtype=jnp.float32) * s, 'b2_tsr': jnp.zeros((H,), dtype=jnp.float32), 'w1_sr': jax.random.normal(ks[6], (H, 2 * H), dtype=jnp.float32) * s, 'b1_sr': jnp.zeros((2 * H,), dtype=jnp.float32), 'w2_sr': jax.random.normal(ks[7], (2 * H, H), dtype=jnp.float32) * (1.0 / np.sqrt(2 * H)), 'b2_sr': jnp.zeros((H,), dtype=jnp.float32), 'w3_sr': jax.random.normal(ks[8], (H, H), dtype=jnp.float32) * s, 'b3_sr': jnp.zeros((H,), dtype=jnp.float32), 'gamma': jnp.ones((H,), dtype=jnp.float32), 'beta': jnp.zeros((H,), dtype=jnp.float32)}
        return inp
    _L3_cond_all = _L3_cond_setup()
    _L3_cond_in = {k: v for k, v in _L3_cond_all.items() if k in ('w1_nr', 'b1_nr', 'w2_nr', 'b2_nr', 'w1_tsr', 'b1_tsr', 'w2_tsr', 'b2_tsr', 'w1_sr', 'b1_sr', 'w2_sr', 'b2_sr', 'w3_sr', 'b3_sr', 'gamma', 'beta')}
    del _L3_cond_all
    return {'x': x, 'itok_B_34_63': itok_B_34_63, 'fside_Bx16xSxS_0': fside_Bx16xSxS_0, 'itok_B_0_15': itok_B_0_15, 'condB_theta': condB_theta, 'condB_phi': condB_phi, 'itok_B_0_2': itok_B_0_2, 'mask_Bx1xSxS_bk0': mask_Bx1xSxS_bk0, 'L0_cond_W_ada': _L0_cond_in['W_ada'], 'L0_cond_b_ada': _L0_cond_in['b_ada'], 'L0_cond_Wq': _L0_cond_in['Wq'], 'L0_cond_bq': _L0_cond_in['bq'], 'L0_cond_Wk': _L0_cond_in['Wk'], 'L0_cond_bk': _L0_cond_in['bk'], 'L0_cond_Wv': _L0_cond_in['Wv'], 'L0_cond_bv': _L0_cond_in['bv'], 'L0_cond_Wo': _L0_cond_in['Wo'], 'L0_cond_bo': _L0_cond_in['bo'], 'L0_cond_W1': _L0_cond_in['W1'], 'L0_cond_b1': _L0_cond_in['b1'], 'L0_cond_W2': _L0_cond_in['W2'], 'L0_cond_b2': _L0_cond_in['b2'], 'L0_cond_g2': _L0_cond_in['g2'], 'L0_cond_beta2': _L0_cond_in['beta2'], 'L1_cond_down_W': _L1_cond_in['down_W'], 'L1_cond_down_b': _L1_cond_in['down_b'], 'L1_cond_up_W': _L1_cond_in['up_W'], 'L1_cond_up_b': _L1_cond_in['up_b'], 'L1_cond_expert_W': _L1_cond_in['expert_W'], 'L1_cond_expert_b': _L1_cond_in['expert_b'], 'L1_cond_domain_emb': _L1_cond_in['domain_emb'], 'L1_cond_ln_gamma': _L1_cond_in['ln_gamma'], 'L1_cond_ln_beta': _L1_cond_in['ln_beta'], 'L3_cond_w1_nr': _L3_cond_in['w1_nr'], 'L3_cond_b1_nr': _L3_cond_in['b1_nr'], 'L3_cond_w2_nr': _L3_cond_in['w2_nr'], 'L3_cond_b2_nr': _L3_cond_in['b2_nr'], 'L3_cond_w1_tsr': _L3_cond_in['w1_tsr'], 'L3_cond_b1_tsr': _L3_cond_in['b1_tsr'], 'L3_cond_w2_tsr': _L3_cond_in['w2_tsr'], 'L3_cond_b2_tsr': _L3_cond_in['b2_tsr'], 'L3_cond_w1_sr': _L3_cond_in['w1_sr'], 'L3_cond_b1_sr': _L3_cond_in['b1_sr'], 'L3_cond_w2_sr': _L3_cond_in['w2_sr'], 'L3_cond_b2_sr': _L3_cond_in['b2_sr'], 'L3_cond_w3_sr': _L3_cond_in['w3_sr'], 'L3_cond_b3_sr': _L3_cond_in['b3_sr'], 'L3_cond_gamma': _L3_cond_in['gamma'], 'L3_cond_beta': _L3_cond_in['beta']}

def reference(x, itok_B_34_63, fside_Bx16xSxS_0, itok_B_0_15, condB_theta, condB_phi, itok_B_0_2, mask_Bx1xSxS_bk0, L0_cond_W_ada, L0_cond_b_ada, L0_cond_Wq, L0_cond_bq, L0_cond_Wk, L0_cond_bk, L0_cond_Wv, L0_cond_bv, L0_cond_Wo, L0_cond_bo, L0_cond_W1, L0_cond_b1, L0_cond_W2, L0_cond_b2, L0_cond_g2, L0_cond_beta2, L1_cond_down_W, L1_cond_down_b, L1_cond_up_W, L1_cond_up_b, L1_cond_expert_W, L1_cond_expert_b, L1_cond_domain_emb, L1_cond_ln_gamma, L1_cond_ln_beta, L3_cond_w1_nr, L3_cond_b1_nr, L3_cond_w2_nr, L3_cond_b2_nr, L3_cond_w1_tsr, L3_cond_b1_tsr, L3_cond_w2_tsr, L3_cond_b2_tsr, L3_cond_w1_sr, L3_cond_b1_sr, L3_cond_w2_sr, L3_cond_b2_sr, L3_cond_w3_sr, L3_cond_b3_sr, L3_cond_gamma, L3_cond_beta):
    import jax
    import jax.numpy as jnp

    def _L0_cond_ref(src, src_mask, timestep, attention_bias, W_ada, b_ada, Wq, bq, Wk, bk, Wv, bv, Wo, bo, W1, b1, W2, b2, g2, beta2):
        import jax, jax.numpy as jnp
        import numpy as np
        import math
        D_MODEL = 512
        N_HEAD = 16
        HEAD_DIM = D_MODEL // N_HEAD
        D_FF = 2048
        NUM_STEPS = 100.0
        RESCALE = 4000.0
        EPS = 1e-05

        def _sin_emb(t):
            half = D_MODEL // 2
            x = t.astype(jnp.float32) / NUM_STEPS * RESCALE
            freqs = jnp.exp(jnp.arange(half, dtype=jnp.float32) * (-math.log(10000.0) / (half - 1)))
            e = x[:, None] * freqs[None, :]
            return jnp.concatenate([jnp.sin(e), jnp.cos(e)], axis=-1)

        def _ln(x):
            m = jnp.mean(x, axis=-1, keepdims=True)
            v = jnp.var(x, axis=-1, keepdims=True)
            return (x - m) / jnp.sqrt(v + EPS)

        def _gelu2(x):
            return x * jax.nn.sigmoid(1.702 * x)
        B, S, D = src.shape
        emb = jax.nn.silu(_sin_emb(timestep)) @ W_ada + b_ada
        scale, shift = jnp.split(emb[:, None, :], 2, axis=-1)
        x = _ln(src) * (1.0 + scale) + shift
        q = (x @ Wq + bq).reshape(B, S, N_HEAD, HEAD_DIM).transpose(0, 2, 1, 3)
        k = (x @ Wk + bk).reshape(B, S, N_HEAD, HEAD_DIM).transpose(0, 2, 1, 3)
        v = (x @ Wv + bv).reshape(B, S, N_HEAD, HEAD_DIM).transpose(0, 2, 1, 3)
        scores = jnp.einsum('bhqd,bhkd->bhqk', q / math.sqrt(HEAD_DIM), k)
        scores = scores + attention_bias
        scores = jnp.where(src_mask, -jnp.inf, scores.astype(jnp.float32))
        probs = jax.nn.softmax(scores, axis=-1).astype(v.dtype)
        ctx = jnp.einsum('bhqk,bhkd->bhqd', probs, v)
        ctx = ctx.transpose(0, 2, 1, 3).reshape(B, S, D)
        x = x + (ctx @ Wo + bo)
        h = _ln(x) * g2 + beta2
        ff = _gelu2(h @ W1 + b1) @ W2 + b2
        return x + ff

    def _L1_cond_ref(hidden_states, domain_id, down_W, down_b, up_W, up_b, expert_W, expert_b, domain_emb, ln_gamma, ln_beta):
        import jax, jax.numpy as jnp
        import numpy as np
        B, S, D = (32, 512, 512)
        A = 128
        E = 16
        LN_EPS = 1e-05
        residual = hidden_states
        hidden = jnp.einsum('bsd,ad->bsa', hidden_states, down_W) + down_b
        hidden = jax.nn.gelu(hidden, approximate=False)
        valid = (domain_id >= 0) & (domain_id < E)
        idx = jnp.clip(domain_id, 0, E - 1)
        Wsel = expert_W[idx]
        bsel = expert_b[idx]
        expert_out = jnp.einsum('bsa,boa->bso', hidden, Wsel) + bsel[:, None, :]
        domain_output = jnp.where(valid[:, None, None], expert_out, hidden)
        hidden = domain_output + domain_emb[idx][:, None, :]
        hidden = jnp.einsum('bsa,da->bsd', hidden, up_W) + up_b
        x = hidden + residual
        mu = jnp.mean(x, axis=-1, keepdims=True)
        var = jnp.mean(jnp.square(x - mu), axis=-1, keepdims=True)
        return (x - mu) * jax.lax.rsqrt(var + LN_EPS) * ln_gamma + ln_beta

    def _L2_cond_ref(embeddings, theta, phi):
        import jax, jax.numpy as jnp
        import numpy as np
        B, N, D = embeddings.shape
        e = embeddings.reshape(B, N, D // 4, 4)
        ct = jnp.cos(theta)[:, None, None]
        st = jnp.sin(theta)[:, None, None]
        cp = jnp.cos(phi)[:, None, None]
        sp = jnp.sin(phi)[:, None, None]
        x0, x1, x2, x3 = (e[..., 0], e[..., 1], e[..., 2], e[..., 3])
        out = jnp.stack([x0 * ct + x1 * st, -x0 * st + x1 * ct, x2 * cp + x3 * sp, -x2 * sp + x3 * cp], axis=-1)
        return out.reshape(B, N, D)

    def _L3_cond_ref(x, condition, w1_nr, b1_nr, w2_nr, b2_nr, w1_tsr, b1_tsr, w2_tsr, b2_tsr, w1_sr, b1_sr, w2_sr, b2_sr, w3_sr, b3_sr, gamma, beta):
        import jax, jax.numpy as jnp
        import numpy as np
        H = 512
        EPS = 1e-05

        def _gelu(x):
            return jax.nn.gelu(x, approximate=False)
        out_nr = _gelu(jnp.einsum('bth,hk->btk', x, w1_nr) + b1_nr)
        out_nr = jnp.einsum('bth,hk->btk', out_nr, w2_nr) + b2_nr
        out_tsr = _gelu(jnp.einsum('bth,hk->btk', x, w1_tsr) + b1_tsr)
        out_tsr = jnp.einsum('bth,hk->btk', out_tsr, w2_tsr) + b2_tsr
        h = _gelu(jnp.einsum('bth,hk->btk', x, w1_sr) + b1_sr)
        h = _gelu(jnp.einsum('bth,hk->btk', h, w2_sr) + b2_sr)
        out_sr = jnp.einsum('bth,hk->btk', h, w3_sr) + b3_sr
        c = condition[:, None, None]
        out = jnp.where(c == 0, out_nr, jnp.where(c == 1, out_tsr, jnp.where(c == 2, out_sr, jnp.zeros_like(x))))
        y = x + out
        mu = jnp.mean(y, axis=-1, keepdims=True)
        var = jnp.mean((y - mu) ** 2, axis=-1, keepdims=True)
        return (y - mu) * jax.lax.rsqrt(var + EPS) * gamma + beta
    x = _L0_cond_ref(x, mask_Bx1xSxS_bk0, itok_B_34_63, fside_Bx16xSxS_0, L0_cond_W_ada, L0_cond_b_ada, L0_cond_Wq, L0_cond_bq, L0_cond_Wk, L0_cond_bk, L0_cond_Wv, L0_cond_bv, L0_cond_Wo, L0_cond_bo, L0_cond_W1, L0_cond_b1, L0_cond_W2, L0_cond_b2, L0_cond_g2, L0_cond_beta2)
    x = _L1_cond_ref(x, itok_B_0_15, L1_cond_down_W, L1_cond_down_b, L1_cond_up_W, L1_cond_up_b, L1_cond_expert_W, L1_cond_expert_b, L1_cond_domain_emb, L1_cond_ln_gamma, L1_cond_ln_beta)
    x = _L2_cond_ref(x, condB_theta, condB_phi)
    x = _L3_cond_ref(x, itok_B_0_2, L3_cond_w1_nr, L3_cond_b1_nr, L3_cond_w2_nr, L3_cond_b2_nr, L3_cond_w1_tsr, L3_cond_b1_tsr, L3_cond_w2_tsr, L3_cond_b2_tsr, L3_cond_w1_sr, L3_cond_b1_sr, L3_cond_w2_sr, L3_cond_b2_sr, L3_cond_w3_sr, L3_cond_b3_sr, L3_cond_gamma, L3_cond_beta)
    return x

_drawn_inputs = setup_inputs


def setup_inputs(seed=0):
    import zlib

    import numpy as np

    out = dict(_drawn_inputs(seed))
    spreads = {'L0_cond_b_ada': (0.0, 0.1),
     'L0_cond_bq': (0.0, 0.8),
     'L0_cond_bk': (0.0, 0.8),
     'L0_cond_bv': (0.0, 0.1),
     'L0_cond_bo': (0.0, 0.1),
     'L0_cond_b1': (0.0, 0.1),
     'L0_cond_b2': (0.0, 0.1),
     'L0_cond_g2': (1.0, 0.2),
     'L0_cond_beta2': (0.0, 0.396),
     'L1_cond_ln_gamma': (1.0, 0.2),
     'L1_cond_ln_beta': (0.0, 0.1),
     'L3_cond_b1_nr': (0.0, 0.1),
     'L3_cond_b2_nr': (0.0, 0.1),
     'L3_cond_b1_tsr': (0.0, 0.1),
     'L3_cond_b2_tsr': (0.0, 0.1),
     'L3_cond_b1_sr': (0.0, 0.1),
     'L3_cond_b2_sr': (0.0, 0.1),
     'L3_cond_b3_sr': (0.0, 0.1),
     'L3_cond_gamma': (1.0, 0.2),
     'L3_cond_beta': (0.0, 0.1)}
    factors = {'fside_Bx16xSxS_0': 8.0, 'L0_cond_Wq': 8.0, 'L0_cond_Wk': 8.0, 'L1_cond_down_b': 8.0}
    for name, (base, spread) in spreads.items():
        noise = np.random.default_rng([zlib.crc32(name.encode()), seed]).standard_normal(out[name].shape)
        drawn = base * np.exp(spread * noise) if base else spread * noise
        out[name] = jnp.asarray(drawn.astype(out[name].dtype))
    for name, factor in factors.items():
        out[name] = (out[name] * factor).astype(out[name].dtype)
    return out
```

```python
import math
from contextlib import ExitStack

import numpy as np

import concourse.bass as bass
from concourse import mybir

ALU = mybir.AluOpType
ACT = mybir.ActivationFunctionType
AX = mybir.AxisListType
F32 = mybir.dt.float32
BF16 = mybir.dt.bfloat16
I32 = mybir.dt.int32
U8 = mybir.dt.uint8

P = 128
D = 512
KD = D // P
H = 16
HD = D // H
HV = HD + 1
CH = 512
NS = CH // P
FF = 2048
KF = FF // P
AD = 128
EXPERTS = 16
EPS = 1e-5
BANK = 512
MASKED = -1.0e30
Q_SCALE = 1.0 / math.sqrt(HD)

COLUMNS = {}
_at = 0
for _name, _width in (("b_ada", 2 * D), ("bq", D), ("bk", D), ("bv", D), ("b1", FF), ("g2", D), ("beta2", D),
                      ("down_b", AD), ("b1_sr", 2 * D), ("b2_sr", D), ("b1_nr", D), ("b1_tsr", D)):
    COLUMNS[_name] = (_at, _width // P)
    _at += _width // P
N_COLUMNS = _at

TWO_PI_1 = 6.28125
TWO_PI_2 = round((2 * math.pi - TWO_PI_1) * 2.0 ** 21) / 2.0 ** 21
TWO_PI_3 = 2 * math.pi - TWO_PI_1 - TWO_PI_2
ROUND = 1.5 * 2.0 ** 23
PI_INSIDE = 3.1415925


class Steps:

    def __init__(self, sem):
        self.sem, self.n = sem, 0

    def mark(self, instruction):
        instruction.then_inc(self.sem, 1)
        self.n += 1
        return self.n


def wait(engine, sem, value):
    if not isinstance(value, int) or value > 0:
        engine.wait_ge(sem, value)


def turns(engine, count, body):
    body(0, True, count == 1)
    if count > 2:
        with engine.Fori(1, count - 1) as n:
            body(n, False, False)
    if count > 1:
        body(count - 1, False, True)


def wait_apart(engine, sem, value, gate):
    engine.wait_ge(sem, value)
    engine.sem_inc(gate, 1)


def column(cols, name, k):
    at, _ = COLUMNS[name]
    return cols[:, at + k:at + k + 1]


def make_identity(pool, ident, s_zero, s_ident):
    pool.memset(ident[:, :], 0.0).then_inc(s_zero, 1)
    pool.wait_ge(s_zero, 1)
    pool.affine_select(out=ident[:, :], in_=ident[:, :], compare_op=ALU.not_equal, fill=1.0, base=0,
                       pattern=[[-1, P]], channel_multiplier=1).then_inc(s_ident, 1)


def project_phase(nc, S, B, io, xada_dram, q3_dram, k3_dram, v_dram):
    NC = S // CH
    x_tiles = io["x"].rearrange("b (c s p) d -> (b c) p s d", s=NS, p=P)
    xada_tiles = xada_dram.rearrange("(n s p) d -> n p s d", s=NS, p=P)
    q_tiles = q3_dram.rearrange("t (b g p) (c n) -> b g c p t n", b=B, p=P, n=CH)
    k_tiles = k3_dram.rearrange("t (b g p) (c n) -> b g c p t n", b=B, p=P, n=CH)
    v_tiles = v_dram.rearrange("(b h) p (c s) v -> b c s p h v", b=B, s=NS)

    with ExitStack() as ctx:
        sb = lambda name, shape, dt=F32: ctx.enter_context(nc.sbuf_tensor(name, shape, dt))
        sem = lambda name: ctx.enter_context(nc.semaphore(name))

        ident = sb("a_ident", [P, P])
        ones = sb("a_ones", [P, P])
        cols = sb("a_cols", [P, N_COLUMNS])
        freqs = sb("a_freqs", [P, KD])
        step_i = sb("a_step_i", [P, B], I32)
        step_x = sb("a_step_x", [P, 5, B])
        angle = sb("a_angle", [P, 4, KD, B])
        emb = sb("a_emb", [P, 3, KD, B])
        ada = sb("a_ada", [P, 2 * KD, B])
        diag = sb("a_diag", [P, KD, P])
        scale1 = sb("a_scale1", [P, B, D])
        shift = sb("a_shift", [P, B, D])
        w_ada = sb("a_w_ada", [P, KD, 2 * D])
        wq = sb("a_wq", [P, KD, D])
        wk = sb("a_wk", [P, KD, D])
        wv = sb("a_wv", [P, KD, D])
        bqs = sb("a_bqs", [P, KD])
        x_in = sb("a_x_in", [P, NS, D])
        stats = sb("a_stats", [P, NS, 6])
        moments = sb("a_moments", [P, NS, 2])
        dev = sb("a_dev", [P, NS])
        rstd = sb("a_rstd", [P, NS])
        xada = sb("a_xada", [P, NS, D])
        xT = sb("a_xT", [P, KD, CH])
        qk_f32 = sb("a_qk_f32", [P, 2, CH])
        rest = sb("a_rest", [P, 2, CH])
        parts = sb("a_parts", [P, 2, 3, CH], BF16)
        v_out = sb("a_v_out", [P, NS, H, HV])
        xT_bank = [ctx.enter_context(nc.psum_tensor(f"a_xT_bank{i}", [P, BANK], F32)) for i in range(2)]
        pr_bank = [ctx.enter_context(nc.psum_tensor(f"a_pr_bank{i}", [P, BANK], F32)) for i in range(6)]

        params_in, weights_in, x_loaded = sem("a_params_in"), sem("a_weights_in"), sem("a_x_loaded")
        zeroed, ident_ready, ones_ready = sem("a_zeroed"), sem("a_ident_ready"), sem("a_ones_ready")
        prep, sin_done, sig_done = sem("a_prep"), sem("a_sin_done"), sem("a_sig_done")
        ada_done, row_done, diag_ready, row_copied = (sem("a_ada_done"), sem("a_row_done"), sem("a_diag_ready"),
                                                      sem("a_row_copied"))
        normed, dev_done = sem("a_normed"), sem("a_dev_done")
        transposed, xT_ready = sem("a_transposed"), sem("a_xT_ready")
        projected, evacuated = sem("a_projected"), sem("a_evacuated")
        split, split_step = sem("a_split"), sem("a_split_step")
        qk_stored = [sem(f"a_qk_stored{r}") for r in range(2)]
        v_stored, xada_stored = sem("a_v_stored"), sem("a_xada_stored")
        f32_copied = sem("a_f32_copied")

        sp_gate, dve_gate, pool_gate = sem("a_sp_gate"), sem("a_dve_gate"), sem("a_pool_gate")
        N_LN = 2 * NS + 2 + 3 * NS
        block = ctx.enter_context(nc.Block())

        @block.sync
        def _(sp):
            sp.dma_start(cols[:, :], io["cols"]).then_inc(params_in, 16)
            sp.dma_start(freqs[:, :], io["freqs"]).then_inc(params_in, 16)
            sp.dma_start(step_i[:, :], io["timestep"].rearrange("(a b) -> a b", a=1).to_broadcast([P, B])
                         ).then_inc(params_in, 16)
            sp.dma_start(w_ada[:, :, :], io["W_ada"].rearrange("(k p) n -> p k n", p=P)).then_inc(params_in, 16)
            sp.dma_start(x_in[:, :, :], x_tiles[0]).then_inc(x_loaded, 16)
            for w, name in ((wq, "Wq"), (wk, "Wk"), (wv, "Wv")):
                sp.dma_start(w[:, :, :], io[name].rearrange("(k p) n -> p k n", p=P)).then_inc(weights_in, 16)
            for b in range(B):
                with sp.Fori(0, NC) as c:
                    n = c + b * NC
                    wait_apart(sp, normed, n * N_LN + N_LN, sp_gate)
                    sp.dma_start(xada_tiles[n], xada[:, :, :]).then_inc(xada_stored, 16)
                    for j in range(2 * KD):
                        wait_apart(sp, split, n * (2 * KD) + j + 1, sp_gate)
                        dst = q_tiles if j < KD else k_tiles
                        sp.dma_start(dst[b, j % KD, c], parts[:, j % 2, :, :]).then_inc(qk_stored[j % 2], 16)
                    for s in range(NS):
                        wait_apart(sp, evacuated, n * (2 * KD + NS) + 2 * KD + s + 1, sp_gate)
                        sp.dma_start(v_tiles[b, c, s], v_out[:, s, :, :]).then_inc(v_stored, 16)
            sp.wait_ge(xada_stored, 16 * B * NC)
            for r in range(2):
                sp.wait_ge(qk_stored[r], 16 * KD * B * NC)
            sp.wait_ge(v_stored, 16 * NS * B * NC)

        @block.gpsimd
        def _(pool):
            make_identity(pool, ident, zeroed, ident_ready)
            pool.memset(ones[:, :], 1.0).then_inc(ones_ready, 1)
            pool.memset(v_out[:, :, :, HD:HV], 1.0).then_inc(ones_ready, 1)
            for b in range(B):
                with pool.Fori(0, NC) as c:
                    n = c + b * NC
                    for j in range(2 * KD):
                        r = j % 2
                        base = (n * (2 * KD) + j) * 2
                        pool.wait_ge(f32_copied, n * (2 * KD) + j + 1)
                        pool.wait_ge(evacuated, n * (2 * KD + NS) + j + 1)
                        pool.tensor_tensor(rest[:, r, :], qk_f32[:, r, :], parts[:, r, 0, :],
                                           ALU.subtract).then_inc(split_step, 1)
                        wait_apart(pool, split_step, base + 1, pool_gate)
                        pool.tensor_copy(parts[:, r, 1, :], rest[:, r, :]).then_inc(split_step, 1)
                        pool.wait_ge(split_step, base + 2)
                        pool.tensor_tensor(parts[:, r, 2, :], rest[:, r, :], parts[:, r, 1, :],
                                           ALU.subtract).then_inc(split, 1)

        @block.vector
        def _(dve):
            st = Steps(prep)
            done = lambda: dve.wait_ge(prep, st.n)
            dve.wait_ge(params_in, 16 * 4)
            for g in range(KD):
                k = st.mark(dve.tensor_scalar(bqs[:, g:g + 1], column(cols, "bq", g), Q_SCALE, None, ALU.mult))
            st.mark(dve.tensor_copy(step_x[:, 0, :], step_i[:, :]))
            done()
            t, q, top, low, left = (step_x[:, i, :] for i in range(5))
            st.mark(dve.tensor_scalar(q, t, 0.01, None, ALU.mult))
            done()
            st.mark(dve.tensor_scalar(top, q, ROUND / 4096, ROUND / 4096, ALU.add, ALU.subtract))
            done()
            st.mark(dve.tensor_tensor(low, q, top, ALU.subtract))
            st.mark(dve.scalar_tensor_tensor(out=left, in0=top, scalar=-100.0, in1=t, op0=ALU.mult, op1=ALU.add))
            done()
            st.mark(dve.scalar_tensor_tensor(out=left, in0=low, scalar=-100.0, in1=left, op0=ALU.mult, op1=ALU.add))
            done()
            st.mark(dve.scalar_tensor_tensor(out=q, in0=left, scalar=0.01, in1=q, op0=ALU.mult, op1=ALU.add))
            done()
            st.mark(dve.tensor_scalar(top, q, 4000.0, None, ALU.mult))
            done()
            for b in range(B):
                st.mark(dve.tensor_scalar(angle[:, 0, :, b], freqs[:, :], step_x[:, 2, b:b + 1], None, ALU.mult))
            done()
            st.mark(dve.tensor_scalar(angle[:, 1, :, :], angle[:, 0, :, :], 1.0 / (2 * math.pi), ROUND,
                                      ALU.mult, ALU.add))
            done()
            st.mark(dve.tensor_scalar(angle[:, 2, :, :], angle[:, 1, :, :], ROUND, None, ALU.subtract))
            for part in (TWO_PI_1, TWO_PI_2, TWO_PI_3):
                done()
                st.mark(dve.scalar_tensor_tensor(out=angle[:, 0, :, :], in0=angle[:, 2, :, :], scalar=-part,
                                                 in1=angle[:, 0, :, :], op0=ALU.mult, op1=ALU.add))
            done()
            half = KD // 2
            st.mark(dve.tensor_scalar(angle[:, 0, half:, :], angle[:, 0, half:, :], math.pi / 2, None, ALU.add))
            done()
            st.mark(dve.tensor_scalar(angle[:, 1, half:, :], angle[:, 0, half:, :], math.pi, -2 * math.pi,
                                      ALU.is_gt, ALU.mult))
            done()
            st.mark(dve.tensor_tensor(angle[:, 0, half:, :], angle[:, 0, half:, :], angle[:, 1, half:, :], ALU.add))
            done()
            angle_ready = st.mark(dve.tensor_scalar(angle[:, 3, :, :], angle[:, 0, :, :], -PI_INSIDE, PI_INSIDE,
                                                    ALU.max, ALU.min))
            assert angle_ready == N_ANGLE
            dve.wait_ge(sig_done, 1)
            st.mark(dve.tensor_tensor(emb[:, 2, :, :], emb[:, 0, :, :], emb[:, 1, :, :], ALU.mult))
            assert st.n == N_SILU
            dve.wait_ge(ada_done, 1)
            for j in range(2 * KD):
                st.mark(dve.tensor_scalar(ada[:, j, :], pr_bank[0][:, j * B:(j + 1) * B], column(cols, "b_ada", j),
                                          1.0 if j < KD else 0.0, ALU.add, ALU.add))
            done()
            dve.wait_ge(ident_ready, 1)
            for i, (b, half_at) in enumerate((b, h) for b in range(B) for h in (0, KD)):
                if i:
                    dve.wait_ge(row_done, i)
                for g in range(KD):
                    last = dve.tensor_scalar(diag[:, g, :], ident[:, :], ada[:, half_at + g, b:b + 1], None, ALU.mult)
                last.then_inc(diag_ready, 1)
                dve.wait_ge(row_done, i + 1)
                dst = scale1 if half_at == 0 else shift
                dve.tensor_copy(dst[:, b, :], pr_bank[1][:, :]).then_inc(row_copied, 1)
            dve.wait_ge(row_copied, 2 * B)
            def chunk(n, b):
                ln = Steps(normed)
                upto = lambda k: dve.wait_ge(normed, n * N_LN + k)
                dve.wait_ge(x_loaded, n * 16 + 16)
                for s in range(NS):
                    k = ln.mark(dve.bn_stats(stats[:, s, :], x_in[:, s, :]))
                wait_apart(dve, normed, n * N_LN + k, dve_gate)
                for s in range(NS):
                    k = ln.mark(dve.bn_aggr(moments[:, s, :], stats[:, s, :]))
                upto(k)
                k = ln.mark(dve.tensor_scalar(rstd[:, :], moments[:, :, 1], EPS, None, ALU.add))
                assert k == N_VAR
                dve.wait_ge(dev_done, n + 1)
                k = ln.mark(dve.reciprocal(rstd[:, :], dev[:, :]))
                upto(k)
                wait(dve, transposed, n * KD)
                wait(dve, xada_stored, n * 16)
                for s in range(NS):
                    k = ln.mark(dve.tensor_scalar(xada[:, s, :], x_in[:, s, :], moments[:, s, 0:1],
                                                  rstd[:, s:s + 1], ALU.subtract, ALU.mult))
                upto(k)
                for s in range(NS):
                    k = ln.mark(dve.tensor_tensor(xada[:, s, :], xada[:, s, :], scale1[:, b, :], ALU.mult))
                upto(k)
                for s in range(NS):
                    k = ln.mark(dve.tensor_tensor(xada[:, s, :], xada[:, s, :], shift[:, b, :], ALU.add))
                assert ln.n == N_LN

            chunk(0, 0)
            for b in range(B):
                if NC > 1 or b:
                    with dve.Fori(b * NC or 1, (b + 1) * NC) as n:
                        chunk(n, b)

        @block.scalar
        def _(act):
            act.wait_ge(prep, N_ANGLE)
            act.activation(emb[:, 0, :, :], angle[:, 3, :, :], ACT.Sin).then_inc(sin_done, 1)
            act.wait_ge(sin_done, 1)
            act.activation(emb[:, 1, :, :], emb[:, 0, :, :], ACT.Sigmoid).then_inc(sig_done, 1)
            act.wait_ge(ones_ready, 2)

            def deviations(n):
                act.wait_ge(normed, n * N_LN + N_VAR)
                act.activation(dev[:, :], rstd[:, :], ACT.Sqrt).then_inc(dev_done, 1)

            def chunk(n, first, last):
                for k in range(KD):
                    act.wait_ge(transposed, n * KD + k + 1)
                    act.activation(xT[:, k, :], xT_bank[k % 2][:, :], ACT.Copy).then_inc(xT_ready, 1)
                if not last:
                    act.wait_ge(normed, n * N_LN + N_LN)
                    act.dma_start(x_in[:, :, :], x_tiles[n + 1]).then_inc(x_loaded, 16)
                for j in range(2 * KD):
                    r, g = j % 2, j % KD
                    scale, bias = (Q_SCALE, bqs[:, g:g + 1]) if j < KD else (1.0, column(cols, "bk", g))
                    act.wait_ge(projected, n * (2 * KD + NS) + j + 1)
                    behind = max(0, j - 1)
                    wait(act, split, n * (2 * KD) + behind)
                    act.activation(qk_f32[:, r, :], pr_bank[j % 6][:, :], ACT.Identity, bias=bias, scale=scale
                                   ).then_inc(f32_copied, 1)
                    wait(act, qk_stored[r], (n * KD + j // 2) * 16)
                    act.activation(parts[:, r, 0, :], pr_bank[j % 6][:, :], ACT.Identity, bias=bias, scale=scale
                                   ).then_inc(evacuated, 1)
                    if j == KD and not last:
                        deviations(n + 1)
                wait(act, v_stored, n * (NS * 16))
                for s in range(NS):
                    j = 2 * KD + s
                    act.wait_ge(projected, n * (2 * KD + NS) + j + 1)
                    act.activation(v_out[:, s, :, 0:HD], pr_bank[j % 6][:, :].rearrange("p (h d) -> p h d", h=H),
                                   ACT.Copy).then_inc(evacuated, 1)

            deviations(0)
            turns(act, B * NC, chunk)

        @block.tensor
        def _(pe):
            pe.wait_ge(params_in, 16 * 4)
            pe.wait_ge(prep, N_SILU)
            for j in range(2 * KD):
                for k in range(KD):
                    last = pe.matmul(pr_bank[0][:, j * B:(j + 1) * B], w_ada[:, k, j * P:(j + 1) * P],
                                     emb[:, 2, k, :], start=(k == 0), stop=(k == KD - 1))
            last.then_inc(ada_done, 1)
            pe.wait_ge(ones_ready, 1)
            for i in range(2 * B):
                pe.wait_ge(diag_ready, i + 1)
                if i:
                    pe.wait_ge(row_copied, i)
                for g in range(KD):
                    last = pe.matmul(pr_bank[1][:, g * P:(g + 1) * P], ones[:, :], diag[:, g, :],
                                     start=True, stop=True)
                last.then_inc(row_done, 1)
            pe.wait_ge(row_copied, 2 * B)
            pe.wait_ge(weights_in, 16 * 3)
            def chunk(n, first, last):
                pe.wait_ge(normed, n * N_LN + N_LN)
                for k in range(KD):
                    if k >= 2:
                        pe.wait_ge(xT_ready, n * KD + k - 1)
                    for s in range(NS):
                        last = pe.transpose(xT_bank[k % 2][:, s * P:(s + 1) * P], xada[:, s, k * P:(k + 1) * P],
                                            ident[:, :])
                    last.then_inc(transposed, 1)
                wait(pe, evacuated, n * (2 * KD + NS))
                pe.wait_ge(xT_ready, n * KD + KD)
                for j in range(2 * KD + NS):
                    bank = pr_bank[j % 6]
                    if j >= 6:
                        pe.wait_ge(evacuated, n * (2 * KD + NS) + j - 5)
                    for k in range(KD):
                        if j < 2 * KD:
                            w, g = (wq, j) if j < KD else (wk, j - KD)
                            lhsT, rhs = w[:, k, g * P:(g + 1) * P], xT[:, k, :]
                        else:
                            s = j - 2 * KD
                            lhsT, rhs = xT[:, k, s * P:(s + 1) * P], wv[:, k, :]
                        last = pe.matmul(bank[:, :], lhsT, rhs, start=(k == 0), stop=(k == KD - 1))
                    last.then_inc(projected, 1)

            turns(pe, B * NC, chunk)


N_ANGLE = KD + 8 + 2 + 2 + 3 + 4
N_SILU = N_ANGLE + 1
N_VAR = 2 * NS + 1


U = 4
HEAD_DMAS = 17
Q_PARTS = ((0, 0), (0, 2), (1, 1), (1, 2))
K_PARTS = ((0, 2), (1, 0), (0, 2), (1, 1))


def attention_phase(nc, S, B, io, q3_dram, k3_dram, v_dram, ctx_dram):
    NQ = S // P
    NCK = S // BANK
    NG = NQ // U
    HEADS = B * H
    PAIRS = HEADS // 2
    TILES = HEADS * NQ
    GROUPS = TILES // U
    bias_tiles = io["fside"].rearrange("b h (q p) k -> (b h q) p k", p=P)
    mask_rows = io["mask"].rearrange("b one (q p) k -> (b one) p q k", p=P)
    q_rows = q3_dram.rearrange("t (n r) k -> n t r k", r=HD)
    k_rows = k3_dram.rearrange("t (n r) k -> n t r k", r=HD)

    with ExitStack() as ctx:
        sb = lambda name, shape, dt=F32: ctx.enter_context(nc.sbuf_tensor(name, shape, dt))
        sem = lambda name: ctx.enter_context(nc.semaphore(name))
        bank = lambda name: ctx.enter_context(nc.psum_tensor(name, [P, BANK], F32))

        ident = sb("b_ident", [P, P])
        mask_in = sb("b_mask_in", [P, NQ, S], U8)
        mask_add = sb("b_mask_add", [P, NQ, S], BF16)
        qst = [sb(f"b_qst{i}", [P, 2, S], BF16) for i in range(2)]
        kst = [sb(f"b_kst{i}", [P, 2, S], BF16) for i in range(2)]
        vh = [sb(f"b_vh{i}", [P, NQ, HV]) for i in range(2)]
        bias = [sb(f"b_bias{i}", [P, S]) for i in range(U)]
        scores = [sb(f"b_scores{i}", [P, S]) for i in range(2)]
        chunk_max = [sb(f"b_chunk_max{i}", [P, NCK]) for i in range(2)]
        row_max = [sb(f"b_row_max{i}", [P, 1]) for i in range(2)]
        probsT = sb("b_probsT", [P, NCK, BANK])
        denom = sb("b_denom", [P, 2])
        ctx_out = [sb(f"b_ctx_out{i}", [P, HD]) for i in range(U)]
        s_bank = [bank(f"b_s_bank{i}") for i in range(NCK)]
        t_bank = [bank(f"b_t_bank{i}") for i in range(2)]
        o_bank = [bank(f"b_o_bank{i}") for i in range(2)]

        zeroed, ident_ready = sem("b_zeroed"), sem("b_ident_ready")
        mask_loaded = [sem(f"b_mask_loaded{b}") for b in range(B)]
        mask_ready = sem("b_mask_ready")
        head_loaded = [sem(f"b_head_loaded{i}") for i in range(2)]
        bias_loaded = [sem(f"b_bias_loaded{i}") for i in range(U)]
        ctx_stored = [sem(f"b_ctx_stored{i}") for i in range(U)]
        bias_masked, qk_done, scored = sem("b_bias_masked"), sem("b_qk_done"), sem("b_scored")
        max_done, shifted, transposed = sem("b_max_done"), sem("b_shifted"), sem("b_transposed")
        exp_done, pv_done, inverted = sem("b_exp_done"), sem("b_pv_done"), sem("b_inverted")
        ctx_ready = sem("b_ctx_ready")

        sp_gate, dve_gate = sem("b_sp_gate"), sem("b_dve_gate")

        def load_head(queue, hd, par):
            for r in range(4):
                rows = slice(HD * r, HD * (r + 1))
                for i in range(2):
                    queue.dma_start(qst[par][rows, i, :], q_rows[hd, Q_PARTS[r][i]]).then_inc(head_loaded[par], 16)
                    queue.dma_start(kst[par][rows, i, :], k_rows[hd, K_PARTS[r][i]]).then_inc(head_loaded[par], 16)
            queue.dma_start(vh[par][:, :, :], v_dram[hd]).then_inc(head_loaded[par], 16)

        block = ctx.enter_context(nc.Block())

        @block.sync
        def _(sp):
            sp.dma_start(mask_in[:, :, :], mask_rows[0]).then_inc(mask_loaded[0], 16)
            load_head(sp, 0, 0)
            for u in range(U):
                sp.dma_start(bias[u][:, :], bias_tiles[u]).then_inc(bias_loaded[u], 16)

            def group(hd, g, ahead=True):
                t0 = (hd * NG + g) * U
                for u in range(U if ahead else 0):
                    wait_apart(sp, scored, (t0 + u + 1) * NCK, sp_gate)
                    sp.dma_start(bias[u][:, :], bias_tiles[t0 + U + u]).then_inc(bias_loaded[u], 16)

            def head(hd, par, last):
                group(hd, 0, ahead=not last or NG > 1)
                if not last:
                    wait_apart(sp, qk_done, hd * (NQ * NCK) + 1, sp_gate)
                    wait_apart(sp, pv_done, hd * NQ + 1, sp_gate)
                    load_head(sp, hd + 1, 1 - par)
                if NG - 1 - last > 0:
                    with sp.Fori(1, NG - last) as g:
                        group(hd, g)

            if PAIRS > 1:
                with sp.Fori(0, PAIRS - 1) as pair:
                    for par in range(2):
                        head(pair * 2 + par, par, False)
            head(HEADS - 2, 0, False)
            head(HEADS - 1, 1, True)

        @block.gpsimd
        def _(pool):
            make_identity(pool, ident, zeroed, ident_ready)

            def tile(b, hd, q, first):
                t = hd * NQ + q
                u = q % U
                if first:
                    if b:
                        pool.wait_ge(bias_masked, b * H * NQ)
                    pool.tensor_scalar(mask_add[:, q, :], mask_in[:, q, :], MASKED, None, ALU.mult
                                       ).then_inc(mask_ready, 1)
                    pool.wait_ge(mask_ready, b * NQ + q + 1)
                pool.wait_ge(bias_loaded[u], (hd * NG + q // U + 1) * 16)
                pool.tensor_tensor(bias[u][:, :], bias[u][:, :], mask_add[:, q, :], ALU.add).then_inc(bias_masked, 1)

            for b in range(B):
                pool.wait_ge(mask_loaded[b], 16)
                for q in range(NQ):
                    tile(b, b * H, q, True)
                if b + 1 < B:
                    pool.wait_ge(mask_ready, (b + 1) * NQ)
                    pool.dma_start(mask_in[:, :, :], mask_rows[b + 1]).then_inc(mask_loaded[b + 1], 16)
                with pool.Fori(b * H + 1, (b + 1) * H) as hd:
                    for q in range(NQ):
                        tile(b, hd, q, False)

        @block.vector
        def _(dve):
            dve.memset(denom[:, :], 0.0).then_inc(ctx_ready, 2)

            def tile(g, u, first):
                t = g * U + u
                par = u % 2
                if not (first and u < 2):
                    w = (u - 2) % U
                    dve.wait_ge(pv_done, t - 1)
                    dve.reciprocal(denom[:, par:par + 1], o_bank[par][:, HD:HV]).then_inc(inverted, 1)
                    if not first:
                        dve.wait_ge(ctx_stored[w], (g + 1) * 16 if u >= 2 else g * 16)
                    dve.wait_ge(inverted, t - 1)
                    dve.tensor_scalar(ctx_out[w][:, :], o_bank[par][:, 0:HD], denom[:, par:par + 1], None,
                                      ALU.mult).then_inc(ctx_ready, 1)
                if not (first and u < 2):
                    dve.wait_ge(transposed, (t - 1) * NCK)
                dve.wait_ge(bias_masked, t + 1)
                for c in range(NCK):
                    cols = slice(c * BANK, (c + 1) * BANK)
                    wait_apart(dve, qk_done, t * NCK + c + 1, dve_gate)
                    dve.tensor_tensor_reduce(scores[par][:, cols], s_bank[c][:, :], bias[u][:, cols], 1.0, -3.0e38,
                                             ALU.add, ALU.max, chunk_max[par][:, c:c + 1]).then_inc(scored, 1)
                dve.wait_ge(scored, (t + 1) * NCK)
                dve.tensor_reduce(row_max[par][:, :], chunk_max[par][:, :], AX.X, ALU.max).then_inc(max_done, 1)
                dve.wait_ge(max_done, t + 1)
                for c in range(NCK):
                    cols = slice(c * BANK, (c + 1) * BANK)
                    dve.tensor_scalar(scores[par][:, cols], scores[par][:, cols], row_max[par][:, 0:1], None,
                                      ALU.subtract).then_inc(shifted, 1)

            def context(t):
                par, w = t % 2, t % U
                dve.wait_ge(pv_done, t + 1)
                dve.reciprocal(denom[:, par:par + 1], o_bank[par][:, HD:HV]).then_inc(inverted, 1)
                dve.wait_ge(ctx_stored[w], t // U * 16 + 16)
                dve.wait_ge(inverted, t + 1)
                dve.tensor_scalar(ctx_out[w][:, :], o_bank[par][:, 0:HD], denom[:, par:par + 1], None,
                                  ALU.mult).then_inc(ctx_ready, 1)

            for u in range(U):
                tile(0, u, True)
            with dve.Fori(1, GROUPS) as g:
                for u in range(U):
                    tile(g, u, False)
            context(TILES - 2)
            context(TILES - 1)

        @block.scalar
        def _(act):
            def store(g, w):
                t = g * U + w
                act.wait_ge(ctx_ready, t + 3)
                act.dma_start(ctx_dram[t], ctx_out[w][:, :]).then_inc(ctx_stored[w], 16)

            def tile(g, u, first):
                t = g * U + u
                for c in range(NCK):
                    act.wait_ge(transposed, t * NCK + c + 1)
                    act.activation(probsT[:, c, :], t_bank[c % 2][:, :], ACT.Exp).then_inc(exp_done, 1)
                if u == 3:
                    store(g, 0)
                elif not first:
                    store(g - 1, u + 1)

            for w in range(U):
                act.sem_inc(ctx_stored[w], 16)
            for u in range(U):
                tile(0, u, True)
            with act.Fori(1, GROUPS) as g:
                for u in range(U):
                    tile(g, u, False)
            for w in range(1, U):
                store(GROUPS - 1, w)
            for w in range(U):
                act.wait_ge(ctx_stored[w], GROUPS * 16 + 16)

        @block.tensor
        def _(pe):
            def qk(t, par, q, c):
                for i in range(2):
                    last = pe.matmul(s_bank[c][:, :], qst[par][:, i, bass.ts(q, P)], kst[par][:, i, bass.ts(c, BANK)],
                                     start=(i == 0), stop=(i == 1))
                last.then_inc(qk_done, 1)

            def turn(t, c):
                pe.wait_ge(shifted, t * NCK + c + 1)
                if c >= 2:
                    pe.wait_ge(exp_done, t * NCK + c - 1)
                for i in range(BANK // P):
                    last = pe.transpose(t_bank[c % 2][:, i * P:(i + 1) * P],
                                        scores_of_turn[0][:, c * BANK + i * P:c * BANK + (i + 1) * P], ident[:, :])
                last.then_inc(transposed, 1)

            def pv(t, par, slot, c):
                pe.wait_ge(exp_done, t * NCK + c + 1)
                if c == 0:
                    pe.wait_ge(ctx_ready, t + 1)
                for i in range(BANK // P):
                    k = c * (BANK // P) + i
                    last = pe.matmul(o_bank[slot][:, 0:HV], probsT[:, c, i * P:(i + 1) * P], vh[par][:, k, :],
                                     start=(k == 0), stop=(k == NQ - 1))
                if c == NCK - 1:
                    last.then_inc(pv_done, 1)

            scores_of_turn = [None]

            def tile(pair, par, g, u, last):
                t = ((pair * 2 + par) * NG + g) * U + u
                q_next = g * U + u + 1
                scores_of_turn[0] = scores[u % 2]
                crosses = isinstance(g, int) and g == NG - 1 and u == U - 1
                follows = not (last and crosses)
                par_next, q_next = (1 - par, 0) if crosses else (par, q_next)
                chunks = list(range(NCK))
                for c in range(NCK):
                    turn(t, c)
                    for _ in range(2):
                        if chunks and follows:
                            cc = chunks.pop(0)
                            if crosses and cc == 0:
                                pe.wait_ge(head_loaded[par_next], (pair + par + 1) * (16 * HEAD_DMAS))
                            pe.wait_ge(scored, t * NCK + cc + 1)
                            qk(t + 1, par_next, q_next, cc)
                    if c:
                        pv(t, par, u % 2, c - 1)
                pv(t, par, u % 2, NCK - 1)

            def head(pair, par, last):
                if NG > 1:
                    with pe.Fori(0, NG - 1) as g:
                        for u in range(U):
                            tile(pair, par, g, u, last)
                for u in range(U):
                    tile(pair, par, NG - 1, u, last)

            pe.wait_ge(ident_ready, 1)
            pe.wait_ge(head_loaded[0], 16 * HEAD_DMAS)
            for c in range(NCK):
                qk(0, 0, 0, c)
            if PAIRS > 1:
                with pe.Fori(0, PAIRS - 1) as pair:
                    for par in range(2):
                        head(pair, par, False)
            head(PAIRS - 1, 0, False)
            head(PAIRS - 1, 1, True)


def batch_turns(engine, B, NC, body):
    for b in range(B):
        first, last = b * NC, (b + 1) * NC - 1
        if b == 0 and NC > 1:
            body(0, 0, 0)
            first = 1
        if last > first:
            with engine.Fori(first, last) as n:
                body(n, b, b)
        body(last, b, b + 1 if b + 1 < B else None)


class Norm:

    N_VAR = 2 * NS + 1
    SIZE = N_VAR + 1 + NS

    def __init__(self, sb, sem, name):
        self.stats = sb(name + "_stats", [P, NS, 6])
        self.moments = sb(name + "_moments", [P, NS, 2])
        self.var = sb(name + "_var", [P, NS])
        self.dev = sb(name + "_dev", [P, NS])
        self.rstd = sb(name + "_rstd", [P, NS])
        self.done, self.dev_done, self.gate = sem(name + "_done"), sem(name + "_dev_done"), sem(name + "_gate")

    def statistics(self, dve, s, row):
        dve.bn_stats(self.stats[:, s, :], row).then_inc(self.done, 1)

    def rows(self, dve, n, out, x):
        base = n * self.SIZE
        wait_apart(dve, self.done, base + NS, self.gate)
        for s in range(NS):
            dve.bn_aggr(self.moments[:, s, :], self.stats[:, s, :]).then_inc(self.done, 1)
        dve.wait_ge(self.done, base + 2 * NS)
        dve.tensor_scalar(self.var[:, :], self.moments[:, :, 1], EPS, None, ALU.add).then_inc(self.done, 1)
        dve.wait_ge(self.dev_done, n + 1)
        dve.reciprocal(self.rstd[:, :], self.dev[:, :]).then_inc(self.done, 1)
        dve.wait_ge(self.done, base + self.N_VAR + 1)
        for s in range(NS):
            dve.tensor_scalar(out[:, s, :], x[:, s, :], self.moments[:, s, 0:1], self.rstd[:, s:s + 1],
                              ALU.subtract, ALU.mult).then_inc(self.done, 1)

    def deviations(self, act, n):
        act.wait_ge(self.done, n * self.SIZE + self.N_VAR)
        act.activation(self.dev[:, :], self.var[:, :], ACT.Sqrt).then_inc(self.dev_done, 1)


def feed_forward_phase(nc, S, B, io, xada_dram, ctx_dram, x2_dram):
    NC = S // CH
    N = B * NC
    ctx_tiles = ctx_dram.rearrange("(b h c s) p d -> b c s p h d", b=B, h=H, s=NS)
    xada_tiles = xada_dram.rearrange("(n s p) d -> n p s d", s=NS, p=P)
    x2_tiles = x2_dram.rearrange("(n s p) d -> n p s d", s=NS, p=P)

    with ExitStack() as ctx:
        sb = lambda name, shape, dt=F32: ctx.enter_context(nc.sbuf_tensor(name, shape, dt))
        sem = lambda name: ctx.enter_context(nc.semaphore(name))

        ident = sb("c_ident", [P, P])
        cols = sb("c_cols", [P, N_COLUMNS])
        b1_sig = sb("c_b1_sig", [P, KF])
        bo_row = sb("c_bo_row", [P, D])
        b2_row = sb("c_b2_row", [P, D])
        wo = sb("c_wo", [P, KD, D])
        w1 = sb("c_w1", [P, KD, FF])
        w2 = sb("c_w2", [P, KF, D])
        ctx_in = sb("c_ctx_in", [P, NS, D])
        xada = sb("c_xada", [P, NS, D])
        ctxT = sb("c_ctxT", [P, KD, CH])
        x1 = sb("c_x1", [P, NS, D])
        x1b = sb("c_x1b", [P, NS, D])
        h = sb("c_h", [P, NS, D])
        hT = sb("c_hT", [P, KD, CH])
        sig = sb("c_sig", [P, 2, CH])
        ff = sb("c_ff", [P, KF, CH])
        x2 = sb("c_x2", [P, NS, D])
        t_bank = [ctx.enter_context(nc.psum_tensor(f"c_t_bank{i}", [P, BANK], F32)) for i in range(2)]
        y_bank = [ctx.enter_context(nc.psum_tensor(f"c_y_bank{i}", [P, BANK], F32)) for i in range(NS)]
        f_bank = [ctx.enter_context(nc.psum_tensor(f"c_f_bank{i}", [P, BANK], F32)) for i in range(2)]
        norm = Norm(sb, sem, "c_norm")

        params_in, wo_in, weights_in = sem("c_params_in"), sem("c_wo_in"), sem("c_weights_in")
        zeroed, ident_ready, b1_ready = sem("c_zeroed"), sem("c_ident_ready"), sem("c_b1_ready")
        ctx_loaded, xada_loaded, x2_stored = sem("c_ctx_loaded"), sem("c_xada_loaded"), sem("c_x2_stored")
        ctx_turned, ctxT_ready = sem("c_ctx_turned"), sem("c_ctxT_ready")
        bo_added, wo_done, x1_ready, x1b_ready = (sem("c_bo_added"), sem("c_wo_done"), sem("c_x1_ready"),
                                                  sem("c_x1b_ready"))
        h_turned, hT_ready = sem("c_h_turned"), sem("c_hT_ready")
        w1_done, sig_ready, ff_ready = sem("c_w1_done"), sem("c_sig_ready"), sem("c_ff_ready")
        w2_done, x2_ready = sem("c_w2_done"), sem("c_x2_ready")
        sp_gate = sem("c_sp_gate")

        block = ctx.enter_context(nc.Block())

        @block.sync
        def _(sp):
            def load_ctx(b, c):
                for s in range(NS):
                    sp.dma_start(ctx_in[:, s, :].rearrange("p (h d) -> p h d", h=H), ctx_tiles[b, c, s]
                                 ).then_inc(ctx_loaded, 16)

            def load_xada(n):
                sp.dma_start(xada[:, :, :], xada_tiles[n]).then_inc(xada_loaded, 16)

            def store_x2(n):
                wait_apart(sp, x2_ready, n * NS + NS, sp_gate)
                sp.dma_start(x2_tiles[n], x2[:, :, :]).then_inc(x2_stored, 16)

            sp.dma_start(cols[:, :], io["cols"]).then_inc(params_in, 16)
            load_ctx(0, 0)
            sp.dma_start(wo[:, :, :], io["Wo"].rearrange("(k p) n -> p k n", p=P)).then_inc(wo_in, 16)
            load_xada(0)
            for row, name in ((bo_row, "bo"), (b2_row, "b2")):
                sp.dma_start(row[:, :], io[name].rearrange("(a n) -> a n", a=1).to_broadcast([P, D])
                             ).then_inc(params_in, 16)
            sp.dma_start(w1[:, :, :], io["W1"].rearrange("(k p) n -> p k n", p=P)).then_inc(weights_in, 16)
            sp.dma_start(w2[:, :, :], io["W2"].rearrange("(k p) n -> p k n", p=P)).then_inc(weights_in, 16)

            def ahead(n, b_next, c_next):
                wait_apart(sp, ctx_turned, n * KD + KD, sp_gate)
                load_ctx(b_next, c_next)
                wait_apart(sp, x1_ready, n * NS + NS, sp_gate)
                load_xada(n + 1)

            ahead(0, 0, 1) if NC > 1 else ahead(0, 1, 0) if B > 1 else None
            for b in range(B):
                first = 0 if b else 1
                if NC - 1 > first:
                    with sp.Fori(first, NC - 1) as c:
                        n = c + b * NC
                        ahead(n, b, c + 1)
                        store_x2(n - 1)
                if (b or NC > 1) and b + 1 < B:
                    ahead((b + 1) * NC - 1, b + 1, 0)
                    store_x2((b + 1) * NC - 2)
            if N > 1:
                store_x2(N - 2)
            store_x2(N - 1)
            sp.wait_ge(x2_stored, N * 16)

        @block.gpsimd
        def _(pool):
            make_identity(pool, ident, zeroed, ident_ready)
            pool.wait_ge(params_in, 16 * 3)

            def turn(n, first, last):
                pool.wait_ge(xada_loaded, n * 16 + 16)
                for s in range(NS):
                    pool.tensor_tensor(xada[:, s, :], xada[:, s, :], bo_row[:, :], ALU.add).then_inc(bo_added, 1)
                pool.wait_ge(x1_ready, n * NS + NS)
                wait(pool, x2_ready, n * NS)
                for s in range(NS):
                    pool.tensor_tensor(x1b[:, s, :], x1[:, s, :], b2_row[:, :], ALU.add).then_inc(x1b_ready, 1)

            turns(pool, N, turn)

        @block.vector
        def _(dve):
            dve.wait_ge(params_in, 16 * 3)
            at, k = COLUMNS["b1"]
            dve.tensor_scalar(b1_sig[:, :], cols[:, at:at + k], 1.702, None, ALU.mult).then_inc(b1_ready, 1)

            def second_residual(n):
                wait(dve, x2_stored, n * 16)
                for s in range(NS):
                    dve.wait_ge(w2_done, n * NS + s + 1)
                    dve.wait_ge(x1b_ready, n * NS + s + 1)
                    dve.tensor_tensor(x2[:, s, :], y_bank[s][:, :], x1b[:, s, :], ALU.add).then_inc(x2_ready, 1)

            def turn(n, first, last):
                if not first:
                    dve.wait_ge(x1b_ready, n * NS)
                for s in range(NS):
                    dve.wait_ge(wo_done, n * NS + s + 1)
                    dve.wait_ge(bo_added, n * NS + s + 1)
                    dve.tensor_tensor(x1[:, s, :], y_bank[s][:, :], xada[:, s, :], ALU.add).then_inc(x1_ready, 1)
                    dve.wait_ge(x1_ready, n * NS + s + 1)
                    norm.statistics(dve, s, x1[:, s, :])
                wait(dve, h_turned, n * KD)
                norm.rows(dve, n, h, x1)
                if not first:
                    second_residual(n - 1)
                for f in range(KF):
                    dve.wait_ge(sig_ready, n * KF + f + 1)
                    dve.scalar_tensor_tensor(out=ff[:, f, :], in0=f_bank[f % 2][:, :], scalar=column(cols, "b1", f),
                                             in1=sig[:, f % 2, :], op0=ALU.add, op1=ALU.mult).then_inc(ff_ready, 1)

            turns(dve, N, turn)
            second_residual(N - 1)

        @block.scalar
        def _(act):
            act.wait_ge(b1_ready, 1)

            def turn(n, first, last):
                for k in range(KD):
                    act.wait_ge(ctx_turned, n * KD + k + 1)
                    act.activation(ctxT[:, k, :], t_bank[k % 2][:, :], ACT.Identity, bias=column(cols, "bv", k)
                                   ).then_inc(ctxT_ready, 1)
                norm.deviations(act, n)
                for k in range(KD):
                    act.wait_ge(h_turned, n * KD + k + 1)
                    act.activation(hT[:, k, :], t_bank[k % 2][:, :], ACT.Identity, bias=column(cols, "beta2", k),
                                   scale=column(cols, "g2", k)).then_inc(hT_ready, 1)
                for f in range(KF):
                    act.wait_ge(w1_done, n * KF + f + 1)
                    wait(act, ff_ready, n * KF + f - 1 if f >= 2 else n * KF)
                    act.activation(sig[:, f % 2, :], f_bank[f % 2][:, :], ACT.Sigmoid, bias=b1_sig[:, f:f + 1],
                                   scale=1.702).then_inc(sig_ready, 1)

            turns(act, N, turn)

        @block.tensor
        def _(pe):
            pe.wait_ge(ident_ready, 1)

            def transposes(n, src, turned, ready):
                for k in range(KD):
                    if k >= 2:
                        pe.wait_ge(ready, n * KD + k - 1)
                    for s in range(NS):
                        last = pe.transpose(t_bank[k % 2][:, s * P:(s + 1) * P], src[:, s, k * P:(k + 1) * P],
                                            ident[:, :])
                    last.then_inc(turned, 1)
                pe.wait_ge(ready, n * KD + KD)

            def second_product(n):
                pe.wait_ge(ff_ready, n * KF + KF)
                for s in range(NS):
                    pe.wait_ge(x1_ready, (n + 1) * NS + s + 1 if not isinstance(n, int) or n < N - 1 else N * NS)
                    for k in range(KF):
                        last = pe.matmul(y_bank[s][:, :], ff[:, k, s * P:(s + 1) * P], w2[:, k, :],
                                         start=(k == 0), stop=(k == KF - 1))
                    last.then_inc(w2_done, 1)

            def turn(n, first, last):
                pe.wait_ge(ctx_loaded, (n + 1) * (16 * NS))
                transposes(n, ctx_in, ctx_turned, ctxT_ready)
                if first:
                    pe.wait_ge(wo_in, 16)
                for s in range(NS):
                    if not first:
                        pe.wait_ge(x1b_ready, n * NS)
                    for k in range(KD):
                        out = pe.matmul(y_bank[s][:, :], ctxT[:, k, s * P:(s + 1) * P], wo[:, k, :],
                                        start=(k == 0), stop=(k == KD - 1))
                    out.then_inc(wo_done, 1)
                if first:
                    pe.wait_ge(weights_in, 32)
                else:
                    second_product(n - 1)
                pe.wait_ge(norm.done, (n + 1) * Norm.SIZE)
                transposes(n, h, h_turned, hT_ready)
                for f in range(KF):
                    wait(pe, ff_ready, n * KF + f - 1 if f >= 2 else n * KF)
                    for k in range(KD):
                        out = pe.matmul(f_bank[f % 2][:, :], w1[:, k, f * P:(f + 1) * P], hT[:, k, :],
                                        start=(k == 0), stop=(k == KD - 1))
                    out.then_inc(w1_done, 1)

            turns(pe, N, turn)
            second_product(N - 1)


def adapter_phase(nc, S, B, io, x2_dram, out):
    NC = S // CH
    N = B * NC
    x2_tiles = x2_dram.rearrange("(n s p) d -> n p s d", s=NS, p=P)
    out_tiles = out.rearrange("b (c s p) d -> (b c) p s d", s=NS, p=P)
    K1 = 2 * KD

    with ExitStack() as ctx:
        sb = lambda name, shape, dt=F32: ctx.enter_context(nc.sbuf_tensor(name, shape, dt))
        sem = lambda name: ctx.enter_context(nc.semaphore(name))

        ident = sb("d_ident", [P, P])
        cols = sb("d_cols", [P, N_COLUMNS])
        ids_i = sb("d_ids_i", [P, 2, B], I32)
        ids = sb("d_ids", [P, 2, B])
        number = sb("d_number", [P, EXPERTS])
        number_i = sb("d_number_i", [P, EXPERTS], I32)
        clipped = sb("d_clipped", [P, B])
        valid = sb("d_valid", [P, 4, B])
        onehot = sb("d_onehot", [P, B, EXPERTS])
        case = sb("d_case", [P, 3, B])
        not_sr = sb("d_not_sr", [P, B])
        angle = sb("d_angle", [P, 4, 2, 2, B])
        turned = sb("d_turned", [P, 2, 2, B])
        minus_sin = sb("d_minus_sin", [P, 2, B])
        vecs = sb("d_vecs", [P, 2, EXPERTS])
        picked = sb("d_picked", [P, EXPERTS])
        sums = sb("d_sums", [P, 2])
        expert_bias = sb("d_expert_bias", [P, B])
        expertT = [sb(f"d_expertT{b}", [P, AD]) for b in range(B)]
        downT = sb("d_downT", [P, KD, AD])
        upT = sb("d_upT", [P, D])
        up_b = sb("d_up_b", [P, D])
        ln1 = sb("d_ln1", [P, 2, D])
        ln3 = sb("d_ln3", [P, 2, D])
        rot = [sb(f"d_rot{b}", [P, 3, D]) for b in range(B)]
        w_first = [sb(f"d_w_first{b}", [P, KD, 2 * D]) for b in range(B)]
        w_mid = sb("d_w_mid", [P, K1, D])
        w_last = [sb(f"d_w_last{b}", [P, KD, D]) for b in range(B)]
        b_first = sb("d_b_first", [P, B, K1])
        b_last = [sb(f"d_b_last{b}", [P, D]) for b in range(B)]

        x2 = sb("d_x2", [P, NS, D])
        x2T = sb("d_x2T", [P, KD, CH])
        hid = sb("d_hid", [P, CH])
        hid2 = sb("d_hid2", [P, CH])
        x3 = sb("d_x3", [P, NS, D])
        x4 = sb("d_x4", [P, NS, D])
        swapped = sb("d_swapped", [P, D])
        x4b = sb("d_x4b", [P, NS, D])
        x4T = sb("d_x4T", [P, KD, CH])
        h1 = sb("d_h1", [P, K1, CH])
        g2 = sb("d_g2", [P, 2, CH])
        kept = sb("d_kept", [P, 2, CH])
        h2 = sb("d_h2", [P, KD, CH])
        y = sb("d_y", [P, NS, D])
        staged = [h1[:, KD * i:KD * (i + 1), :] for i in range(2)] + [h2[:, :, :], x4T[:, :, :]]
        experts = y[:, :, :].rearrange("p s (e o) -> p (s e) o", o=AD)
        t_bank = [ctx.enter_context(nc.psum_tensor(f"d_t_bank{i}", [P, BANK], F32)) for i in range(2)]
        y_bank = [ctx.enter_context(nc.psum_tensor(f"d_y_bank{i}", [P, BANK], F32)) for i in range(NS)]
        w_bank = [ctx.enter_context(nc.psum_tensor(f"d_w_bank{i}", [P, BANK], F32)) for i in range(2)]
        norm1, norm3 = Norm(sb, sem, "d_norm1"), Norm(sb, sem, "d_norm3")

        params_in, experts_in, weights_in = sem("d_params_in"), sem("d_experts_in"), sem("d_weights_in")
        fixed_in, rows_in = sem("d_fixed_in"), sem("d_rows_in")
        x2_loaded, y_stored = sem("d_x2_loaded"), sem("d_y_stored")
        zeroed, ident_ready, numbered = sem("d_zeroed"), sem("d_ident_ready"), sem("d_numbered")
        prep, turned_done = sem("d_prep"), sem("d_turned_done")
        x2_turned, x2T_ready, up_b_added = sem("d_x2_turned"), sem("d_x2T_ready"), sem("d_up_b_added")
        down_done, hid_ready, expert_done, hid2_ready = (sem("d_down_done"), sem("d_hid_ready"),
                                                         sem("d_expert_done"), sem("d_hid2_ready"))
        up_done, x3_ready = sem("d_up_done"), sem("d_x3_ready")
        swap_done, rot_done, x4_ready, x4b_ready = (sem("d_swap_done"), sem("d_rot_done"), sem("d_x4_ready"),
                                                    sem("d_x4b_ready"))
        x4_turned, x4T_ready = sem("d_x4_turned"), sem("d_x4T_ready")
        first_done, h1_ready, mid_done, g2_ready = (sem("d_first_done"), sem("d_h1_ready"), sem("d_mid_done"),
                                                    sem("d_g2_ready"))
        kept_ready, h2_ready, last_done = sem("d_kept_ready"), sem("d_h2_ready"), sem("d_last_done")
        y_sum, y_scaled, y_ready = sem("d_y_sum"), sem("d_y_scaled"), sem("d_y_ready")
        sp_gate = sem("d_sp_gate")

        block = ctx.enter_context(nc.Block())

        @block.sync
        def _(sp):
            row = lambda name: io[name].rearrange("(a n) -> a n", a=1)
            tiled = lambda name: io[name].rearrange("(k p) n -> p k n", p=P)
            sp.dma_start(cols[:, :], io["cols"]).then_inc(params_in, 16)
            for i, name in enumerate(("domain", "condition")):
                sp.dma_start(ids_i[:, i, :], row(name).to_broadcast([P, B])).then_inc(params_in, 16)
            for i, name in enumerate(("theta", "phi")):
                for quarter in range(2):
                    sp.dma_start(angle[:, 0, quarter, i, :], row(name).to_broadcast([P, B])).then_inc(params_in, 16)
            sp.dma_start(vecs[:, 0, :], io["expert_bT"]).then_inc(params_in, 16)
            sp.dma_start(vecs[:, 1, :], io["domain_embT"]).then_inc(params_in, 16)
            sp.dma_start(x2[:, :, :], x2_tiles[0]).then_inc(x2_loaded, 16)
            for i, name in enumerate(("ln1_gamma", "ln1_beta")):
                sp.dma_start(ln1[:, i, :], row(name).to_broadcast([P, D])).then_inc(rows_in, 16)
            for i, name in enumerate(("ln3_gamma", "ln3_beta")):
                sp.dma_start(ln3[:, i, :], row(name).to_broadcast([P, D])).then_inc(rows_in, 16)
            sp.dma_start(up_b[:, :], row("up_b").to_broadcast([P, D])).then_inc(rows_in, 16)
            sp.dma_start(downT[:, :, :], tiled("down_WT")).then_inc(fixed_in, 16)
            sp.dma_start(upT[:, :], io["up_WT"]).then_inc(fixed_in, 16)
            sp.dma_start(experts, io["expert_WT"]).then_inc(experts_in, 16)
            for i, name in enumerate(("b3_sr", "b2_nr", "b2_tsr")):
                sp.dma_start(x4b[:, i, :], row(name).to_broadcast([P, D])).then_inc(weights_in, 16)
            for i, name in enumerate(("w1_nr", "w1_tsr", "w2_nr", "w2_tsr")):
                sp.dma_start(staged[i], tiled(name)).then_inc(weights_in, 16)
            for b in range(B):
                sp.dma_start(w_first[b][:, :, :], tiled("w1_sr")).then_inc(weights_in, 16)
                sp.dma_start(w_last[b][:, :, :], tiled("w3_sr")).then_inc(weights_in, 16)
            sp.dma_start(w_mid[:, :, :], tiled("w2_sr")).then_inc(fixed_in, 16)

            def turn(n, first, last):
                if not last:
                    wait_apart(sp, x3_ready, n * NS + NS, sp_gate)
                    sp.dma_start(x2[:, :, :], x2_tiles[n + 1]).then_inc(x2_loaded, 16)
                wait_apart(sp, y_ready, n * NS + NS, sp_gate)
                sp.dma_start(out_tiles[n], y[:, :, :]).then_inc(y_stored, 16)

            turns(sp, N, turn)
            sp.wait_ge(y_stored, 16 * N)

        @block.gpsimd
        def _(pool):
            make_identity(pool, ident, zeroed, ident_ready)
            pool.iota(number_i[:, :], pattern=[[1, EXPERTS]], base=0, channel_multiplier=0).then_inc(numbered, 1)
            pool.wait_ge(rows_in, 16 * 5)

            def residual_bias(n):
                pool.wait_ge(x2_loaded, n * 16 + 16)
                pool.wait_ge(x2_turned, n * KD + KD)
                for s in range(NS):
                    pool.tensor_tensor(x2[:, s, :], x2[:, s, :], up_b[:, :], ALU.add).then_inc(up_b_added, 1)

            def rotation(n, b):
                for s in range(NS):
                    pool.wait_ge(norm1.done, n * Norm.SIZE + Norm.N_VAR + 1 + s + 1)
                    if s:
                        pool.wait_ge(x4_ready, n * NS + s)
                    else:
                        wait(pool, x4_ready, n * NS)
                    pairs = lambda ap: ap.rearrange("p (g u) -> p g u", u=2)
                    for u in range(2):
                        pool.tensor_tensor(pairs(swapped[:, :])[:, :, u], pairs(x3[:, s, :])[:, :, 1 - u],
                                           pairs(rot[b][:, 1, :])[:, :, u], ALU.mult).then_inc(swap_done, 1)

            def last_bias(n, b):
                wait(pool, y_sum, n * NS)
                pool.wait_ge(x4_ready, n * NS + NS)
                for s in range(NS):
                    pool.tensor_tensor(x4b[:, s, :], x4[:, s, :], b_last[b][:, :], ALU.add).then_inc(x4b_ready, 1)

            pool.wait_ge(prep, N_PREP)
            residual_bias(0)
            rotation(0, 0)

            def chunk(n, b, b_next):
                last_bias(n, b)
                if b_next is not None:
                    residual_bias(n + 1)
                    rotation(n + 1, b_next)

            batch_turns(pool, B, NC, chunk)

        @block.vector
        def _(dve):
            st = Steps(prep)
            done = lambda: dve.wait_ge(prep, st.n)
            dve.wait_ge(params_in, 16 * 9)
            st.mark(dve.tensor_scalar(angle[:, 1, :, :, :], angle[:, 0, :, :, :], 1.0 / (2 * math.pi), ROUND,
                                      ALU.mult, ALU.add))
            done()
            st.mark(dve.tensor_scalar(angle[:, 2, :, :, :], angle[:, 1, :, :, :], ROUND, None, ALU.subtract))
            for part in (TWO_PI_1, TWO_PI_2, TWO_PI_3):
                done()
                st.mark(dve.scalar_tensor_tensor(out=angle[:, 0, :, :, :], in0=angle[:, 2, :, :, :], scalar=-part,
                                                 in1=angle[:, 0, :, :, :], op0=ALU.mult, op1=ALU.add))
            done()
            st.mark(dve.tensor_scalar(angle[:, 0, 1, :, :], angle[:, 0, 1, :, :], math.pi / 2, None, ALU.add))
            done()
            st.mark(dve.tensor_scalar(angle[:, 1, 1, :, :], angle[:, 0, 1, :, :], math.pi, -2 * math.pi,
                                      ALU.is_gt, ALU.mult))
            done()
            st.mark(dve.tensor_tensor(angle[:, 0, 1, :, :], angle[:, 0, 1, :, :], angle[:, 1, 1, :, :], ALU.add))
            done()
            k = st.mark(dve.tensor_scalar(angle[:, 3, :, :, :], angle[:, 0, :, :, :], -PI_INSIDE, PI_INSIDE,
                                          ALU.max, ALU.min))
            assert k == N_TURN
            dve.wait_ge(numbered, 1)
            st.mark(dve.tensor_copy(number[:, :], number_i[:, :]))
            st.mark(dve.tensor_copy(ids[:, :, :], ids_i[:, :, :]))
            done()
            st.mark(dve.tensor_scalar(clipped[:, :], ids[:, 0, :], 0.0, EXPERTS - 1.0, ALU.max, ALU.min))
            for i in range(3):
                st.mark(dve.tensor_scalar(case[:, i, :], ids[:, 1, :], float(i), None, ALU.is_equal))
            done()
            st.mark(dve.tensor_tensor(valid[:, 0, :], clipped[:, :], ids[:, 0, :], ALU.is_equal))
            st.mark(dve.tensor_scalar(not_sr[:, :], case[:, 2, :], -1.0, 1.0, ALU.mult, ALU.add))
            done()
            st.mark(dve.tensor_scalar(valid[:, 1, :], valid[:, 0, :], -1.0, 1.0, ALU.mult, ALU.add))
            for b in range(B):
                st.mark(dve.tensor_scalar(onehot[:, b, :], number[:, :], clipped[:, b:b + 1], None, ALU.is_equal))
            dve.wait_ge(experts_in, 16)
            for b in range(B):
                done()
                st.mark(dve.tensor_scalar(expertT[b][:, :], experts[:, 0, :], onehot[:, b, 0:1], None, ALU.mult))
                for e in range(1, EXPERTS):
                    done()
                    st.mark(dve.scalar_tensor_tensor(out=expertT[b][:, :], in0=experts[:, e, :],
                                                     scalar=onehot[:, b, e:e + 1], in1=expertT[b][:, :],
                                                     op0=ALU.mult, op1=ALU.add))
                done()
                st.mark(dve.tensor_scalar(expertT[b][:, :], expertT[b][:, :], valid[:, 0, b:b + 1], None, ALU.mult))
                dve.wait_ge(ident_ready, 1)
                done()
                st.mark(dve.scalar_tensor_tensor(out=expertT[b][:, :], in0=ident[:, :], scalar=valid[:, 1, b:b + 1],
                                                 in1=expertT[b][:, :], op0=ALU.mult, op1=ALU.add))
                for i in range(2):
                    done()
                    st.mark(dve.tensor_tensor(picked[:, :], vecs[:, i, :], onehot[:, b, :], ALU.mult))
                    done()
                    st.mark(dve.tensor_reduce(sums[:, i:i + 1], picked[:, :], AX.X, ALU.add))
                done()
                st.mark(dve.scalar_tensor_tensor(out=expert_bias[:, b:b + 1], in0=sums[:, 0:1],
                                                 scalar=valid[:, 0, b:b + 1], in1=sums[:, 1:2],
                                                 op0=ALU.mult, op1=ALU.add))
            dve.wait_ge(rows_in, 16 * 5)
            dve.wait_ge(turned_done, 1)
            st.mark(dve.tensor_scalar(minus_sin[:, :, :], turned[:, 0, :, :], -1.0, None, ALU.mult))
            done()
            quads = lambda ap: ap.rearrange("p (g t u) -> p g t u", t=2, u=2)
            for b in range(B):
                for t in range(2):
                    cos, sin, neg = turned[:, 1, t, b:b + 1], turned[:, 0, t, b:b + 1], minus_sin[:, t, b:b + 1]
                    st.mark(dve.tensor_scalar(quads(rot[b][:, 0, :])[:, :, t, :], quads(ln1[:, 0, :])[:, :, t, :],
                                              cos, None, ALU.mult))
                    st.mark(dve.tensor_scalar(quads(rot[b][:, 2, :])[:, :, t, :], quads(ln1[:, 1, :])[:, :, t, :],
                                              cos, None, ALU.mult))
                    done()
                    for u, factor in ((0, sin), (1, neg)):
                        st.mark(dve.tensor_scalar(quads(rot[b][:, 1, :])[:, :, t, u],
                                                  quads(ln1[:, 0, :])[:, :, t, 1 - u], factor, None, ALU.mult))
                        st.mark(dve.scalar_tensor_tensor(out=quads(rot[b][:, 2, :])[:, :, t, u],
                                                         in0=quads(ln1[:, 1, :])[:, :, t, 1 - u], scalar=factor,
                                                         in1=quads(rot[b][:, 2, :])[:, :, t, u],
                                                         op0=ALU.mult, op1=ALU.add))
            dve.wait_ge(weights_in, 16 * (7 + 2 * B))
            at = {name: slice(COLUMNS[name][0], COLUMNS[name][0] + COLUMNS[name][1])
                  for name in ("b1_sr", "b1_nr", "b1_tsr")}
            for b in range(B):
                pick = lambda i: case[:, i, b:b + 1]
                done()
                st.mark(dve.tensor_scalar(w_first[b][:, :, :], w_first[b][:, :, :], pick(2), None, ALU.mult))
                st.mark(dve.tensor_scalar(w_last[b][:, :, :], w_last[b][:, :, :], pick(2), None, ALU.mult))
                st.mark(dve.tensor_scalar(b_first[:, b, :], cols[:, at["b1_sr"]], pick(2), None, ALU.mult))
                st.mark(dve.tensor_scalar(b_last[b][:, :], x4b[:, 0, :], pick(2), None, ALU.mult))
                for i, name in ((0, "b1_nr"), (1, "b1_tsr")):
                    done()
                    for out, part in ((w_first[b][:, :, 0:D], staged[i]), (w_last[b][:, :, :], staged[2 + i]),
                                      (b_first[:, b, 0:KD], cols[:, at[name]]), (b_last[b][:, :], x4b[:, 1 + i, :])):
                        st.mark(dve.scalar_tensor_tensor(out=out, in0=part, scalar=pick(i), in1=out, op0=ALU.mult, op1=ALU.add))
            done()
            assert st.n == N_PREP, st.n

            def adapter_rows(n, b):
                wait(dve, x4_turned, n * KD)
                wait(dve, x4b_ready, n * NS)
                for s in range(NS):
                    dve.wait_ge(up_done, n * NS + s + 1)
                    dve.wait_ge(up_b_added, n * NS + s + 1)
                    dve.tensor_tensor(x3[:, s, :], y_bank[s][:, :], x2[:, s, :], ALU.add).then_inc(x3_ready, 1)
                    dve.wait_ge(x3_ready, n * NS + s + 1)
                    norm1.statistics(dve, s, x3[:, s, :])
                norm1.rows(dve, n, x3, x3)
                for s in range(NS):
                    r = (n * NS + s) * 2
                    dve.wait_ge(norm1.done, n * Norm.SIZE + Norm.N_VAR + 2 + s)
                    dve.tensor_tensor(x4[:, s, :], x3[:, s, :], rot[b][:, 0, :], ALU.mult).then_inc(rot_done, 1)
                    dve.wait_ge(rot_done, r + 1)
                    dve.tensor_tensor(x4[:, s, :], x4[:, s, :], rot[b][:, 2, :], ALU.add).then_inc(rot_done, 1)
                    dve.wait_ge(rot_done, r + 2)
                    dve.wait_ge(swap_done, r + 2)
                    dve.tensor_tensor(x4[:, s, :], x4[:, s, :], swapped[:, :], ALU.add).then_inc(x4_ready, 1)

            def middle(n, b):
                for k in range(KD):
                    i = n * KD + k
                    dve.wait_ge(h1_ready, n * K1 + k + 1)
                    if k >= 2:
                        dve.wait_ge(h2_ready, i - 1)
                    dve.tensor_scalar(kept[:, k % 2, :], h1[:, k, :], not_sr[:, b:b + 1], None, ALU.mult
                                      ).then_inc(kept_ready, 1)
                    dve.wait_ge(g2_ready, i + 1)
                    dve.wait_ge(kept_ready, i + 1)
                    dve.scalar_tensor_tensor(out=h2[:, k, :], in0=g2[:, k % 2, :], scalar=case[:, 2, b:b + 1],
                                             in1=kept[:, k % 2, :], op0=ALU.mult, op1=ALU.add).then_inc(h2_ready, 1)

            def result(n):
                wait(dve, y_stored, n * 16)
                for s in range(NS):
                    dve.wait_ge(last_done, n * NS + s + 1)
                    dve.wait_ge(x4b_ready, n * NS + s + 1)
                    dve.tensor_tensor(y[:, s, :], y_bank[s][:, :], x4b[:, s, :], ALU.add).then_inc(y_sum, 1)
                    dve.wait_ge(y_sum, n * NS + s + 1)
                    norm3.statistics(dve, s, y[:, s, :])
                norm3.rows(dve, n, y, y)
                for s in range(NS):
                    dve.wait_ge(norm3.done, n * Norm.SIZE + Norm.N_VAR + 2 + s)
                    dve.tensor_tensor(y[:, s, :], y[:, s, :], ln3[:, 0, :], ALU.mult).then_inc(y_scaled, 1)
                    dve.wait_ge(y_scaled, n * NS + s + 1)
                    dve.tensor_tensor(y[:, s, :], y[:, s, :], ln3[:, 1, :], ALU.add).then_inc(y_ready, 1)

            adapter_rows(0, 0)

            def chunk(n, b, b_next):
                if b_next is not None:
                    adapter_rows(n + 1, b_next)
                middle(n, b)
                result(n)

            batch_turns(dve, B, NC, chunk)

        @block.scalar
        def _(act):
            act.wait_ge(prep, N_TURN)
            act.activation(turned[:, :, :, :], angle[:, 3, :, :, :], ACT.Sin).then_inc(turned_done, 1)
            act.wait_ge(prep, N_PREP)

            def copy_turned(n, dst, turned_sem, ready):
                for k in range(KD):
                    act.wait_ge(turned_sem, n * KD + k + 1)
                    act.activation(dst[:, k, :], t_bank[k % 2][:, :], ACT.Copy).then_inc(ready, 1)

            def adapter_down(n):
                copy_turned(n, x2T, x2_turned, x2T_ready)
                act.wait_ge(down_done, n + 1)
                act.activation(hid[:, :], w_bank[0][:, :], ACT.Gelu, bias=column(cols, "down_b", 0)
                               ).then_inc(hid_ready, 1)

            def adapter_expert(n, b):
                act.wait_ge(expert_done, n + 1)
                act.activation(hid2[:, :], w_bank[1][:, :], ACT.Identity, bias=expert_bias[:, b:b + 1]
                               ).then_inc(hid2_ready, 1)

            def first_layer(n, b):
                wait(act, h2_ready, n * KD)
                for j in range(K1):
                    act.wait_ge(first_done, n * K1 + j + 1)
                    act.activation(h1[:, j, :], w_bank[j % 2][:, :], ACT.Gelu, bias=b_first[:, b, j:j + 1]
                                   ).then_inc(h1_ready, 1)

            def middle_layer(n):
                for j in range(KD):
                    act.wait_ge(mid_done, n * KD + j + 1)
                    if j >= 2:
                        act.wait_ge(h2_ready, n * KD + j - 1)
                    act.activation(g2[:, j % 2, :], w_bank[j % 2][:, :], ACT.Gelu, bias=column(cols, "b2_sr", j)
                                   ).then_inc(g2_ready, 1)

            def chunk(n, b, b_next):
                ahead = b_next is not None
                if ahead:
                    adapter_down(n + 1)
                first_layer(n, b)
                if ahead:
                    adapter_expert(n + 1, b_next)
                    norm1.deviations(act, n + 1)
                middle_layer(n)
                if ahead:
                    copy_turned(n + 1, x4T, x4_turned, x4T_ready)
                norm3.deviations(act, n)

            adapter_down(0)
            adapter_expert(0, 0)
            norm1.deviations(act, 0)
            copy_turned(0, x4T, x4_turned, x4T_ready)
            batch_turns(act, B, NC, chunk)

        @block.tensor
        def _(pe):
            pe.wait_ge(ident_ready, 1)
            pe.wait_ge(fixed_in, 16 * 3)
            pe.wait_ge(prep, N_PREP)

            def transposes(n, src, turned_sem, ready):
                for k in range(KD):
                    if k >= 2:
                        pe.wait_ge(ready, n * KD + k - 1)
                    for s in range(NS):
                        out = pe.transpose(t_bank[k % 2][:, s * P:(s + 1) * P], src[:, s, k * P:(k + 1) * P],
                                           ident[:, :])
                    out.then_inc(turned_sem, 1)
                pe.wait_ge(ready, n * KD + KD)

            def adapter_down(n):
                pe.wait_ge(x2_loaded, n * 16 + 16)
                transposes(n, x2, x2_turned, x2T_ready)
                wait(pe, g2_ready, (n - 1) * KD)
                for k in range(KD):
                    out = pe.matmul(w_bank[0][:, :], downT[:, k, :], x2T[:, k, :], start=(k == 0), stop=(k == KD - 1))
                out.then_inc(down_done, 1)
                pe.wait_ge(hid_ready, n + 1)

            def adapter_expert(n, b):
                wait(pe, h1_ready, n * K1)
                pe.matmul(w_bank[1][:, :], expertT[b][:, :], hid[:, :], start=True, stop=True).then_inc(expert_done, 1)

            def adapter_up(n):
                pe.wait_ge(hid2_ready, n + 1)
                wait(pe, y_sum, (n - 1) * NS)
                for s in range(NS):
                    pe.matmul(y_bank[s][:, :], hid2[:, s * P:(s + 1) * P], upT[:, :], start=True, stop=True
                              ).then_inc(up_done, 1)

            def first_layer(n, b):
                for j in range(K1):
                    if j >= 2:
                        pe.wait_ge(h1_ready, n * K1 + j - 1)
                    else:
                        wait(pe, g2_ready, n * KD)
                    for k in range(KD):
                        out = pe.matmul(w_bank[j % 2][:, :], w_first[b][:, k, j * P:(j + 1) * P], x4T[:, k, :],
                                        start=(k == 0), stop=(k == KD - 1))
                    out.then_inc(first_done, 1)

            def middle_layer(n, ahead):
                for j in range(KD):
                    if j >= 2:
                        pe.wait_ge(g2_ready, n * KD + j - 1)
                    else:
                        pe.wait_ge(h1_ready, n * K1 + K1)
                    if j == 1 and ahead:
                        pe.wait_ge(hid2_ready, n + 2)
                    for k in range(K1):
                        out = pe.matmul(w_bank[j % 2][:, :], w_mid[:, k, j * P:(j + 1) * P], h1[:, k, :],
                                        start=(k == 0), stop=(k == K1 - 1))
                    out.then_inc(mid_done, 1)

            def last_layer(n, b, ahead):
                pe.wait_ge(h2_ready, n * KD + KD)
                for s in range(NS):
                    pe.wait_ge(x3_ready, (n + 1) * NS + s + 1 if ahead else (n + 1) * NS)
                    for k in range(KD):
                        out = pe.matmul(y_bank[s][:, :], h2[:, k, s * P:(s + 1) * P], w_last[b][:, k, :],
                                        start=(k == 0), stop=(k == KD - 1))
                    out.then_inc(last_done, 1)

            def chunk(n, b, b_next):
                ahead = b_next is not None
                if ahead:
                    adapter_down(n + 1)
                first_layer(n, b)
                if ahead:
                    adapter_expert(n + 1, b_next)
                    adapter_up(n + 1)
                middle_layer(n, ahead)
                last_layer(n, b, ahead)
                if ahead:
                    pe.wait_ge(x4_ready, (n + 2) * NS)
                    transposes(n + 1, x4, x4_turned, x4T_ready)

            adapter_down(0)
            adapter_expert(0, 0)
            adapter_up(0)
            pe.wait_ge(x4_ready, NS)
            transposes(0, x4, x4_turned, x4T_ready)
            batch_turns(pe, B, NC, chunk)


N_TURN = 9
N_PREP = 115


def frequencies():
    half = D // 2
    f = np.exp(np.arange(half, dtype=np.float32) * np.float32(-math.log(10000.0) / (half - 1)))
    return np.concatenate([f, f]).reshape(KD, P).T


def block_program(nc, S, B, io, out):
    scratch = lambda name, shape, dt=F32: nc.dram_tensor(name, shape, dt, kind="Internal").ap()
    xada = scratch("xada", (B * S, D))
    q3 = scratch("q3", (3, B * D, S), BF16)
    k3 = scratch("k3", (3, B * D, S), BF16)
    v = scratch("v", (B * H, P, S // P, HV))
    context = scratch("context", (B * H * (S // P), P, HD))
    x2 = scratch("x2", (B * S, D))
    project_phase(nc, S, B, io, xada, q3, k3, v)
    attention_phase(nc, S, B, io, q3, k3, v, context)
    feed_forward_phase(nc, S, B, io, xada, context, x2)
    adapter_phase(nc, S, B, io, x2, out)


_NAMES = {
    "x": "x", "fside": "fside_Bx16xSxS_0", "mask": "mask_Bx1xSxS_bk0", "timestep": "itok_B_34_63",
    "domain": "itok_B_0_15", "condition": "itok_B_0_2", "theta": "condB_theta", "phi": "condB_phi",
    "W_ada": "L0_cond_W_ada", "Wq": "L0_cond_Wq", "Wk": "L0_cond_Wk", "Wv": "L0_cond_Wv", "Wo": "L0_cond_Wo",
    "W1": "L0_cond_W1", "W2": "L0_cond_W2", "bo": "L0_cond_bo", "b2": "L0_cond_b2", "up_b": "L1_cond_up_b",
    "ln1_gamma": "L1_cond_ln_gamma", "ln1_beta": "L1_cond_ln_beta", "ln3_gamma": "L3_cond_gamma",
    "ln3_beta": "L3_cond_beta", "w1_nr": "L3_cond_w1_nr", "w2_nr": "L3_cond_w2_nr", "w1_tsr": "L3_cond_w1_tsr",
    "w2_tsr": "L3_cond_w2_tsr", "w1_sr": "L3_cond_w1_sr", "w2_sr": "L3_cond_w2_sr", "w3_sr": "L3_cond_w3_sr",
    "b2_nr": "L3_cond_b2_nr", "b2_tsr": "L3_cond_b2_tsr", "b3_sr": "L3_cond_b3_sr",
}
_COLUMN_NAMES = {
    "b_ada": "L0_cond_b_ada", "bq": "L0_cond_bq", "bk": "L0_cond_bk", "bv": "L0_cond_bv", "b1": "L0_cond_b1",
    "g2": "L0_cond_g2", "beta2": "L0_cond_beta2", "down_b": "L1_cond_down_b", "b1_sr": "L3_cond_b1_sr",
    "b2_sr": "L3_cond_b2_sr", "b1_nr": "L3_cond_b1_nr", "b1_tsr": "L3_cond_b1_tsr",
}


def kernel(**inputs):
    import numpy as _np
    import concourse.bacc as _bacc
    from concourse import mybir as _mybir
    from concourse.bass_utils import run_bass_kernel_spmd as _run

    nc = _bacc.Bacc("TRN2", target_bir_lowering=False, num_devices=1)
    arrays, io = {}, {}

    def give(name, a):
        a = _np.ascontiguousarray(a)
        arrays[f"in_{name}"] = a
        io[name] = nc.dram_tensor(f"in_{name}", a.shape, _mybir.dt.from_np(a.dtype), kind="ExternalInput").ap()

    array = lambda name: _np.asarray(inputs[name])
    for name, given in _NAMES.items():
        give(name, array(given))
    give("cols", _np.concatenate([array(_COLUMN_NAMES[c]).reshape(-1, P).T for c in COLUMNS], axis=1))
    give("freqs", frequencies())
    give("down_WT", array("L1_cond_down_W").T)
    give("up_WT", array("L1_cond_up_W").T)
    give("expert_WT", array("L1_cond_expert_W").transpose(2, 0, 1))
    give("expert_bT", array("L1_cond_expert_b").T)
    give("domain_embT", array("L1_cond_domain_emb").T)
    B, S, _ = inputs["x"].shape
    out = nc.dram_tensor("out_0", (B, S, D), _mybir.dt.float32, kind="ExternalOutput").ap()
    block_program(nc, S, B, io, out)
    r = _run(nc, [arrays], core_ids=[0])
    return r.results[0]["out_0"]
```

```python
import math
from contextlib import ExitStack

import numpy as np

import concourse.bass as bass
from concourse import mybir

ALU = mybir.AluOpType
ACT = mybir.ActivationFunctionType
AX = mybir.AxisListType
F32 = mybir.dt.float32
BF16 = mybir.dt.bfloat16
F16 = mybir.dt.float16
F8 = mybir.dt.float8e4
I32 = mybir.dt.int32
U8 = mybir.dt.uint8

P = 128
D = 512
KD = D // P
H = 16
HD = D // H
HV = HD + 1
VP = 3 * HV
CH = 512
NS = CH // P
FF = 2048
KF = FF // P
AD = 128
EXPERTS = 16
EPS = 1e-5
BANK = 512
MASKED = -1.0e30
Q_SCALE = 1.0 / math.sqrt(HD)

COLUMNS = {}
_at = 0
for _name, _width in (("b_ada", 2 * D), ("bq", D), ("bk", D), ("bv", D), ("b1", FF), ("g2", D), ("beta2", D),
                      ("down_b", AD), ("b1_sr", 2 * D), ("b2_sr", D), ("b1_nr", D), ("b1_tsr", D)):
    COLUMNS[_name] = (_at, _width // P)
    _at += _width // P
N_COLUMNS = _at

TWO_PI_1 = 6.28125
TWO_PI_2 = round((2 * math.pi - TWO_PI_1) * 2.0 ** 21) / 2.0 ** 21
TWO_PI_3 = 2 * math.pi - TWO_PI_1 - TWO_PI_2
ROUND = 1.5 * 2.0 ** 23
PI_INSIDE = 3.1415925


class Steps:

    def __init__(self, sem):
        self.sem, self.n = sem, 0

    def mark(self, instruction):
        instruction.then_inc(self.sem, 1)
        self.n += 1
        return self.n


def wait(engine, sem, value):
    if not isinstance(value, int) or value > 0:
        engine.wait_ge(sem, value)


def turns(engine, count, body):
    body(0, True, count == 1)
    if count > 2:
        with engine.Fori(1, count - 1) as n:
            body(n, False, False)
    if count > 1:
        body(count - 1, False, True)


def wait_apart(engine, sem, value, gate):
    engine.wait_ge(sem, value)
    engine.sem_inc(gate, 1)


def column(cols, name, k):
    at, _ = COLUMNS[name]
    return cols[:, at + k:at + k + 1]


def make_identity(pool, ident, s_zero, s_ident):
    pool.memset(ident[:, :], 0.0).then_inc(s_zero, 1)
    pool.wait_ge(s_zero, 1)
    pool.affine_select(out=ident[:, :], in_=ident[:, :], compare_op=ALU.not_equal, fill=1.0, base=0,
                       pattern=[[-1, P]], channel_multiplier=1).then_inc(s_ident, 1)


def project_phase(nc, S, B, io, xada_dram, q3_dram, k3_dram, v_dram, mask8_dram):
    NC = S // CH
    x_tiles = io["x"].rearrange("b (c s p) d -> (b c) p s d", s=NS, p=P)
    xada_tiles = xada_dram.rearrange("(n s p) d -> n p s d", s=NS, p=P)
    q_tiles = q3_dram.rearrange("t (b g p) (c n) -> b g c p t n", b=B, p=P, n=CH)
    k_tiles = k3_dram.rearrange("t (b g p) (c n) -> b g c p t n", b=B, p=P, n=CH)
    v_tiles = v_dram.rearrange("(b h) p (c s) v -> b c p h (s v)", b=B, s=NS)
    mask_tiles = io["mask"].rearrange("b one (c s p) k -> (b one c) p s k", s=NS, p=P)
    mask8_tiles = mask8_dram.rearrange("(n s p) k -> n p s k", s=NS, p=P)

    with ExitStack() as ctx:
        sb = lambda name, shape, dt=F32: ctx.enter_context(nc.sbuf_tensor(name, shape, dt))
        sem = lambda name: ctx.enter_context(nc.semaphore(name))

        ident = sb("a_ident", [P, P])
        ones = sb("a_ones", [P, P])
        cols = sb("a_cols", [P, N_COLUMNS])
        freqs = sb("a_freqs", [P, KD])
        step_i = sb("a_step_i", [P, B], I32)
        step_x = sb("a_step_x", [P, 5, B])
        angle = sb("a_angle", [P, 4, KD, B])
        emb = sb("a_emb", [P, 3, KD, B])
        ada = sb("a_ada", [P, 2 * KD, B])
        diag = sb("a_diag", [P, KD, P])
        scale1 = sb("a_scale1", [P, B, D])
        shift = sb("a_shift", [P, B, D])
        w_ada = sb("a_w_ada", [P, KD, 2 * D])
        wq = sb("a_wq", [P, KD, D])
        wk = sb("a_wk", [P, KD, D])
        wv = sb("a_wv", [P, KD, D])
        bqs = sb("a_bqs", [P, KD])
        x_in = sb("a_x_in", [P, NS, D])
        stats = sb("a_stats", [P, NS, 6])
        moments = sb("a_moments", [P, NS, 2])
        dev = sb("a_dev", [P, NS])
        rstd = sb("a_rstd", [P, NS])
        xada = sb("a_xada", [P, NS, D])
        xT = sb("a_xT", [P, KD, CH])
        qk_f32 = sb("a_qk_f32", [P, 2, CH])
        rest = sb("a_rest", [P, 2, CH])
        parts = sb("a_parts", [P, 2, 3, CH], BF16)
        v_f32 = sb("a_v_f32", [P, H, NS, HD])
        v_out = sb("a_v_out", [P, H, NS, 3, HV], BF16)
        v_rest = v_f32.rearrange("p h s d -> p (h s) d")
        v_part = lambda i: v_out.rearrange("p h s t v -> p (h s) t v")[:, :, i, 0:HD]
        mask_in = sb("a_mask_in", [P, NS, S], U8)
        mask8 = sb("a_mask8", [P, NS, S], F8)
        xT_bank = [ctx.enter_context(nc.psum_tensor(f"a_xT_bank{i}", [P, BANK], F32)) for i in range(2)]
        pr_bank = [ctx.enter_context(nc.psum_tensor(f"a_pr_bank{i}", [P, BANK], F32)) for i in range(6)]

        params_in, weights_in, x_loaded = sem("a_params_in"), sem("a_weights_in"), sem("a_x_loaded")
        zeroed, ident_ready, ones_ready = sem("a_zeroed"), sem("a_ident_ready"), sem("a_ones_ready")
        prep, sin_done, sig_done = sem("a_prep"), sem("a_sin_done"), sem("a_sig_done")
        ada_done, row_done, diag_ready, row_copied = (sem("a_ada_done"), sem("a_row_done"), sem("a_diag_ready"),
                                                      sem("a_row_copied"))
        normed, dev_done = sem("a_normed"), sem("a_dev_done")
        transposed, xT_ready = sem("a_transposed"), sem("a_xT_ready")
        projected, evacuated = sem("a_projected"), sem("a_evacuated")
        split, split_step = sem("a_split"), sem("a_split_step")
        qk_stored = [sem(f"a_qk_stored{r}") for r in range(2)]
        v_stored, xada_stored = sem("a_v_stored"), sem("a_xada_stored")
        f32_copied, v_copied, v_split = sem("a_f32_copied"), sem("a_v_copied"), sem("a_v_split")
        mask_loaded, mask_turned, mask_stored = sem("a_mask_loaded"), sem("a_mask_turned"), sem("a_mask_stored")

        sp_gate, dve_gate, pool_gate = sem("a_sp_gate"), sem("a_dve_gate"), sem("a_pool_gate")
        N_LN = 2 * NS + 2 + 3 * NS
        block = ctx.enter_context(nc.Block())

        @block.sync
        def _(sp):
            sp.dma_start(cols[:, :], io["cols"]).then_inc(params_in, 16)
            sp.dma_start(freqs[:, :], io["freqs"]).then_inc(params_in, 16)
            sp.dma_start(step_i[:, :], io["timestep"].rearrange("(a b) -> a b", a=1).to_broadcast([P, B])
                         ).then_inc(params_in, 16)
            sp.dma_start(w_ada[:, :, :], io["W_ada"].rearrange("(k p) n -> p k n", p=P)).then_inc(params_in, 16)
            sp.dma_start(x_in[:, :, :], x_tiles[0]).then_inc(x_loaded, 16)
            for w, name in ((wq, "Wq"), (wk, "Wk"), (wv, "Wv")):
                sp.dma_start(w[:, :, :], io[name].rearrange("(k p) n -> p k n", p=P)).then_inc(weights_in, 16)
            sp.sem_inc(mask_turned, 1)
            sp.sem_inc(mask_stored, 16)
            for b in range(B):
                with sp.Fori(0, NC) as c:
                    n = c + b * NC
                    wait_apart(sp, mask_turned, n + 1, sp_gate)
                    sp.dma_start(mask_in[:, :, :], mask_tiles[n]).then_inc(mask_loaded, 16)
                    wait_apart(sp, normed, n * N_LN + N_LN, sp_gate)
                    sp.dma_start(xada_tiles[n], xada[:, :, :]).then_inc(xada_stored, 16)
                    for j in range(2 * KD):
                        wait_apart(sp, split, n * (2 * KD) + j + 1, sp_gate)
                        dst = q_tiles if j < KD else k_tiles
                        sp.dma_start(dst[b, j % KD, c], parts[:, j % 2, :, :]).then_inc(qk_stored[j % 2], 16)
                    wait_apart(sp, mask_turned, n + 2, sp_gate)
                    sp.dma_start(mask8_tiles[n], mask8[:, :, :].bitcast(BF16)).then_inc(mask_stored, 16)
                    wait_apart(sp, v_split, n * 3 + 3, sp_gate)
                    sp.dma_start(v_tiles[b, c], v_out.rearrange("p h s t v -> p h (s t v)")).then_inc(v_stored, 16)
            sp.wait_ge(xada_stored, 16 * B * NC)
            for r in range(2):
                sp.wait_ge(qk_stored[r], 16 * KD * B * NC)
            sp.wait_ge(v_stored, 16 * B * NC)
            sp.wait_ge(mask_stored, 16 * B * NC + 16)

        @block.gpsimd
        def _(pool):
            make_identity(pool, ident, zeroed, ident_ready)
            pool.memset(ones[:, :], 1.0).then_inc(ones_ready, 1)
            pool.memset(v_out[:, :, :, 0, HD:HV], 1.0).then_inc(ones_ready, 1)
            pool.memset(v_out[:, :, :, 1:3, HD:HV], 0.0).then_inc(ones_ready, 1)
            for b in range(B):
                with pool.Fori(0, NC) as c:
                    n = c + b * NC
                    for j in range(2 * KD):
                        r = j % 2
                        base = (n * (2 * KD) + j) * 2
                        pool.wait_ge(f32_copied, n * (2 * KD) + j + 1)
                        pool.wait_ge(evacuated, n * (2 * KD + NS) + j + 1)
                        pool.tensor_tensor(rest[:, r, :], qk_f32[:, r, :], parts[:, r, 0, :],
                                           ALU.subtract).then_inc(split_step, 1)
                        wait_apart(pool, split_step, base + 1, pool_gate)
                        pool.tensor_copy(parts[:, r, 1, :], rest[:, r, :]).then_inc(split_step, 1)
                        pool.wait_ge(split_step, base + 2)
                        pool.tensor_tensor(parts[:, r, 2, :], rest[:, r, :], parts[:, r, 1, :],
                                           ALU.subtract).then_inc(split, 1)

        @block.vector
        def _(dve):
            st = Steps(prep)
            done = lambda: dve.wait_ge(prep, st.n)
            dve.wait_ge(params_in, 16 * 4)
            for g in range(KD):
                k = st.mark(dve.tensor_scalar(bqs[:, g:g + 1], column(cols, "bq", g), Q_SCALE, None, ALU.mult))
            st.mark(dve.tensor_copy(step_x[:, 0, :], step_i[:, :]))
            done()
            t, q, top, low, left = (step_x[:, i, :] for i in range(5))
            st.mark(dve.tensor_scalar(q, t, 0.01, None, ALU.mult))
            done()
            st.mark(dve.tensor_scalar(top, q, ROUND / 4096, ROUND / 4096, ALU.add, ALU.subtract))
            done()
            st.mark(dve.tensor_tensor(low, q, top, ALU.subtract))
            st.mark(dve.scalar_tensor_tensor(out=left, in0=top, scalar=-100.0, in1=t, op0=ALU.mult, op1=ALU.add))
            done()
            st.mark(dve.scalar_tensor_tensor(out=left, in0=low, scalar=-100.0, in1=left, op0=ALU.mult, op1=ALU.add))
            done()
            st.mark(dve.scalar_tensor_tensor(out=q, in0=left, scalar=0.01, in1=q, op0=ALU.mult, op1=ALU.add))
            done()
            st.mark(dve.tensor_scalar(top, q, 4000.0, None, ALU.mult))
            done()
            for b in range(B):
                st.mark(dve.tensor_scalar(angle[:, 0, :, b], freqs[:, :], step_x[:, 2, b:b + 1], None, ALU.mult))
            done()
            st.mark(dve.tensor_scalar(angle[:, 1, :, :], angle[:, 0, :, :], 1.0 / (2 * math.pi), ROUND,
                                      ALU.mult, ALU.add))
            done()
            st.mark(dve.tensor_scalar(angle[:, 2, :, :], angle[:, 1, :, :], ROUND, None, ALU.subtract))
            for part in (TWO_PI_1, TWO_PI_2, TWO_PI_3):
                done()
                st.mark(dve.scalar_tensor_tensor(out=angle[:, 0, :, :], in0=angle[:, 2, :, :], scalar=-part,
                                                 in1=angle[:, 0, :, :], op0=ALU.mult, op1=ALU.add))
            done()
            half = KD // 2
            st.mark(dve.tensor_scalar(angle[:, 0, half:, :], angle[:, 0, half:, :], math.pi / 2, None, ALU.add))
            done()
            st.mark(dve.tensor_scalar(angle[:, 1, half:, :], angle[:, 0, half:, :], math.pi, -2 * math.pi,
                                      ALU.is_gt, ALU.mult))
            done()
            st.mark(dve.tensor_tensor(angle[:, 0, half:, :], angle[:, 0, half:, :], angle[:, 1, half:, :], ALU.add))
            done()
            angle_ready = st.mark(dve.tensor_scalar(angle[:, 3, :, :], angle[:, 0, :, :], -PI_INSIDE, PI_INSIDE,
                                                    ALU.max, ALU.min))
            assert angle_ready == N_ANGLE
            dve.wait_ge(sig_done, 1)
            st.mark(dve.tensor_tensor(emb[:, 2, :, :], emb[:, 0, :, :], emb[:, 1, :, :], ALU.mult))
            assert st.n == N_SILU
            dve.wait_ge(ada_done, 1)
            for j in range(2 * KD):
                st.mark(dve.tensor_scalar(ada[:, j, :], pr_bank[0][:, j * B:(j + 1) * B], column(cols, "b_ada", j),
                                          1.0 if j < KD else 0.0, ALU.add, ALU.add))
            done()
            dve.wait_ge(ident_ready, 1)
            for i, (b, half_at) in enumerate((b, h) for b in range(B) for h in (0, KD)):
                if i:
                    dve.wait_ge(row_done, i)
                for g in range(KD):
                    last = dve.tensor_scalar(diag[:, g, :], ident[:, :], ada[:, half_at + g, b:b + 1], None, ALU.mult)
                last.then_inc(diag_ready, 1)
                dve.wait_ge(row_done, i + 1)
                dst = scale1 if half_at == 0 else shift
                dve.tensor_copy(dst[:, b, :], pr_bank[1][:, :]).then_inc(row_copied, 1)
            dve.wait_ge(row_copied, 2 * B)
            def chunk(n, b):
                ln = Steps(normed)
                upto = lambda k: dve.wait_ge(normed, n * N_LN + k)
                dve.wait_ge(x_loaded, n * 16 + 16)
                for s in range(NS):
                    k = ln.mark(dve.bn_stats(stats[:, s, :], x_in[:, s, :]))
                wait_apart(dve, normed, n * N_LN + k, dve_gate)
                for s in range(NS):
                    k = ln.mark(dve.bn_aggr(moments[:, s, :], stats[:, s, :]))
                upto(k)
                k = ln.mark(dve.tensor_scalar(rstd[:, :], moments[:, :, 1], EPS, None, ALU.add))
                assert k == N_VAR
                dve.wait_ge(dev_done, n + 1)
                k = ln.mark(dve.reciprocal(rstd[:, :], dev[:, :]))
                upto(k)
                wait(dve, transposed, n * KD)
                wait(dve, xada_stored, n * 16)
                for s in range(NS):
                    k = ln.mark(dve.tensor_scalar(xada[:, s, :], x_in[:, s, :], moments[:, s, 0:1],
                                                  rstd[:, s:s + 1], ALU.subtract, ALU.mult))
                upto(k)
                for s in range(NS):
                    k = ln.mark(dve.tensor_tensor(xada[:, s, :], xada[:, s, :], scale1[:, b, :], ALU.mult))
                upto(k)
                for s in range(NS):
                    k = ln.mark(dve.tensor_tensor(xada[:, s, :], xada[:, s, :], shift[:, b, :], ALU.add))
                assert ln.n == N_LN

            def split_values(n):
                dve.wait_ge(v_copied, (n + 1) * NS)
                dve.wait_ge(evacuated, (n + 1) * (2 * KD + NS))
                dve.tensor_tensor(v_rest, v_rest, v_part(0), ALU.subtract).then_inc(v_split, 1)
                dve.wait_ge(v_split, n * 3 + 1)
                dve.tensor_copy(v_part(1), v_rest).then_inc(v_split, 1)
                dve.wait_ge(v_split, n * 3 + 2)
                dve.tensor_tensor(v_part(2), v_rest, v_part(1), ALU.subtract).then_inc(v_split, 1)

            def turn_mask(n):
                wait_apart(dve, mask_loaded, n * 16 + 16, dve_gate)
                wait_apart(dve, mask_stored, n * 16 + 16, dve_gate)
                dve.tensor_copy(mask8[:, :, :], mask_in[:, :, :], saturate=False).then_inc(mask_turned, 1)

            chunk(0, 0)
            turn_mask(0)
            for b in range(B):
                if NC > 1 or b:
                    with dve.Fori(b * NC or 1, (b + 1) * NC) as n:
                        chunk(n, b)
                        split_values(n - 1)
                        turn_mask(n)
            split_values(B * NC - 1)

        @block.scalar
        def _(act):
            act.wait_ge(prep, N_ANGLE)
            act.activation(emb[:, 0, :, :], angle[:, 3, :, :], ACT.Sin).then_inc(sin_done, 1)
            act.wait_ge(sin_done, 1)
            act.activation(emb[:, 1, :, :], emb[:, 0, :, :], ACT.Sigmoid).then_inc(sig_done, 1)
            act.wait_ge(ones_ready, 3)

            def deviations(n):
                act.wait_ge(normed, n * N_LN + N_VAR)
                act.activation(dev[:, :], rstd[:, :], ACT.Sqrt).then_inc(dev_done, 1)

            def chunk(n, first, last):
                for k in range(KD):
                    act.wait_ge(transposed, n * KD + k + 1)
                    act.activation(xT[:, k, :], xT_bank[k % 2][:, :], ACT.Copy).then_inc(xT_ready, 1)
                if not last:
                    act.wait_ge(normed, n * N_LN + N_LN)
                    act.dma_start(x_in[:, :, :], x_tiles[n + 1]).then_inc(x_loaded, 16)
                for j in range(2 * KD):
                    r, g = j % 2, j % KD
                    scale, bias = (Q_SCALE, bqs[:, g:g + 1]) if j < KD else (1.0, column(cols, "bk", g))
                    act.wait_ge(projected, n * (2 * KD + NS) + j + 1)
                    behind = max(0, j - 1)
                    wait(act, split, n * (2 * KD) + behind)
                    act.activation(qk_f32[:, r, :], pr_bank[j % 6][:, :], ACT.Identity, bias=bias, scale=scale
                                   ).then_inc(f32_copied, 1)
                    wait(act, qk_stored[r], (n * KD + j // 2) * 16)
                    act.activation(parts[:, r, 0, :], pr_bank[j % 6][:, :], ACT.Identity, bias=bias, scale=scale
                                   ).then_inc(evacuated, 1)
                    if j == KD and not last:
                        deviations(n + 1)
                wait(act, v_split, n * 3)
                wait(act, v_stored, n * 16)
                for s in range(NS):
                    j = 2 * KD + s
                    values = pr_bank[j % 6][:, :].rearrange("p (h d) -> p h d", h=H)
                    act.wait_ge(projected, n * (2 * KD + NS) + j + 1)
                    act.activation(v_f32[:, :, s, :], values, ACT.Copy).then_inc(v_copied, 1)
                    act.activation(v_out[:, :, s, 0, 0:HD], values, ACT.Copy).then_inc(evacuated, 1)

            deviations(0)
            turns(act, B * NC, chunk)

        @block.tensor
        def _(pe):
            pe.wait_ge(params_in, 16 * 4)
            pe.wait_ge(prep, N_SILU)
            for j in range(2 * KD):
                for k in range(KD):
                    last = pe.matmul(pr_bank[0][:, j * B:(j + 1) * B], w_ada[:, k, j * P:(j + 1) * P],
                                     emb[:, 2, k, :], start=(k == 0), stop=(k == KD - 1))
            last.then_inc(ada_done, 1)
            pe.wait_ge(ones_ready, 1)
            for i in range(2 * B):
                pe.wait_ge(diag_ready, i + 1)
                if i:
                    pe.wait_ge(row_copied, i)
                for g in range(KD):
                    last = pe.matmul(pr_bank[1][:, g * P:(g + 1) * P], ones[:, :], diag[:, g, :],
                                     start=True, stop=True)
                last.then_inc(row_done, 1)
            pe.wait_ge(row_copied, 2 * B)
            pe.wait_ge(weights_in, 16 * 3)
            def chunk(n, first, last):
                pe.wait_ge(normed, n * N_LN + N_LN)
                for k in range(KD):
                    if k >= 2:
                        pe.wait_ge(xT_ready, n * KD + k - 1)
                    for s in range(NS):
                        last = pe.transpose(xT_bank[k % 2][:, s * P:(s + 1) * P], xada[:, s, k * P:(k + 1) * P],
                                            ident[:, :])
                    last.then_inc(transposed, 1)
                wait(pe, evacuated, n * (2 * KD + NS))
                pe.wait_ge(xT_ready, n * KD + KD)
                for j in range(2 * KD + NS):
                    bank = pr_bank[j % 6]
                    if j >= 6:
                        pe.wait_ge(evacuated, n * (2 * KD + NS) + j - 5)
                    for k in range(KD):
                        if j < 2 * KD:
                            w, g = (wq, j) if j < KD else (wk, j - KD)
                            lhsT, rhs = w[:, k, g * P:(g + 1) * P], xT[:, k, :]
                        else:
                            s = j - 2 * KD
                            lhsT, rhs = xT[:, k, s * P:(s + 1) * P], wv[:, k, :]
                        last = pe.matmul(bank[:, :], lhsT, rhs, start=(k == 0), stop=(k == KD - 1))
                    last.then_inc(projected, 1)

            turns(pe, B * NC, chunk)


N_ANGLE = KD + 8 + 2 + 2 + 3 + 4
N_SILU = N_ANGLE + 1
N_VAR = 2 * NS + 1


U = 4
HEAD_DMAS = 17
Q_PARTS = ((0, 0), (0, 2), (1, 1), (1, 2))
K_PARTS = ((0, 2), (1, 0), (0, 2), (1, 1))


def attention_phase(nc, S, B, io, q3_dram, k3_dram, v_dram, mask8_dram, ctx_dram):
    assert B == 2
    NQ = S // P
    NCK = S // BANK
    NG = NQ // U
    TILES = B * H * NQ
    GROUPS = TILES // U
    bias_tiles = io["fside"].rearrange("b h (q p) k -> (b h q) p k", p=P)
    mask_rows = mask8_dram.rearrange("(b q p) k -> b p q k", b=B, p=P)
    q_rows = q3_dram.rearrange("t (n r) k -> n t r k", r=HD)
    k_rows = k3_dram.rearrange("t (n r) k -> n t r k", r=HD)

    with ExitStack() as ctx:
        sb = lambda name, shape, dt=F32: ctx.enter_context(nc.sbuf_tensor(name, shape, dt))
        sem = lambda name: ctx.enter_context(nc.semaphore(name))
        bank = lambda name: ctx.enter_context(nc.psum_tensor(name, [P, BANK], F32))

        ident = sb("b_ident", [P, P])
        mask_diag = sb("b_mask_diag", [P, P], BF16)
        mask = [sb(f"b_mask{b}", [P, NQ, S], F8) for b in range(B)]
        qst = [sb(f"b_qst{i}", [P, 2, S], BF16) for i in range(2)]
        kst = [sb(f"b_kst{i}", [P, 2, S], BF16) for i in range(2)]
        vh = [sb(f"b_vh{i}", [P, NQ, VP], BF16) for i in range(2)]
        bias = [sb(f"b_bias{i}", [P, S]) for i in range(U)]
        scores = [sb(f"b_scores{i}", [P, S]) for i in range(2)]
        chunk_max = [sb(f"b_chunk_max{i}", [P, NCK]) for i in range(2)]
        row_max = [sb(f"b_row_max{i}", [P, 1]) for i in range(2)]
        probs = sb("b_probs", [P, 2, BANK])
        top = [sb(f"b_top{i}", [P, NCK, BANK], F16) for i in range(2)]
        low = [sb(f"b_low{i}", [P, NCK, BANK], BF16) for i in range(2)]
        total = sb("b_total", [P, 2, HV])
        denom = sb("b_denom", [P, 2])
        ctx_out = [sb(f"b_ctx_out{i}", [P, HD]) for i in range(U)]
        s_bank = [bank(f"b_s_bank{i}") for i in range(NCK)]
        t_bank = [bank(f"b_t_bank{i}") for i in range(2)]
        o_bank = [bank(f"b_o_bank{i}") for i in range(2)]

        zeroed, ident_ready, blank_ready = sem("b_zeroed"), sem("b_ident_ready"), sem("b_blank_ready")
        first_mask, mask_loaded = sem("b_first_mask"), sem("b_mask_loaded")
        head_loaded = [sem(f"b_head_loaded{i}") for i in range(2)]
        bias_loaded = [sem(f"b_bias_loaded{i}") for i in range(U)]
        ctx_stored = [sem(f"b_ctx_stored{i}") for i in range(U)]
        qk_done, scored = sem("b_qk_done"), sem("b_scored")
        max_done, shifted, transposed = sem("b_max_done"), sem("b_shifted"), sem("b_transposed")
        exp_done, top_done, low_done = sem("b_exp_done"), sem("b_top_done"), sem("b_low_done")
        pv_done, summed, inverted, ctx_ready = sem("b_pv_done"), sem("b_summed"), sem("b_inverted"), sem("b_ctx_ready")
        sp_gate, dve_gate = sem("b_sp_gate"), sem("b_dve_gate")

        def load_head(queue, h, b):
            row = b * H + h
            for r in range(4):
                rows = slice(HD * r, HD * (r + 1))
                for i in range(2):
                    queue.dma_start(qst[b][rows, i, :], q_rows[row, Q_PARTS[r][i]]).then_inc(head_loaded[b], 16)
                    queue.dma_start(kst[b][rows, i, :], k_rows[row, K_PARTS[r][i]]).then_inc(head_loaded[b], 16)
            queue.dma_start(vh[b][:, :, :], v_dram[row]).then_inc(head_loaded[b], 16)

        block = ctx.enter_context(nc.Block())

        @block.sync
        def _(sp):
            for w in range(U):
                sp.sem_inc(ctx_stored[w], 16)
            load_head(sp, 0, 0)
            sp.dma_start(mask[0][:, 0:U, :].bitcast(BF16), mask_rows[0][:, 0:U, :]).then_inc(first_mask, 16)
            for u in range(U):
                sp.dma_start(bias[u][:, :], bias_tiles[u]).then_inc(bias_loaded[u], 16)
            sp.dma_start(mask[0][:, U:, :].bitcast(BF16), mask_rows[0][:, U:, :]).then_inc(mask_loaded, 16)
            sp.dma_start(mask[1][:, :, :].bitcast(BF16), mask_rows[1]).then_inc(mask_loaded, 16)

            def store(t, w):
                wait_apart(sp, ctx_ready, t + 4, sp_gate)
                sp.dma_start(ctx_dram[t], ctx_out[w][:, :]).then_inc(ctx_stored[w], 16)

            def group(hd, g, rows_next, first=False):
                t0 = (hd * NG + g) * U
                for u in range(U):
                    if rows_next is not None:
                        wait_apart(sp, scored, (t0 + u + 1) * NCK, sp_gate)
                        sp.dma_start(bias[u][:, :], bias_tiles[rows_next + u]).then_inc(bias_loaded[u], 16)
                    if not first or u == U - 1:
                        store(t0 + u - 3, (u + 1) % U)

            def head(h, b, first, last):
                hd = h * B + b
                row = (b * H + h) * NQ
                h_next, b_next = (h, 1) if b == 0 else (h + 1, 0)
                row_next = None if last else (b_next * H + h_next) * NQ
                group(hd, 0, row + U if NG > 1 else row_next, first)
                if not last:
                    wait_apart(sp, qk_done, hd * (NQ * NCK) + 1, sp_gate)
                    wait_apart(sp, pv_done, hd * NQ + 1, sp_gate)
                    load_head(sp, h_next, b_next)
                if NG > 2:
                    with sp.Fori(1, NG - 1) as g:
                        group(hd, g, row + U + g * U)
                if NG > 1:
                    group(hd, NG - 1, row_next)

            head(0, 0, True, False)
            head(0, 1, False, False)
            with sp.Fori(1, H - 1) as h:
                for b in range(B):
                    head(h, b, False, False)
            head(H - 1, 0, False, False)
            head(H - 1, 1, False, True)
            for t in range(TILES - 3, TILES):
                store(t, t % U)
            for w in range(U):
                sp.wait_ge(ctx_stored[w], GROUPS * 16 + 16)

        @block.gpsimd
        def _(pool):
            make_identity(pool, ident, zeroed, ident_ready)
            pool.memset(mask_diag[:, :], 0.0).then_inc(zeroed, 1)
            pool.wait_ge(zeroed, 2)
            pool.affine_select(out=mask_diag[:, :], in_=mask_diag[:, :], compare_op=ALU.not_equal, fill=MASKED,
                               base=0, pattern=[[-1, P]], channel_multiplier=1).then_inc(ident_ready, 1)
            pool.memset(top[1][:, :, :], 0.0).then_inc(blank_ready, 1)
            pool.memset(low[1][:, :, :], 0.0).then_inc(blank_ready, 1)
            pool.memset(vh[1][:, :, :], 0.0).then_inc(blank_ready, 1)

            def tile(g, u):
                t, par = g * U + u, u % 2
                for c in range(NCK):
                    x = t * NCK + c
                    if c == 0:
                        wait(pool, pv_done, t)
                    pool.wait_ge(exp_done, x + 1)
                    pool.wait_ge(top_done, x + 1 + NCK)
                    pool.tensor_tensor(low[par][:, c, :], probs[:, c % 2, :], top[par][:, c, :], ALU.subtract
                                       ).then_inc(low_done, 1)

            pool.sem_inc(low_done, NCK)
            for u in range(U):
                tile(0, u)
            with pool.Fori(1, GROUPS) as g:
                for u in range(U):
                    tile(g, u)

        @block.vector
        def _(dve):
            dve.sem_inc(ctx_ready, 3)

            def context(t, par, w, in_group):
                dve.wait_ge(pv_done, t + 2)
                dve.tensor_reduce(total[:, par, :], o_bank[par][:, 0:VP].rearrange("p (t v) -> p v t", t=3),
                                  AX.X, ALU.add).then_inc(summed, 1)
                dve.wait_ge(summed, t + 1)
                dve.reciprocal(denom[:, par:par + 1], total[:, par, HD:HV]).then_inc(inverted, 1)
                dve.wait_ge(ctx_stored[w], in_group * 16 + 16)
                dve.wait_ge(inverted, t + 1)
                dve.tensor_scalar(ctx_out[w][:, :], total[:, par, 0:HD], denom[:, par:par + 1], None,
                                  ALU.mult).then_inc(ctx_ready, 1)

            def tile(g, u, first):
                t = g * U + u
                par = u % 2
                if u == U - 1:
                    context(t - 3, 0, 0, g)
                elif not first:
                    context(t - 3, (u + 1) % 2, u + 1, g - 1)
                if not (first and u < 2):
                    dve.wait_ge(transposed, (t - 1) * NCK)
                dve.wait_ge(bias_loaded[u], g * 16 + 16)
                for c in range(NCK):
                    cols = slice(c * BANK, (c + 1) * BANK)
                    wait_apart(dve, qk_done, t * NCK + c + 1, dve_gate)
                    dve.tensor_tensor_reduce(scores[par][:, cols], s_bank[c][:, :], bias[u][:, cols], 1.0, -3.0e38,
                                             ALU.add, ALU.max, chunk_max[par][:, c:c + 1]).then_inc(scored, 1)
                dve.wait_ge(scored, (t + 1) * NCK)
                dve.tensor_reduce(row_max[par][:, :], chunk_max[par][:, :], AX.X, ALU.max).then_inc(max_done, 1)
                dve.wait_ge(max_done, t + 1)
                for c in range(NCK):
                    cols = slice(c * BANK, (c + 1) * BANK)
                    dve.tensor_scalar(scores[par][:, cols], scores[par][:, cols], row_max[par][:, 0:1], None,
                                      ALU.subtract).then_inc(shifted, 1)

            for u in range(U):
                tile(0, u, True)
            with dve.Fori(1, GROUPS) as g:
                for u in range(U):
                    tile(g, u, False)
            for t in range(TILES - 3, TILES):
                context(t, t % 2, t % U, t // U)

        @block.scalar
        def _(act):
            act.sem_inc(top_done, NCK)

            def tile(g, u):
                t, par = g * U + u, u % 2
                for c in range(NCK):
                    x = t * NCK + c
                    if c == 0:
                        wait(act, pv_done, t)
                    act.wait_ge(transposed, x + 1)
                    act.wait_ge(low_done, x - 1 + NCK)
                    act.activation(probs[:, c % 2, :], t_bank[c % 2][:, :], ACT.Exp).then_inc(exp_done, 1)
                    act.activation(top[par][:, c, :], t_bank[c % 2][:, :], ACT.Exp).then_inc(top_done, 1)

            for u in range(U):
                tile(0, u)
            with act.Fori(1, GROUPS) as g:
                for u in range(U):
                    tile(g, u)

        @block.tensor
        def _(pe):
            def qk(t, b, q, c):
                for i in range(2):
                    pe.matmul(s_bank[c][:, :], qst[b][:, i, bass.ts(q, P)], kst[b][:, i, bass.ts(c, BANK)],
                              start=(i == 0), stop=False)
                pe.matmul(s_bank[c][:, :], mask_diag[:, :], mask[b][:, q, bass.ts(c, BANK)], start=False, stop=True
                          ).then_inc(qk_done, 1)

            def turn(t, par, c):
                pe.wait_ge(shifted, t * NCK + c + 1)
                pe.wait_ge(top_done, t * NCK + c - 1 + NCK)
                for i in range(BANK // P):
                    last = pe.transpose(t_bank[c % 2][:, i * P:(i + 1) * P],
                                        scores[par][:, c * BANK + i * P:c * BANK + (i + 1) * P], ident[:, :])
                last.then_inc(transposed, 1)

            def pv(t_next, b, par, c):
                if c == 0:
                    pe.wait_ge(ctx_ready, t_next + 1)
                pe.wait_ge(top_done, t_next * NCK + c + 1)
                pe.wait_ge(low_done, t_next * NCK + c + 1)
                for i in range(BANK // P):
                    k = c * (BANK // P) + i
                    tops = (top[par][:, c, i * P:(i + 1) * P], VP)
                    lows = (low[par][:, c, i * P:(i + 1) * P], 2 * HV)
                    for j, (lhsT, width) in enumerate((tops, lows) if k == 0 else (lows, tops)):
                        last = pe.matmul(o_bank[par][:, 0:width], lhsT, vh[b][:, k, 0:width],
                                         start=(k == 0 and j == 0), stop=(k == NQ - 1 and j == 1))
                if c == NCK - 1:
                    last.then_inc(pv_done, 1)

            def tile(h, b, g, u, last):
                t = ((h * B + b) * NG + g) * U + u
                crosses = g == NG - 1 and u == U - 1
                b_next, q_next = (1 - b, 0) if crosses else (b, g * U + u + 1)
                b_before = 1 - b if g == 0 and u == 0 else b

                def score(c):
                    if last and crosses:
                        return
                    if crosses and c == 0:
                        pe.wait_ge(head_loaded[b_next], (h + 1 + b) * (16 * HEAD_DMAS))
                    if u == U - 1 and c == 0:
                        pe.wait_ge(mask_loaded, 32)
                    pe.wait_ge(scored, t * NCK + c + 1)
                    qk(t + 1, b_next, q_next, c)

                scores_left, contexts_left = list(range(NCK)), list(range(NCK))
                for c in range(NCK):
                    turn(t, u % 2, c)
                    for _ in range(2):
                        if scores_left:
                            score(scores_left.pop(0))
                        elif contexts_left:
                            pv(t, b_before, 1 - u % 2, contexts_left.pop(0))
                for c in contexts_left:
                    pv(t, b_before, 1 - u % 2, c)

            def head(h, b, last):
                for g in range(NG):
                    for u in range(U):
                        tile(h, b, g, u, last)

            pe.wait_ge(ident_ready, 2)
            pe.wait_ge(blank_ready, 3)
            pe.wait_ge(head_loaded[0], 16 * HEAD_DMAS)
            pe.wait_ge(first_mask, 16)
            for c in range(NCK):
                qk(0, 0, 0, c)
            with pe.Fori(0, H - 1) as h:
                for b in range(B):
                    head(h, b, False)
            head(H - 1, 0, False)
            head(H - 1, 1, True)
            for c in range(NCK):
                pv(TILES, 1, (TILES - 1) % 2, c)


def batch_turns(engine, B, NC, body):
    for b in range(B):
        first, last = b * NC, (b + 1) * NC - 1
        if b == 0 and NC > 1:
            body(0, 0, 0)
            first = 1
        if last > first:
            with engine.Fori(first, last) as n:
                body(n, b, b)
        body(last, b, b + 1 if b + 1 < B else None)


class Norm:

    N_VAR = 2 * NS + 1
    SIZE = N_VAR + 1 + NS

    def __init__(self, sb, sem, name):
        self.stats = sb(name + "_stats", [P, NS, 6])
        self.moments = sb(name + "_moments", [P, NS, 2])
        self.var = sb(name + "_var", [P, NS])
        self.dev = sb(name + "_dev", [P, NS])
        self.rstd = sb(name + "_rstd", [P, NS])
        self.done, self.dev_done, self.gate = sem(name + "_done"), sem(name + "_dev_done"), sem(name + "_gate")

    def statistics(self, dve, s, row):
        dve.bn_stats(self.stats[:, s, :], row).then_inc(self.done, 1)

    def rows(self, dve, n, out, x):
        base = n * self.SIZE
        wait_apart(dve, self.done, base + NS, self.gate)
        for s in range(NS):
            dve.bn_aggr(self.moments[:, s, :], self.stats[:, s, :]).then_inc(self.done, 1)
        dve.wait_ge(self.done, base + 2 * NS)
        dve.tensor_scalar(self.var[:, :], self.moments[:, :, 1], EPS, None, ALU.add).then_inc(self.done, 1)
        dve.wait_ge(self.dev_done, n + 1)
        dve.reciprocal(self.rstd[:, :], self.dev[:, :]).then_inc(self.done, 1)
        dve.wait_ge(self.done, base + self.N_VAR + 1)
        for s in range(NS):
            dve.tensor_scalar(out[:, s, :], x[:, s, :], self.moments[:, s, 0:1], self.rstd[:, s:s + 1],
                              ALU.subtract, ALU.mult).then_inc(self.done, 1)

    def deviations(self, act, n):
        act.wait_ge(self.done, n * self.SIZE + self.N_VAR)
        act.activation(self.dev[:, :], self.var[:, :], ACT.Sqrt).then_inc(self.dev_done, 1)


def feed_forward_phase(nc, S, B, io, xada_dram, ctx_dram, x2_dram):
    NC = S // CH
    N = B * NC
    ctx_tiles = ctx_dram.rearrange("(h b c s) p d -> b c s p h d", b=B, h=H, s=NS)
    xada_tiles = xada_dram.rearrange("(n s p) d -> n p s d", s=NS, p=P)
    x2_tiles = x2_dram.rearrange("(n s p) d -> n p s d", s=NS, p=P)

    with ExitStack() as ctx:
        sb = lambda name, shape, dt=F32: ctx.enter_context(nc.sbuf_tensor(name, shape, dt))
        sem = lambda name: ctx.enter_context(nc.semaphore(name))

        ident = sb("c_ident", [P, P])
        cols = sb("c_cols", [P, N_COLUMNS])
        b1_sig = sb("c_b1_sig", [P, KF])
        bo_row = sb("c_bo_row", [P, D])
        b2_row = sb("c_b2_row", [P, D])
        wo = sb("c_wo", [P, KD, D])
        w1 = sb("c_w1", [P, KD, FF])
        w2 = sb("c_w2", [P, KF, D])
        ctx_in = sb("c_ctx_in", [P, NS, D])
        xada = sb("c_xada", [P, NS, D])
        ctxT = sb("c_ctxT", [P, KD, CH])
        x1 = sb("c_x1", [P, NS, D])
        x1b = sb("c_x1b", [P, NS, D])
        h = sb("c_h", [P, NS, D])
        hT = sb("c_hT", [P, KD, CH])
        sig = sb("c_sig", [P, 2, CH])
        ff = sb("c_ff", [P, KF, CH])
        x2 = sb("c_x2", [P, NS, D])
        t_bank = [ctx.enter_context(nc.psum_tensor(f"c_t_bank{i}", [P, BANK], F32)) for i in range(2)]
        y_bank = [ctx.enter_context(nc.psum_tensor(f"c_y_bank{i}", [P, BANK], F32)) for i in range(NS)]
        f_bank = [ctx.enter_context(nc.psum_tensor(f"c_f_bank{i}", [P, BANK], F32)) for i in range(2)]
        norm = Norm(sb, sem, "c_norm")

        params_in, wo_in, weights_in = sem("c_params_in"), sem("c_wo_in"), sem("c_weights_in")
        zeroed, ident_ready, b1_ready = sem("c_zeroed"), sem("c_ident_ready"), sem("c_b1_ready")
        ctx_loaded, xada_loaded, x2_stored = sem("c_ctx_loaded"), sem("c_xada_loaded"), sem("c_x2_stored")
        ctx_turned, ctxT_ready = sem("c_ctx_turned"), sem("c_ctxT_ready")
        bo_added, wo_done, x1_ready, x1b_ready = (sem("c_bo_added"), sem("c_wo_done"), sem("c_x1_ready"),
                                                  sem("c_x1b_ready"))
        h_turned, hT_ready = sem("c_h_turned"), sem("c_hT_ready")
        w1_done, sig_ready, ff_ready = sem("c_w1_done"), sem("c_sig_ready"), sem("c_ff_ready")
        w2_done, x2_ready = sem("c_w2_done"), sem("c_x2_ready")
        sp_gate = sem("c_sp_gate")

        block = ctx.enter_context(nc.Block())

        @block.sync
        def _(sp):
            def load_ctx(b, c):
                for s in range(NS):
                    sp.dma_start(ctx_in[:, s, :].rearrange("p (h d) -> p h d", h=H), ctx_tiles[b, c, s]
                                 ).then_inc(ctx_loaded, 16)

            def load_xada(n):
                sp.dma_start(xada[:, :, :], xada_tiles[n]).then_inc(xada_loaded, 16)

            def store_x2(n):
                wait_apart(sp, x2_ready, n * NS + NS, sp_gate)
                sp.dma_start(x2_tiles[n], x2[:, :, :]).then_inc(x2_stored, 16)

            sp.sem_inc(x2_stored, 16)
            sp.dma_start(cols[:, :], io["cols"]).then_inc(params_in, 16)
            load_ctx(0, 0)
            sp.dma_start(wo[:, :, :], io["Wo"].rearrange("(k p) n -> p k n", p=P)).then_inc(wo_in, 16)
            load_xada(0)
            for row, name in ((bo_row, "bo"), (b2_row, "b2")):
                sp.dma_start(row[:, :], io[name].rearrange("(a n) -> a n", a=1).to_broadcast([P, D])
                             ).then_inc(params_in, 16)
            sp.dma_start(w1[:, :, :], io["W1"].rearrange("(k p) n -> p k n", p=P)).then_inc(weights_in, 16)
            sp.dma_start(w2[:, :, :], io["W2"].rearrange("(k p) n -> p k n", p=P)).then_inc(weights_in, 16)

            def ahead(n, b_next, c_next):
                wait_apart(sp, ctx_turned, n * KD + KD, sp_gate)
                load_ctx(b_next, c_next)
                wait_apart(sp, x1_ready, n * NS + NS, sp_gate)
                load_xada(n + 1)

            ahead(0, 0, 1) if NC > 1 else ahead(0, 1, 0) if B > 1 else None
            for b in range(B):
                first = 0 if b else 1
                if NC - 1 > first:
                    with sp.Fori(first, NC - 1) as c:
                        n = c + b * NC
                        ahead(n, b, c + 1)
                        store_x2(n - 1)
                if (b or NC > 1) and b + 1 < B:
                    ahead((b + 1) * NC - 1, b + 1, 0)
                    store_x2((b + 1) * NC - 2)
            if N > 1:
                store_x2(N - 2)
            store_x2(N - 1)
            sp.wait_ge(x2_stored, N * 16 + 16)

        @block.gpsimd
        def _(pool):
            make_identity(pool, ident, zeroed, ident_ready)
            pool.wait_ge(params_in, 16 * 3)

            def turn(n, first, last):
                pool.wait_ge(xada_loaded, n * 16 + 16)
                for s in range(NS):
                    pool.tensor_tensor(xada[:, s, :], xada[:, s, :], bo_row[:, :], ALU.add).then_inc(bo_added, 1)
                pool.wait_ge(x1_ready, n * NS + NS)
                wait(pool, x2_ready, n * NS)
                for s in range(NS):
                    pool.tensor_tensor(x1b[:, s, :], x1[:, s, :], b2_row[:, :], ALU.add).then_inc(x1b_ready, 1)

            turns(pool, N, turn)

        @block.vector
        def _(dve):
            dve.wait_ge(params_in, 16 * 3)
            at, k = COLUMNS["b1"]
            dve.tensor_scalar(b1_sig[:, :], cols[:, at:at + k], 1.702, None, ALU.mult).then_inc(b1_ready, 1)

            def second_residual(n):
                dve.wait_ge(x2_stored, n * 16 + 16)
                for s in range(NS):
                    dve.wait_ge(w2_done, n * NS + s + 1)
                    dve.wait_ge(x1b_ready, n * NS + s + 1)
                    dve.tensor_tensor(x2[:, s, :], y_bank[s][:, :], x1b[:, s, :], ALU.add).then_inc(x2_ready, 1)

            def turn(n, first, last):
                if not first:
                    dve.wait_ge(x1b_ready, n * NS)
                for s in range(NS):
                    dve.wait_ge(wo_done, n * NS + s + 1)
                    dve.wait_ge(bo_added, n * NS + s + 1)
                    dve.tensor_tensor(x1[:, s, :], y_bank[s][:, :], xada[:, s, :], ALU.add).then_inc(x1_ready, 1)
                    dve.wait_ge(x1_ready, n * NS + s + 1)
                    norm.statistics(dve, s, x1[:, s, :])
                wait(dve, h_turned, n * KD)
                norm.rows(dve, n, h, x1)
                if not first:
                    second_residual(n - 1)
                for f in range(KF):
                    dve.wait_ge(sig_ready, n * KF + f + 1)
                    dve.scalar_tensor_tensor(out=ff[:, f, :], in0=f_bank[f % 2][:, :], scalar=column(cols, "b1", f),
                                             in1=sig[:, f % 2, :], op0=ALU.add, op1=ALU.mult).then_inc(ff_ready, 1)

            turns(dve, N, turn)
            second_residual(N - 1)

        @block.scalar
        def _(act):
            act.wait_ge(b1_ready, 1)

            def turn(n, first, last):
                for k in range(KD):
                    act.wait_ge(ctx_turned, n * KD + k + 1)
                    act.activation(ctxT[:, k, :], t_bank[k % 2][:, :], ACT.Identity, bias=column(cols, "bv", k)
                                   ).then_inc(ctxT_ready, 1)
                norm.deviations(act, n)
                for k in range(KD):
                    act.wait_ge(h_turned, n * KD + k + 1)
                    act.activation(hT[:, k, :], t_bank[k % 2][:, :], ACT.Identity, bias=column(cols, "beta2", k),
                                   scale=column(cols, "g2", k)).then_inc(hT_ready, 1)
                for f in range(KF):
                    act.wait_ge(w1_done, n * KF + f + 1)
                    wait(act, ff_ready, n * KF + f - 1 if f >= 2 else n * KF)
                    act.activation(sig[:, f % 2, :], f_bank[f % 2][:, :], ACT.Sigmoid, bias=b1_sig[:, f:f + 1],
                                   scale=1.702).then_inc(sig_ready, 1)

            turns(act, N, turn)

        @block.tensor
        def _(pe):
            pe.wait_ge(ident_ready, 1)

            def transposes(n, src, turned, ready):
                for k in range(KD):
                    if k >= 2:
                        pe.wait_ge(ready, n * KD + k - 1)
                    for s in range(NS):
                        last = pe.transpose(t_bank[k % 2][:, s * P:(s + 1) * P], src[:, s, k * P:(k + 1) * P],
                                            ident[:, :])
                    last.then_inc(turned, 1)
                pe.wait_ge(ready, n * KD + KD)

            def second_product(n):
                pe.wait_ge(ff_ready, n * KF + KF)
                for s in range(NS):
                    pe.wait_ge(x1_ready, (n + 1) * NS + s + 1 if not isinstance(n, int) or n < N - 1 else N * NS)
                    for k in range(KF):
                        last = pe.matmul(y_bank[s][:, :], ff[:, k, s * P:(s + 1) * P], w2[:, k, :],
                                         start=(k == 0), stop=(k == KF - 1))
                    last.then_inc(w2_done, 1)

            def turn(n, first, last):
                pe.wait_ge(ctx_loaded, (n + 1) * (16 * NS))
                transposes(n, ctx_in, ctx_turned, ctxT_ready)
                if first:
                    pe.wait_ge(wo_in, 16)
                for s in range(NS):
                    if not first:
                        pe.wait_ge(x1b_ready, n * NS)
                    for k in range(KD):
                        out = pe.matmul(y_bank[s][:, :], ctxT[:, k, s * P:(s + 1) * P], wo[:, k, :],
                                        start=(k == 0), stop=(k == KD - 1))
                    out.then_inc(wo_done, 1)
                if first:
                    pe.wait_ge(weights_in, 32)
                else:
                    second_product(n - 1)
                pe.wait_ge(norm.done, (n + 1) * Norm.SIZE)
                transposes(n, h, h_turned, hT_ready)
                for f in range(KF):
                    wait(pe, ff_ready, n * KF + f - 1 if f >= 2 else n * KF)
                    for k in range(KD):
                        out = pe.matmul(f_bank[f % 2][:, :], w1[:, k, f * P:(f + 1) * P], hT[:, k, :],
                                        start=(k == 0), stop=(k == KD - 1))
                    out.then_inc(w1_done, 1)

            turns(pe, N, turn)
            second_product(N - 1)


def adapter_phase(nc, S, B, io, x2_dram, out):
    NC = S // CH
    N = B * NC
    x2_tiles = x2_dram.rearrange("(n s p) d -> n p s d", s=NS, p=P)
    out_tiles = out.rearrange("b (c s p) d -> (b c) p s d", s=NS, p=P)
    K1 = 2 * KD

    with ExitStack() as ctx:
        sb = lambda name, shape, dt=F32: ctx.enter_context(nc.sbuf_tensor(name, shape, dt))
        sem = lambda name: ctx.enter_context(nc.semaphore(name))

        ident = sb("d_ident", [P, P])
        cols = sb("d_cols", [P, N_COLUMNS])
        ids_i = sb("d_ids_i", [P, 2, B], I32)
        ids = sb("d_ids", [P, 2, B])
        number = sb("d_number", [P, EXPERTS])
        number_i = sb("d_number_i", [P, EXPERTS], I32)
        clipped = sb("d_clipped", [P, B])
        valid = sb("d_valid", [P, 4, B])
        onehot = sb("d_onehot", [P, B, EXPERTS])
        case = sb("d_case", [P, 3, B])
        not_sr = sb("d_not_sr", [P, B])
        angle = sb("d_angle", [P, 4, 2, 2, B])
        turned = sb("d_turned", [P, 2, 2, B])
        minus_sin = sb("d_minus_sin", [P, 2, B])
        vecs = sb("d_vecs", [P, 2, EXPERTS])
        picked = sb("d_picked", [P, EXPERTS])
        sums = sb("d_sums", [P, 2])
        expert_bias = sb("d_expert_bias", [P, B])
        expertT = [sb(f"d_expertT{b}", [P, AD]) for b in range(B)]
        downT = sb("d_downT", [P, KD, AD])
        upT = sb("d_upT", [P, D])
        up_b = sb("d_up_b", [P, D])
        ln1 = sb("d_ln1", [P, 2, D])
        ln3 = sb("d_ln3", [P, 2, D])
        rot = [sb(f"d_rot{b}", [P, 3, D]) for b in range(B)]
        w_first = [sb(f"d_w_first{b}", [P, KD, 2 * D]) for b in range(B)]
        w_mid = sb("d_w_mid", [P, K1, D])
        w_last = [sb(f"d_w_last{b}", [P, KD, D]) for b in range(B)]
        b_first = sb("d_b_first", [P, B, K1])
        b_last = [sb(f"d_b_last{b}", [P, D]) for b in range(B)]

        x2 = sb("d_x2", [P, NS, D])
        x2T = sb("d_x2T", [P, KD, CH])
        hid = sb("d_hid", [P, CH])
        hid2 = sb("d_hid2", [P, CH])
        x3 = sb("d_x3", [P, NS, D])
        x4 = sb("d_x4", [P, NS, D])
        swapped = sb("d_swapped", [P, D])
        x4b = sb("d_x4b", [P, NS, D])
        x4T = sb("d_x4T", [P, KD, CH])
        h1 = sb("d_h1", [P, K1, CH])
        g2 = sb("d_g2", [P, 2, CH])
        kept = sb("d_kept", [P, 2, CH])
        h2 = sb("d_h2", [P, KD, CH])
        y = sb("d_y", [P, NS, D])
        staged = [h1[:, KD * i:KD * (i + 1), :] for i in range(2)] + [h2[:, :, :], x4T[:, :, :]]
        experts = y[:, :, :].rearrange("p s (e o) -> p (s e) o", o=AD)
        t_bank = [ctx.enter_context(nc.psum_tensor(f"d_t_bank{i}", [P, BANK], F32)) for i in range(2)]
        y_bank = [ctx.enter_context(nc.psum_tensor(f"d_y_bank{i}", [P, BANK], F32)) for i in range(NS)]
        w_bank = [ctx.enter_context(nc.psum_tensor(f"d_w_bank{i}", [P, BANK], F32)) for i in range(2)]
        norm1, norm3 = Norm(sb, sem, "d_norm1"), Norm(sb, sem, "d_norm3")

        params_in, experts_in, weights_in = sem("d_params_in"), sem("d_experts_in"), sem("d_weights_in")
        fixed_in, mid_in, rows_in = sem("d_fixed_in"), sem("d_mid_in"), sem("d_rows_in")
        x2_loaded, y_stored = sem("d_x2_loaded"), sem("d_y_stored")
        zeroed, ident_ready, numbered = sem("d_zeroed"), sem("d_ident_ready"), sem("d_numbered")
        prep, turned_done = sem("d_prep"), sem("d_turned_done")
        x2_turned, x2T_ready, up_b_added = sem("d_x2_turned"), sem("d_x2T_ready"), sem("d_up_b_added")
        down_done, hid_ready, expert_done, hid2_ready = (sem("d_down_done"), sem("d_hid_ready"),
                                                         sem("d_expert_done"), sem("d_hid2_ready"))
        up_done, x3_ready = sem("d_up_done"), sem("d_x3_ready")
        swap_done, rot_done, x4_ready, x4b_ready = (sem("d_swap_done"), sem("d_rot_done"), sem("d_x4_ready"),
                                                    sem("d_x4b_ready"))
        x4_turned, x4T_ready = sem("d_x4_turned"), sem("d_x4T_ready")
        first_done, h1_ready, mid_done, g2_ready = (sem("d_first_done"), sem("d_h1_ready"), sem("d_mid_done"),
                                                    sem("d_g2_ready"))
        kept_ready, h2_ready, last_done = sem("d_kept_ready"), sem("d_h2_ready"), sem("d_last_done")
        y_sum, y_scaled, y_ready = sem("d_y_sum"), sem("d_y_scaled"), sem("d_y_ready")
        sp_gate = sem("d_sp_gate")

        block = ctx.enter_context(nc.Block())

        @block.sync
        def _(sp):
            row = lambda name: io[name].rearrange("(a n) -> a n", a=1)
            tiled = lambda name: io[name].rearrange("(k p) n -> p k n", p=P)
            sp.dma_start(cols[:, :], io["cols"]).then_inc(params_in, 16)
            for i, name in enumerate(("domain", "condition")):
                sp.dma_start(ids_i[:, i, :], row(name).to_broadcast([P, B])).then_inc(params_in, 16)
            for i, name in enumerate(("theta", "phi")):
                for quarter in range(2):
                    sp.dma_start(angle[:, 0, quarter, i, :], row(name).to_broadcast([P, B])).then_inc(params_in, 16)
            sp.dma_start(vecs[:, 0, :], io["expert_bT"]).then_inc(params_in, 16)
            sp.dma_start(vecs[:, 1, :], io["domain_embT"]).then_inc(params_in, 16)
            sp.dma_start(x2[:, :, :], x2_tiles[0]).then_inc(x2_loaded, 16)
            for i, name in enumerate(("ln1_gamma", "ln1_beta")):
                sp.dma_start(ln1[:, i, :], row(name).to_broadcast([P, D])).then_inc(rows_in, 16)
            for i, name in enumerate(("ln3_gamma", "ln3_beta")):
                sp.dma_start(ln3[:, i, :], row(name).to_broadcast([P, D])).then_inc(rows_in, 16)
            sp.dma_start(up_b[:, :], row("up_b").to_broadcast([P, D])).then_inc(rows_in, 16)
            sp.dma_start(downT[:, :, :], tiled("down_WT")).then_inc(fixed_in, 16)
            sp.dma_start(upT[:, :], io["up_WT"]).then_inc(fixed_in, 16)
            sp.dma_start(experts, io["expert_WT"]).then_inc(experts_in, 16)
            for i, name in enumerate(("b3_sr", "b2_nr", "b2_tsr")):
                sp.dma_start(x4b[:, i, :], row(name).to_broadcast([P, D])).then_inc(weights_in, 16)
            for i, name in enumerate(("w1_nr", "w1_tsr", "w2_nr", "w2_tsr")):
                sp.dma_start(staged[i], tiled(name)).then_inc(weights_in, 16)
            for b in range(B):
                sp.dma_start(w_first[b][:, :, :], tiled("w1_sr")).then_inc(weights_in, 16)
                sp.dma_start(w_last[b][:, :, :], tiled("w3_sr")).then_inc(weights_in, 16)
            sp.dma_start(w_mid[:, :, :], tiled("w2_sr")).then_inc(mid_in, 16)

            def load(n):
                wait_apart(sp, x3_ready, n * NS, sp_gate)
                sp.dma_start(x2[:, :, :], x2_tiles[n]).then_inc(x2_loaded, 16)

            def store(n):
                wait_apart(sp, y_ready, n * NS + NS, sp_gate)
                sp.dma_start(out_tiles[n], y[:, :, :]).then_inc(y_stored, 16)

            if N > 1:
                load(1)
            if N > 2:
                with sp.Fori(0, N - 2) as n:
                    load(n + 2)
                    store(n)
            for n in range(max(0, N - 2), N):
                store(n)
            sp.wait_ge(y_stored, 16 * N)

        @block.gpsimd
        def _(pool):
            make_identity(pool, ident, zeroed, ident_ready)
            pool.iota(number_i[:, :], pattern=[[1, EXPERTS]], base=0, channel_multiplier=0).then_inc(numbered, 1)
            pool.wait_ge(rows_in, 16 * 5)

            def residual_bias(n):
                pool.wait_ge(x2_loaded, n * 16 + 16)
                pool.wait_ge(x2_turned, n * KD + KD)
                for s in range(NS):
                    pool.tensor_tensor(x2[:, s, :], x2[:, s, :], up_b[:, :], ALU.add).then_inc(up_b_added, 1)

            def rotation(n, b):
                for s in range(NS):
                    pool.wait_ge(norm1.done, n * Norm.SIZE + Norm.N_VAR + 1 + s + 1)
                    if s:
                        pool.wait_ge(x4_ready, n * NS + s)
                    else:
                        wait(pool, x4_ready, n * NS)
                    pairs = lambda ap: ap.rearrange("p (g u) -> p g u", u=2)
                    for u in range(2):
                        pool.tensor_tensor(pairs(swapped[:, :])[:, :, u], pairs(x3[:, s, :])[:, :, 1 - u],
                                           pairs(rot[b][:, 1, :])[:, :, u], ALU.mult).then_inc(swap_done, 1)

            def last_bias(n, b):
                wait(pool, y_sum, n * NS)
                pool.wait_ge(x4_ready, n * NS + NS)
                for s in range(NS):
                    pool.tensor_tensor(x4b[:, s, :], x4[:, s, :], b_last[b][:, :], ALU.add).then_inc(x4b_ready, 1)

            residual_bias(0)
            pool.wait_ge(prep, N_PREP)
            rotation(0, 0)

            def chunk(n, b, b_next):
                last_bias(n, b)
                if b_next is not None:
                    residual_bias(n + 1)
                    rotation(n + 1, b_next)

            batch_turns(pool, B, NC, chunk)

        @block.vector
        def _(dve):
            st = Steps(prep)
            done = lambda: dve.wait_ge(prep, st.n)
            dve.wait_ge(params_in, 16 * 9)
            st.mark(dve.tensor_scalar(angle[:, 1, :, :, :], angle[:, 0, :, :, :], 1.0 / (2 * math.pi), ROUND,
                                      ALU.mult, ALU.add))
            done()
            st.mark(dve.tensor_scalar(angle[:, 2, :, :, :], angle[:, 1, :, :, :], ROUND, None, ALU.subtract))
            for part in (TWO_PI_1, TWO_PI_2, TWO_PI_3):
                done()
                st.mark(dve.scalar_tensor_tensor(out=angle[:, 0, :, :, :], in0=angle[:, 2, :, :, :], scalar=-part,
                                                 in1=angle[:, 0, :, :, :], op0=ALU.mult, op1=ALU.add))
            done()
            st.mark(dve.tensor_scalar(angle[:, 0, 1, :, :], angle[:, 0, 1, :, :], math.pi / 2, None, ALU.add))
            done()
            st.mark(dve.tensor_scalar(angle[:, 1, 1, :, :], angle[:, 0, 1, :, :], math.pi, -2 * math.pi,
                                      ALU.is_gt, ALU.mult))
            done()
            st.mark(dve.tensor_tensor(angle[:, 0, 1, :, :], angle[:, 0, 1, :, :], angle[:, 1, 1, :, :], ALU.add))
            done()
            k = st.mark(dve.tensor_scalar(angle[:, 3, :, :, :], angle[:, 0, :, :, :], -PI_INSIDE, PI_INSIDE,
                                          ALU.max, ALU.min))
            assert k == N_TURN
            dve.wait_ge(numbered, 1)
            st.mark(dve.tensor_copy(number[:, :], number_i[:, :]))
            st.mark(dve.tensor_copy(ids[:, :, :], ids_i[:, :, :]))
            done()
            st.mark(dve.tensor_scalar(clipped[:, :], ids[:, 0, :], 0.0, EXPERTS - 1.0, ALU.max, ALU.min))
            for i in range(3):
                st.mark(dve.tensor_scalar(case[:, i, :], ids[:, 1, :], float(i), None, ALU.is_equal))
            done()
            st.mark(dve.tensor_tensor(valid[:, 0, :], clipped[:, :], ids[:, 0, :], ALU.is_equal))
            st.mark(dve.tensor_scalar(not_sr[:, :], case[:, 2, :], -1.0, 1.0, ALU.mult, ALU.add))
            done()
            st.mark(dve.tensor_scalar(valid[:, 1, :], valid[:, 0, :], -1.0, 1.0, ALU.mult, ALU.add))
            for b in range(B):
                st.mark(dve.tensor_scalar(onehot[:, b, :], number[:, :], clipped[:, b:b + 1], None, ALU.is_equal))
            dve.wait_ge(experts_in, 16)
            for b in range(B):
                done()
                st.mark(dve.tensor_scalar(expertT[b][:, :], experts[:, 0, :], onehot[:, b, 0:1], None, ALU.mult))
                for e in range(1, EXPERTS):
                    done()
                    st.mark(dve.scalar_tensor_tensor(out=expertT[b][:, :], in0=experts[:, e, :],
                                                     scalar=onehot[:, b, e:e + 1], in1=expertT[b][:, :],
                                                     op0=ALU.mult, op1=ALU.add))
                done()
                st.mark(dve.tensor_scalar(expertT[b][:, :], expertT[b][:, :], valid[:, 0, b:b + 1], None, ALU.mult))
                dve.wait_ge(ident_ready, 1)
                done()
                st.mark(dve.scalar_tensor_tensor(out=expertT[b][:, :], in0=ident[:, :], scalar=valid[:, 1, b:b + 1],
                                                 in1=expertT[b][:, :], op0=ALU.mult, op1=ALU.add))
                for i in range(2):
                    done()
                    st.mark(dve.tensor_tensor(picked[:, :], vecs[:, i, :], onehot[:, b, :], ALU.mult))
                    done()
                    st.mark(dve.tensor_reduce(sums[:, i:i + 1], picked[:, :], AX.X, ALU.add))
                done()
                st.mark(dve.scalar_tensor_tensor(out=expert_bias[:, b:b + 1], in0=sums[:, 0:1],
                                                 scalar=valid[:, 0, b:b + 1], in1=sums[:, 1:2],
                                                 op0=ALU.mult, op1=ALU.add))
            assert st.n == N_EXPERT, st.n
            dve.wait_ge(rows_in, 16 * 5)
            dve.wait_ge(turned_done, 1)
            st.mark(dve.tensor_scalar(minus_sin[:, :, :], turned[:, 0, :, :], -1.0, None, ALU.mult))
            done()
            quads = lambda ap: ap.rearrange("p (g t u) -> p g t u", t=2, u=2)
            for b in range(B):
                for t in range(2):
                    cos, sin, neg = turned[:, 1, t, b:b + 1], turned[:, 0, t, b:b + 1], minus_sin[:, t, b:b + 1]
                    st.mark(dve.tensor_scalar(quads(rot[b][:, 0, :])[:, :, t, :], quads(ln1[:, 0, :])[:, :, t, :],
                                              cos, None, ALU.mult))
                    st.mark(dve.tensor_scalar(quads(rot[b][:, 2, :])[:, :, t, :], quads(ln1[:, 1, :])[:, :, t, :],
                                              cos, None, ALU.mult))
                    done()
                    for u, factor in ((0, sin), (1, neg)):
                        st.mark(dve.tensor_scalar(quads(rot[b][:, 1, :])[:, :, t, u],
                                                  quads(ln1[:, 0, :])[:, :, t, 1 - u], factor, None, ALU.mult))
                        st.mark(dve.scalar_tensor_tensor(out=quads(rot[b][:, 2, :])[:, :, t, u],
                                                         in0=quads(ln1[:, 1, :])[:, :, t, 1 - u], scalar=factor,
                                                         in1=quads(rot[b][:, 2, :])[:, :, t, u],
                                                         op0=ALU.mult, op1=ALU.add))
            dve.wait_ge(weights_in, 16 * (7 + 2 * B))
            at = {name: slice(COLUMNS[name][0], COLUMNS[name][0] + COLUMNS[name][1])
                  for name in ("b1_sr", "b1_nr", "b1_tsr")}
            for b in range(B):
                pick = lambda i: case[:, i, b:b + 1]
                done()
                st.mark(dve.tensor_scalar(w_first[b][:, :, :], w_first[b][:, :, :], pick(2), None, ALU.mult))
                st.mark(dve.tensor_scalar(w_last[b][:, :, :], w_last[b][:, :, :], pick(2), None, ALU.mult))
                st.mark(dve.tensor_scalar(b_first[:, b, :], cols[:, at["b1_sr"]], pick(2), None, ALU.mult))
                st.mark(dve.tensor_scalar(b_last[b][:, :], x4b[:, 0, :], pick(2), None, ALU.mult))
                for i, name in ((0, "b1_nr"), (1, "b1_tsr")):
                    done()
                    for out, part in ((w_first[b][:, :, 0:D], staged[i]), (w_last[b][:, :, :], staged[2 + i]),
                                      (b_first[:, b, 0:KD], cols[:, at[name]]), (b_last[b][:, :], x4b[:, 1 + i, :])):
                        st.mark(dve.scalar_tensor_tensor(out=out, in0=part, scalar=pick(i), in1=out, op0=ALU.mult, op1=ALU.add))
            done()
            assert st.n == N_PREP, st.n

            def adapter_rows(n, b):
                wait(dve, x4_turned, n * KD)
                wait(dve, x4b_ready, n * NS)
                for s in range(NS):
                    dve.wait_ge(up_done, n * NS + s + 1)
                    dve.wait_ge(up_b_added, n * NS + s + 1)
                    dve.tensor_tensor(x3[:, s, :], y_bank[s][:, :], x2[:, s, :], ALU.add).then_inc(x3_ready, 1)
                    dve.wait_ge(x3_ready, n * NS + s + 1)
                    norm1.statistics(dve, s, x3[:, s, :])
                norm1.rows(dve, n, x3, x3)
                for s in range(NS):
                    r = (n * NS + s) * 2
                    dve.wait_ge(norm1.done, n * Norm.SIZE + Norm.N_VAR + 2 + s)
                    dve.tensor_tensor(x4[:, s, :], x3[:, s, :], rot[b][:, 0, :], ALU.mult).then_inc(rot_done, 1)
                    dve.wait_ge(rot_done, r + 1)
                    dve.tensor_tensor(x4[:, s, :], x4[:, s, :], rot[b][:, 2, :], ALU.add).then_inc(rot_done, 1)
                    dve.wait_ge(rot_done, r + 2)
                    dve.wait_ge(swap_done, r + 2)
                    dve.tensor_tensor(x4[:, s, :], x4[:, s, :], swapped[:, :], ALU.add).then_inc(x4_ready, 1)

            def middle(n, b):
                for k in range(KD):
                    i = n * KD + k
                    dve.wait_ge(h1_ready, n * K1 + k + 1)
                    if k >= 2:
                        dve.wait_ge(h2_ready, i - 1)
                    dve.tensor_scalar(kept[:, k % 2, :], h1[:, k, :], not_sr[:, b:b + 1], None, ALU.mult
                                      ).then_inc(kept_ready, 1)
                    dve.wait_ge(g2_ready, i + 1)
                    dve.wait_ge(kept_ready, i + 1)
                    dve.scalar_tensor_tensor(out=h2[:, k, :], in0=g2[:, k % 2, :], scalar=case[:, 2, b:b + 1],
                                             in1=kept[:, k % 2, :], op0=ALU.mult, op1=ALU.add).then_inc(h2_ready, 1)

            def result(n):
                wait(dve, y_stored, n * 16)
                for s in range(NS):
                    dve.wait_ge(last_done, n * NS + s + 1)
                    dve.wait_ge(x4b_ready, n * NS + s + 1)
                    dve.tensor_tensor(y[:, s, :], y_bank[s][:, :], x4b[:, s, :], ALU.add).then_inc(y_sum, 1)
                    dve.wait_ge(y_sum, n * NS + s + 1)
                    norm3.statistics(dve, s, y[:, s, :])
                norm3.rows(dve, n, y, y)
                for s in range(NS):
                    dve.wait_ge(norm3.done, n * Norm.SIZE + Norm.N_VAR + 2 + s)
                    dve.tensor_tensor(y[:, s, :], y[:, s, :], ln3[:, 0, :], ALU.mult).then_inc(y_scaled, 1)
                    dve.wait_ge(y_scaled, n * NS + s + 1)
                    dve.tensor_tensor(y[:, s, :], y[:, s, :], ln3[:, 1, :], ALU.add).then_inc(y_ready, 1)

            adapter_rows(0, 0)

            def chunk(n, b, b_next):
                if b_next is not None:
                    adapter_rows(n + 1, b_next)
                middle(n, b)
                result(n)

            batch_turns(dve, B, NC, chunk)

        @block.scalar
        def _(act):
            act.wait_ge(prep, N_TURN)
            act.activation(turned[:, :, :, :], angle[:, 3, :, :, :], ACT.Sin).then_inc(turned_done, 1)

            def copy_turned(n, dst, turned_sem, ready):
                for k in range(KD):
                    act.wait_ge(turned_sem, n * KD + k + 1)
                    act.activation(dst[:, k, :], t_bank[k % 2][:, :], ACT.Copy).then_inc(ready, 1)

            def adapter_down(n):
                copy_turned(n, x2T, x2_turned, x2T_ready)
                act.wait_ge(down_done, n + 1)
                act.activation(hid[:, :], w_bank[0][:, :], ACT.Gelu, bias=column(cols, "down_b", 0)
                               ).then_inc(hid_ready, 1)

            def adapter_expert(n, b):
                act.wait_ge(expert_done, n + 1)
                act.activation(hid2[:, :], w_bank[1][:, :], ACT.Identity, bias=expert_bias[:, b:b + 1]
                               ).then_inc(hid2_ready, 1)

            def first_layer(n, b):
                wait(act, h2_ready, n * KD)
                for j in range(K1):
                    act.wait_ge(first_done, n * K1 + j + 1)
                    act.activation(h1[:, j, :], w_bank[j % 2][:, :], ACT.Gelu, bias=b_first[:, b, j:j + 1]
                                   ).then_inc(h1_ready, 1)

            def middle_layer(n):
                for j in range(KD):
                    act.wait_ge(mid_done, n * KD + j + 1)
                    if j >= 2:
                        act.wait_ge(h2_ready, n * KD + j - 1)
                    act.activation(g2[:, j % 2, :], w_bank[j % 2][:, :], ACT.Gelu, bias=column(cols, "b2_sr", j)
                                   ).then_inc(g2_ready, 1)

            def chunk(n, b, b_next):
                ahead = b_next is not None
                if ahead:
                    adapter_down(n + 1)
                first_layer(n, b)
                if ahead:
                    adapter_expert(n + 1, b_next)
                    norm1.deviations(act, n + 1)
                middle_layer(n)
                if ahead:
                    copy_turned(n + 1, x4T, x4_turned, x4T_ready)
                norm3.deviations(act, n)

            act.wait_ge(params_in, 16 * 9)
            adapter_down(0)
            act.wait_ge(prep, N_EXPERT)
            adapter_expert(0, 0)
            norm1.deviations(act, 0)
            copy_turned(0, x4T, x4_turned, x4T_ready)
            batch_turns(act, B, NC, chunk)

        @block.tensor
        def _(pe):
            pe.wait_ge(ident_ready, 1)
            pe.wait_ge(fixed_in, 16 * 2)

            def transposes(n, src, turned_sem, ready):
                for k in range(KD):
                    if k >= 2:
                        pe.wait_ge(ready, n * KD + k - 1)
                    for s in range(NS):
                        out = pe.transpose(t_bank[k % 2][:, s * P:(s + 1) * P], src[:, s, k * P:(k + 1) * P],
                                           ident[:, :])
                    out.then_inc(turned_sem, 1)
                pe.wait_ge(ready, n * KD + KD)

            def adapter_down(n):
                pe.wait_ge(x2_loaded, n * 16 + 16)
                transposes(n, x2, x2_turned, x2T_ready)
                wait(pe, g2_ready, (n - 1) * KD)
                for k in range(KD):
                    out = pe.matmul(w_bank[0][:, :], downT[:, k, :], x2T[:, k, :], start=(k == 0), stop=(k == KD - 1))
                out.then_inc(down_done, 1)
                pe.wait_ge(hid_ready, n + 1)

            def adapter_expert(n, b):
                wait(pe, h1_ready, n * K1)
                pe.matmul(w_bank[1][:, :], expertT[b][:, :], hid[:, :], start=True, stop=True).then_inc(expert_done, 1)

            def adapter_up(n):
                pe.wait_ge(hid2_ready, n + 1)
                wait(pe, y_sum, (n - 1) * NS)
                for s in range(NS):
                    pe.matmul(y_bank[s][:, :], hid2[:, s * P:(s + 1) * P], upT[:, :], start=True, stop=True
                              ).then_inc(up_done, 1)

            def first_layer(n, b):
                for j in range(K1):
                    if j >= 2:
                        pe.wait_ge(h1_ready, n * K1 + j - 1)
                    else:
                        wait(pe, g2_ready, n * KD)
                    for k in range(KD):
                        out = pe.matmul(w_bank[j % 2][:, :], w_first[b][:, k, j * P:(j + 1) * P], x4T[:, k, :],
                                        start=(k == 0), stop=(k == KD - 1))
                    out.then_inc(first_done, 1)

            def middle_layer(n, ahead):
                for j in range(KD):
                    if j >= 2:
                        pe.wait_ge(g2_ready, n * KD + j - 1)
                    else:
                        pe.wait_ge(h1_ready, n * K1 + K1)
                    if j == 1 and ahead:
                        pe.wait_ge(hid2_ready, n + 2)
                    for k in range(K1):
                        out = pe.matmul(w_bank[j % 2][:, :], w_mid[:, k, j * P:(j + 1) * P], h1[:, k, :],
                                        start=(k == 0), stop=(k == K1 - 1))
                    out.then_inc(mid_done, 1)

            def last_layer(n, b, ahead):
                pe.wait_ge(h2_ready, n * KD + KD)
                for s in range(NS):
                    pe.wait_ge(x3_ready, (n + 1) * NS + s + 1 if ahead else (n + 1) * NS)
                    for k in range(KD):
                        out = pe.matmul(y_bank[s][:, :], h2[:, k, s * P:(s + 1) * P], w_last[b][:, k, :],
                                        start=(k == 0), stop=(k == KD - 1))
                    out.then_inc(last_done, 1)

            def chunk(n, b, b_next):
                ahead = b_next is not None
                if ahead:
                    adapter_down(n + 1)
                first_layer(n, b)
                if ahead:
                    adapter_expert(n + 1, b_next)
                    adapter_up(n + 1)
                middle_layer(n, ahead)
                last_layer(n, b, ahead)
                if ahead:
                    pe.wait_ge(x4_ready, (n + 2) * NS)
                    transposes(n + 1, x4, x4_turned, x4T_ready)

            adapter_down(0)
            pe.wait_ge(prep, N_EXPERT)
            adapter_expert(0, 0)
            adapter_up(0)
            pe.wait_ge(prep, N_PREP)
            pe.wait_ge(mid_in, 16)
            pe.wait_ge(x4_ready, NS)
            transposes(0, x4, x4_turned, x4T_ready)
            batch_turns(pe, B, NC, chunk)


N_TURN = 9
N_EXPERT = 66
N_PREP = 115


def frequencies():
    half = D // 2
    f = np.exp(np.arange(half, dtype=np.float32) * np.float32(-math.log(10000.0) / (half - 1)))
    return np.concatenate([f, f]).reshape(KD, P).T


def block_program(nc, S, B, io, out):
    scratch = lambda name, shape, dt=F32: nc.dram_tensor(name, shape, dt, kind="Internal").ap()
    xada = scratch("xada", (B * S, D))
    q3 = scratch("q3", (3, B * D, S), BF16)
    k3 = scratch("k3", (3, B * D, S), BF16)
    v = scratch("v", (B * H, P, S // P, VP), BF16)
    mask8 = scratch("mask8", (B * S, S // 2), BF16)
    context = scratch("context", (B * H * (S // P), P, HD))
    x2 = scratch("x2", (B * S, D))
    project_phase(nc, S, B, io, xada, q3, k3, v, mask8)
    attention_phase(nc, S, B, io, q3, k3, v, mask8, context)
    feed_forward_phase(nc, S, B, io, xada, context, x2)
    adapter_phase(nc, S, B, io, x2, out)


_NAMES = {
    "x": "x", "fside": "fside_Bx16xSxS_0", "mask": "mask_Bx1xSxS_bk0", "timestep": "itok_B_34_63",
    "domain": "itok_B_0_15", "condition": "itok_B_0_2", "theta": "condB_theta", "phi": "condB_phi",
    "W_ada": "L0_cond_W_ada", "Wq": "L0_cond_Wq", "Wk": "L0_cond_Wk", "Wv": "L0_cond_Wv", "Wo": "L0_cond_Wo",
    "W1": "L0_cond_W1", "W2": "L0_cond_W2", "bo": "L0_cond_bo", "b2": "L0_cond_b2", "up_b": "L1_cond_up_b",
    "ln1_gamma": "L1_cond_ln_gamma", "ln1_beta": "L1_cond_ln_beta", "ln3_gamma": "L3_cond_gamma",
    "ln3_beta": "L3_cond_beta", "w1_nr": "L3_cond_w1_nr", "w2_nr": "L3_cond_w2_nr", "w1_tsr": "L3_cond_w1_tsr",
    "w2_tsr": "L3_cond_w2_tsr", "w1_sr": "L3_cond_w1_sr", "w2_sr": "L3_cond_w2_sr", "w3_sr": "L3_cond_w3_sr",
    "b2_nr": "L3_cond_b2_nr", "b2_tsr": "L3_cond_b2_tsr", "b3_sr": "L3_cond_b3_sr",
}
_COLUMN_NAMES = {
    "b_ada": "L0_cond_b_ada", "bq": "L0_cond_bq", "bk": "L0_cond_bk", "bv": "L0_cond_bv", "b1": "L0_cond_b1",
    "g2": "L0_cond_g2", "beta2": "L0_cond_beta2", "down_b": "L1_cond_down_b", "b1_sr": "L3_cond_b1_sr",
    "b2_sr": "L3_cond_b2_sr", "b1_nr": "L3_cond_b1_nr", "b1_tsr": "L3_cond_b1_tsr",
}


def kernel(**inputs):
    import numpy as _np
    import concourse.bacc as _bacc
    from concourse import mybir as _mybir
    from concourse.bass_utils import run_bass_kernel_spmd as _run

    nc = _bacc.Bacc("TRN2", target_bir_lowering=False, num_devices=1)
    arrays, io = {}, {}

    def give(name, a):
        a = _np.ascontiguousarray(a)
        arrays[f"in_{name}"] = a
        io[name] = nc.dram_tensor(f"in_{name}", a.shape, _mybir.dt.from_np(a.dtype), kind="ExternalInput").ap()

    array = lambda name: _np.asarray(inputs[name])
    for name, given in _NAMES.items():
        give(name, array(given))
    give("cols", _np.concatenate([array(_COLUMN_NAMES[c]).reshape(-1, P).T for c in COLUMNS], axis=1))
    give("freqs", frequencies())
    give("down_WT", array("L1_cond_down_W").T)
    give("up_WT", array("L1_cond_up_W").T)
    give("expert_WT", array("L1_cond_expert_W").transpose(2, 0, 1))
    give("expert_bT", array("L1_cond_expert_b").T)
    give("domain_embT", array("L1_cond_domain_emb").T)
    B, S, _ = inputs["x"].shape
    out = nc.dram_tensor("out_0", (B, S, D), _mybir.dt.float32, kind="ExternalOutput").ap()
    block_program(nc, S, B, io, out)
    r = _run(nc, [arrays], core_ids=[0])
    return r.results[0]["out_0"]
```

```python
import math
from contextlib import ExitStack

import numpy as np

import concourse.bass as bass
from concourse import mybir

ALU = mybir.AluOpType
ACT = mybir.ActivationFunctionType
AX = mybir.AxisListType
F32 = mybir.dt.float32
BF16 = mybir.dt.bfloat16
F16 = mybir.dt.float16
F32R = mybir.dt.float32r
F8 = mybir.dt.float8e4
I32 = mybir.dt.int32
U8 = mybir.dt.uint8

P = 128
D = 512
KD = D // P
H = 16
HD = D // H
HV = HD + 1
VP = 3 * HV
CH = 512
NS = CH // P
FF = 2048
KF = FF // P
AD = 128
EXPERTS = 16
EPS = 1e-5
BANK = 512
MASKED = -1.0e30
Q_SCALE = 1.0 / math.sqrt(HD)

COLUMNS = {}
_at = 0
for _name, _width in (("b_ada", 2 * D), ("bq", D), ("bk", D), ("bv", D), ("b1", FF), ("g2", D), ("beta2", D),
                      ("down_b", AD), ("b1_sr", 2 * D), ("b2_sr", D), ("b1_nr", D), ("b1_tsr", D)):
    COLUMNS[_name] = (_at, _width // P)
    _at += _width // P
N_COLUMNS = _at

TWO_PI_1 = 6.28125
TWO_PI_2 = round((2 * math.pi - TWO_PI_1) * 2.0 ** 21) / 2.0 ** 21
TWO_PI_3 = 2 * math.pi - TWO_PI_1 - TWO_PI_2
ROUND = 1.5 * 2.0 ** 23
PI_INSIDE = 3.1415925


class Steps:

    def __init__(self, sem):
        self.sem, self.n = sem, 0

    def mark(self, instruction):
        instruction.then_inc(self.sem, 1)
        self.n += 1
        return self.n


def wait(engine, sem, value):
    if not isinstance(value, int) or value > 0:
        engine.wait_ge(sem, value)


def turns(engine, count, body):
    body(0, True, count == 1)
    if count > 2:
        with engine.Fori(1, count - 1) as n:
            body(n, False, False)
    if count > 1:
        body(count - 1, False, True)


def wait_apart(engine, sem, value, gate):
    engine.wait_ge(sem, value)
    engine.sem_inc(gate, 1)


def column(cols, name, k):
    at, _ = COLUMNS[name]
    return cols[:, at + k:at + k + 1]


def make_identity(pool, ident, s_zero, s_ident):
    pool.memset(ident[:, :], 0.0).then_inc(s_zero, 1)
    pool.wait_ge(s_zero, 1)
    pool.affine_select(out=ident[:, :], in_=ident[:, :], compare_op=ALU.not_equal, fill=1.0, base=0,
                       pattern=[[-1, P]], channel_multiplier=1).then_inc(s_ident, 1)


def project_phase(nc, S, B, io, xada_dram, q2_dram, k2_dram, v_dram, mask8_dram):
    NC = S // CH
    RING = 4
    x_tiles = io["x"].rearrange("b (c s p) d -> (b c) p s d", s=NS, p=P)
    xada_tiles = xada_dram.rearrange("(n s p) d -> n p s d", s=NS, p=P)
    q_tiles = q2_dram.rearrange("t (b g p) (c n) -> b g c p t n", b=B, p=P, n=CH)
    k_tiles = k2_dram.rearrange("t (b g p) (c n) -> b g c p t n", b=B, p=P, n=CH)
    v_tiles = v_dram.rearrange("n h p v -> n p h v")
    mask_tiles = io["mask"].rearrange("b one (c s p) k -> (b one c) p s k", s=NS, p=P)
    mask8_tiles = mask8_dram.rearrange("(n s p) k -> n p s k", s=NS, p=P)

    with ExitStack() as ctx:
        sb = lambda name, shape, dt=F32: ctx.enter_context(nc.sbuf_tensor(name, shape, dt))
        sem = lambda name: ctx.enter_context(nc.semaphore(name))

        ident = sb("a_ident", [P, P])
        ones = sb("a_ones", [P, P])
        cols = sb("a_cols", [P, N_COLUMNS])
        freqs = sb("a_freqs", [P, KD])
        step_i = sb("a_step_i", [P, B], I32)
        step_x = sb("a_step_x", [P, 5, B])
        angle = sb("a_angle", [P, 4, KD, B])
        emb = sb("a_emb", [P, 3, KD, B])
        ada = sb("a_ada", [P, 2 * KD, B])
        diag = sb("a_diag", [P, KD, P])
        scale1 = sb("a_scale1", [P, B, D])
        shift = sb("a_shift", [P, B, D])
        w_ada = sb("a_w_ada", [P, KD, 2 * D])
        w_f32 = [sb(f"a_w_f32_{i}", [P, KD, D]) for i in range(3)]
        w_parts = [sb(f"a_w_parts{i}", [P, 2, KD, D], F32R) for i in range(3)]
        bqs = sb("a_bqs", [P, KD])
        x_in = sb("a_x_in", [P, NS, D])
        stats = sb("a_stats", [P, NS, 6])
        moments = sb("a_moments", [P, NS, 2])
        dev = sb("a_dev", [P, NS])
        rstd = sb("a_rstd", [P, NS])
        xada = sb("a_xada", [P, NS, D])
        xT = sb("a_xT", [P, 2, KD, CH], F32R)
        qk_f32 = sb("a_qk_f32", [P, RING, CH])
        parts = sb("a_parts", [P, RING, 2, CH], F32R)
        v_f32 = sb("a_v_f32", [P, H, NS, HD])
        v_out = sb("a_v_out", [P, H, NS, 3, HV], BF16)
        v_rest = v_f32.rearrange("p h s d -> p (h s) d")
        v_part = lambda i: v_out.rearrange("p h s t v -> p (h s) t v")[:, :, i, 0:HD]
        mask_in = sb("a_mask_in", [P, NS, S], U8)
        mask8 = sb("a_mask8", [P, NS, S], F8)
        xT_bank = [ctx.enter_context(nc.psum_tensor(f"a_xT_bank{i}", [P, BANK], F32)) for i in range(2)]
        pr_bank = [ctx.enter_context(nc.psum_tensor(f"a_pr_bank{i}", [P, BANK], F32)) for i in range(6)]

        params_in, weights_in, x_loaded = sem("a_params_in"), sem("a_weights_in"), sem("a_x_loaded")
        ada_in = sem("a_ada_in")
        zeroed, ident_ready, ones_ready = sem("a_zeroed"), sem("a_ident_ready"), sem("a_ones_ready")
        prep, sin_done, sig_done = sem("a_prep"), sem("a_sin_done"), sem("a_sig_done")
        ada_done, row_done, diag_ready, row_copied = (sem("a_ada_done"), sem("a_row_done"), sem("a_diag_ready"),
                                                      sem("a_row_copied"))
        normed, dev_done = sem("a_normed"), sem("a_dev_done")
        w_top_ready, w_low_ready = sem("a_w_top_ready"), sem("a_w_low_ready")
        transposed, xT_top_ready, xT_low_ready = sem("a_transposed"), sem("a_xT_top_ready"), sem("a_xT_low_ready")
        projected, evacuated = sem("a_projected"), sem("a_evacuated")
        split = sem("a_split")
        qk_stored = [sem(f"a_qk_stored{r}") for r in range(RING)]
        v_stored, xada_stored = sem("a_v_stored"), sem("a_xada_stored")
        f32_copied, v_copied, v_split = sem("a_f32_copied"), sem("a_v_copied"), sem("a_v_split")
        mask_loaded, mask_turned, mask_stored = sem("a_mask_loaded"), sem("a_mask_turned"), sem("a_mask_stored")

        sp_gate, dve_gate = sem("a_sp_gate"), sem("a_dve_gate")
        N_NORM = 2 * NS + 2 + NS
        N_LN = N_NORM + 2 * NS
        OUTPUTS = NS + 2 * KD
        block = ctx.enter_context(nc.Block())

        @block.sync
        def _(sp):
            sp.dma_start(cols[:, :], io["cols"]).then_inc(params_in, 16)
            sp.dma_start(freqs[:, :], io["freqs"]).then_inc(params_in, 16)
            sp.dma_start(step_i[:, :], io["timestep"].rearrange("(a b) -> a b", a=1).to_broadcast([P, B])
                         ).then_inc(params_in, 16)
            sp.dma_start(x_in[:, :, :], x_tiles[0]).then_inc(x_loaded, 16)
            sp.dma_start(w_ada[:, :, :], io["W_ada"].rearrange("(k p) n -> p k n", p=P)).then_inc(ada_in, 16)
            for w, name in zip(w_f32, ("Wq", "Wk", "Wv")):
                sp.dma_start(w[:, :, :], io[name].rearrange("(k p) n -> p k n", p=P)).then_inc(weights_in, 16)
            sp.dma_start(mask_in[:, :, :], mask_tiles[0]).then_inc(mask_loaded, 16)
            sp.sem_inc(mask_stored, 16)
            for b in range(B):
                with sp.Fori(0, NC) as c:
                    n = c + b * NC
                    wait_apart(sp, normed, n * N_LN + N_LN, sp_gate)
                    sp.dma_start(xada_tiles[n], xada[:, :, :]).then_inc(xada_stored, 16)
                    wait_apart(sp, mask_turned, n + 1, sp_gate)
                    sp.dma_start(mask8_tiles[n], mask8[:, :, :].bitcast(BF16)).then_inc(mask_stored, 16)
                    for j in range(2 * KD):
                        wait_apart(sp, split, n * (2 * KD) + j + 1, sp_gate)
                        dst = q_tiles if j < KD else k_tiles
                        sp.dma_start(dst[b, j % KD, c], parts[:, j % RING, :, :].bitcast(F32)
                                     ).then_inc(qk_stored[j % RING], 16)
            sp.wait_ge(xada_stored, 16 * B * NC)
            for r in range(RING):
                sp.wait_ge(qk_stored[r], 16 * (2 * KD // RING) * B * NC)
            sp.wait_ge(v_stored, 16 * B * NC)
            sp.wait_ge(mask_stored, 16 * B * NC + 16)

        @block.gpsimd
        def _(pool):
            make_identity(pool, ident, zeroed, ident_ready)
            pool.memset(ones[:, :], 1.0).then_inc(ones_ready, 1)
            pool.memset(v_out[:, :, :, 0, HD:HV], 1.0).then_inc(ones_ready, 1)
            pool.memset(v_out[:, :, :, 1:3, HD:HV], 0.0).then_inc(ones_ready, 1)
            for i in range(3):
                pool.wait_ge(w_top_ready, i + 1)
                pool.tensor_tensor(w_parts[i][:, 1, :, :], w_f32[i][:, :, :], w_parts[i][:, 0, :, :], ALU.subtract
                                   ).then_inc(w_low_ready, 1)
            for b in range(B):
                with pool.Fori(0, NC) as c:
                    n = c + b * NC
                    for j in range(2 * KD):
                        r = j % RING
                        pool.wait_ge(f32_copied, n * (2 * KD) + j + 1)
                        pool.wait_ge(evacuated, n * OUTPUTS + NS + j + 1)
                        pool.tensor_tensor(parts[:, r, 1, :], qk_f32[:, r, :], parts[:, r, 0, :],
                                           ALU.subtract).then_inc(split, 1)

        @block.vector
        def _(dve):
            st = Steps(prep)
            done = lambda: dve.wait_ge(prep, st.n)
            dve.wait_ge(params_in, 16 * 3)
            for g in range(KD):
                k = st.mark(dve.tensor_scalar(bqs[:, g:g + 1], column(cols, "bq", g), Q_SCALE, None, ALU.mult))
            st.mark(dve.tensor_copy(step_x[:, 0, :], step_i[:, :]))
            done()
            t, q, top, low, left = (step_x[:, i, :] for i in range(5))
            st.mark(dve.tensor_scalar(q, t, 0.01, None, ALU.mult))
            done()
            st.mark(dve.tensor_scalar(top, q, ROUND / 4096, ROUND / 4096, ALU.add, ALU.subtract))
            done()
            st.mark(dve.tensor_tensor(low, q, top, ALU.subtract))
            st.mark(dve.scalar_tensor_tensor(out=left, in0=top, scalar=-100.0, in1=t, op0=ALU.mult, op1=ALU.add))
            done()
            st.mark(dve.scalar_tensor_tensor(out=left, in0=low, scalar=-100.0, in1=left, op0=ALU.mult, op1=ALU.add))
            done()
            st.mark(dve.scalar_tensor_tensor(out=q, in0=left, scalar=0.01, in1=q, op0=ALU.mult, op1=ALU.add))
            done()
            st.mark(dve.tensor_scalar(top, q, 4000.0, None, ALU.mult))
            done()
            for b in range(B):
                st.mark(dve.tensor_scalar(angle[:, 0, :, b], freqs[:, :], step_x[:, 2, b:b + 1], None, ALU.mult))
            done()
            st.mark(dve.tensor_scalar(angle[:, 1, :, :], angle[:, 0, :, :], 1.0 / (2 * math.pi), ROUND,
                                      ALU.mult, ALU.add))
            done()
            st.mark(dve.tensor_scalar(angle[:, 2, :, :], angle[:, 1, :, :], ROUND, None, ALU.subtract))
            for part in (TWO_PI_1, TWO_PI_2, TWO_PI_3):
                done()
                st.mark(dve.scalar_tensor_tensor(out=angle[:, 0, :, :], in0=angle[:, 2, :, :], scalar=-part,
                                                 in1=angle[:, 0, :, :], op0=ALU.mult, op1=ALU.add))
            done()
            half = KD // 2
            st.mark(dve.tensor_scalar(angle[:, 0, half:, :], angle[:, 0, half:, :], math.pi / 2, None, ALU.add))
            done()
            st.mark(dve.tensor_scalar(angle[:, 1, half:, :], angle[:, 0, half:, :], math.pi, -2 * math.pi,
                                      ALU.is_gt, ALU.mult))
            done()
            st.mark(dve.tensor_tensor(angle[:, 0, half:, :], angle[:, 0, half:, :], angle[:, 1, half:, :], ALU.add))
            done()
            angle_ready = st.mark(dve.tensor_scalar(angle[:, 3, :, :], angle[:, 0, :, :], -PI_INSIDE, PI_INSIDE,
                                                    ALU.max, ALU.min))
            assert angle_ready == N_ANGLE
            dve.wait_ge(sig_done, 1)
            st.mark(dve.tensor_tensor(emb[:, 2, :, :], emb[:, 0, :, :], emb[:, 1, :, :], ALU.mult))
            assert st.n == N_SILU
            def normalise(n):
                ln = Steps(normed)
                upto = lambda k: dve.wait_ge(normed, n * N_LN + k)
                dve.wait_ge(x_loaded, n * 16 + 16)
                for s in range(NS):
                    k = ln.mark(dve.bn_stats(stats[:, s, :], x_in[:, s, :]))
                wait_apart(dve, normed, n * N_LN + k, dve_gate)
                for s in range(NS):
                    k = ln.mark(dve.bn_aggr(moments[:, s, :], stats[:, s, :]))
                upto(k)
                k = ln.mark(dve.tensor_scalar(rstd[:, :], moments[:, :, 1], EPS, None, ALU.add))
                assert k == N_VAR
                dve.wait_ge(dev_done, n + 1)
                k = ln.mark(dve.reciprocal(rstd[:, :], dev[:, :]))
                upto(k)
                wait(dve, transposed, n * KD)
                wait(dve, xada_stored, n * 16)
                for s in range(NS):
                    k = ln.mark(dve.tensor_scalar(xada[:, s, :], x_in[:, s, :], moments[:, s, 0:1],
                                                  rstd[:, s:s + 1], ALU.subtract, ALU.mult))
                assert ln.n == N_NORM

            def scale_shift(n, b):
                ln = Steps(normed)
                ln.n = N_NORM
                upto = lambda k: dve.wait_ge(normed, n * N_LN + k)
                upto(N_NORM)
                for s in range(NS):
                    k = ln.mark(dve.tensor_tensor(xada[:, s, :], xada[:, s, :], scale1[:, b, :], ALU.mult))
                upto(k)
                for s in range(NS):
                    k = ln.mark(dve.tensor_tensor(xada[:, s, :], xada[:, s, :], shift[:, b, :], ALU.add))
                assert ln.n == N_LN

            normalise(0)
            dve.wait_ge(ada_done, 1)
            for j in range(2 * KD):
                st.mark(dve.tensor_scalar(ada[:, j, :], pr_bank[0][:, j * B:(j + 1) * B], column(cols, "b_ada", j),
                                          1.0 if j < KD else 0.0, ALU.add, ALU.add))
            done()
            dve.wait_ge(ident_ready, 1)
            for i, (b, half_at) in enumerate((b, h) for b in range(B) for h in (0, KD)):
                if i:
                    dve.wait_ge(row_done, i)
                for g in range(KD):
                    last = dve.tensor_scalar(diag[:, g, :], ident[:, :], ada[:, half_at + g, b:b + 1], None, ALU.mult)
                last.then_inc(diag_ready, 1)
                dve.wait_ge(row_done, i + 1)
                dst = scale1 if half_at == 0 else shift
                dve.tensor_copy(dst[:, b, :], pr_bank[1][:, :]).then_inc(row_copied, 1)
            dve.wait_ge(row_copied, 2 * B)
            def lower_rows(n):
                for k in range(KD):
                    dve.wait_ge(xT_top_ready, n * KD + k + 1)
                    dve.tensor_tensor(xT[:, 1, k, :], xT_bank[k % 2][:, :], xT[:, 0, k, :], ALU.subtract
                                      ).then_inc(xT_low_ready, 1)

            def turn_mask(n):
                wait_apart(dve, mask_loaded, n * 16 + 16, dve_gate)
                wait_apart(dve, mask_stored, n * 16 + 16, dve_gate)
                dve.tensor_copy(mask8[:, :, :], mask_in[:, :, :], saturate=False).then_inc(mask_turned, 1)

            def split_values(n):
                dve.wait_ge(v_copied, (n + 1) * NS)
                dve.wait_ge(evacuated, n * OUTPUTS + NS)
                dve.tensor_tensor(v_rest, v_rest, v_part(0), ALU.subtract).then_inc(v_split, 1)
                dve.wait_ge(v_split, n * 3 + 1)
                dve.tensor_copy(v_part(1), v_rest).then_inc(v_split, 1)
                dve.wait_ge(v_split, n * 3 + 2)
                dve.tensor_tensor(v_part(2), v_rest, v_part(1), ALU.subtract).then_inc(v_split, 1)

            scale_shift(0, 0)
            for b in range(B):
                if NC > 1 or b:
                    with dve.Fori(b * NC or 1, (b + 1) * NC) as n:
                        lower_rows(n - 1)
                        turn_mask(n - 1)
                        split_values(n - 1)
                        normalise(n)
                        scale_shift(n, b)
            lower_rows(B * NC - 1)
            turn_mask(B * NC - 1)
            split_values(B * NC - 1)

        @block.scalar
        def _(act):
            act.wait_ge(prep, N_ANGLE)
            act.activation(emb[:, 0, :, :], angle[:, 3, :, :], ACT.Sin).then_inc(sin_done, 1)
            act.wait_ge(sin_done, 1)
            act.activation(emb[:, 1, :, :], emb[:, 0, :, :], ACT.Sigmoid).then_inc(sig_done, 1)
            def deviations(n):
                act.wait_ge(normed, n * N_LN + N_VAR)
                act.activation(dev[:, :], rstd[:, :], ACT.Sqrt).then_inc(dev_done, 1)

            deviations(0)
            act.wait_ge(weights_in, 16 * 3)
            for i in range(3):
                act.activation(w_parts[i][:, 0, :, :], w_f32[i][:, :, :], ACT.Copy).then_inc(w_top_ready, 1)
            act.wait_ge(ones_ready, 3)

            def store_values(n):
                act.wait_ge(v_split, (n + 1) * 3)
                act.dma_start(v_tiles[n], v_out.rearrange("p h s t v -> p h (s t v)")).then_inc(v_stored, 16)

            def chunk(n, first, last):
                for k in range(KD):
                    act.wait_ge(transposed, n * KD + k + 1)
                    act.activation(xT[:, 0, k, :], xT_bank[k % 2][:, :], ACT.Copy).then_inc(xT_top_ready, 1)
                if not last:
                    act.wait_ge(normed, n * N_LN + N_LN)
                    act.dma_start(x_in[:, :, :], x_tiles[n + 1]).then_inc(x_loaded, 16)
                wait(act, v_stored, n * 16)
                for s in range(NS):
                    values = pr_bank[s % 6][:, :].rearrange("p (h d) -> p h d", h=H)
                    act.wait_ge(projected, n * OUTPUTS + s + 1)
                    act.activation(v_f32[:, :, s, :], values, ACT.Copy).then_inc(v_copied, 1)
                    act.activation(v_out[:, :, s, 0, 0:HD], values, ACT.Copy).then_inc(evacuated, 1)
                for j in range(2 * KD):
                    r, g = j % RING, j % KD
                    product = pr_bank[(NS + j) % 6][:, :]
                    scale, bias = (Q_SCALE, bqs[:, g:g + 1]) if j < KD else (1.0, column(cols, "bk", g))
                    act.wait_ge(projected, n * OUTPUTS + NS + j + 1)
                    behind = max(0, j + 1 - RING)
                    wait(act, split, n * (2 * KD) + behind)
                    act.activation(qk_f32[:, r, :], product, ACT.Identity, bias=bias, scale=scale
                                   ).then_inc(f32_copied, 1)
                    wait(act, qk_stored[r], (n * (2 * KD // RING) + j // RING) * 16)
                    act.activation(parts[:, r, 0, :], product, ACT.Identity, bias=bias, scale=scale
                                   ).then_inc(evacuated, 1)
                    if j == 1 and not last:
                        deviations(n + 1)
                    if j == 2 * KD - 2:
                        store_values(n)
                        if not last:
                            act.wait_ge(mask_turned, n + 1)
                            act.dma_start(mask_in[:, :, :], mask_tiles[n + 1]).then_inc(mask_loaded, 16)

            turns(act, B * NC, chunk)

        @block.tensor
        def _(pe):
            pe.wait_ge(ada_in, 16)
            pe.wait_ge(prep, N_SILU)
            for j in range(2 * KD):
                for k in range(KD):
                    last = pe.matmul(pr_bank[0][:, j * B:(j + 1) * B], w_ada[:, k, j * P:(j + 1) * P],
                                     emb[:, 2, k, :], start=(k == 0), stop=(k == KD - 1))
            last.then_inc(ada_done, 1)
            pe.wait_ge(ones_ready, 1)
            for i in range(2 * B):
                pe.wait_ge(diag_ready, i + 1)
                if i:
                    pe.wait_ge(row_copied, i)
                for g in range(KD):
                    last = pe.matmul(pr_bank[1][:, g * P:(g + 1) * P], ones[:, :], diag[:, g, :],
                                     start=True, stop=True)
                last.then_inc(row_done, 1)
            pe.wait_ge(row_copied, 2 * B)
            pe.wait_ge(w_low_ready, 3)
            def chunk(n, first, last):
                pe.wait_ge(normed, n * N_LN + N_LN)
                for k in range(KD):
                    if k >= 2:
                        pe.wait_ge(xT_low_ready, n * KD + k - 1)
                    for s in range(NS):
                        last = pe.transpose(xT_bank[k % 2][:, s * P:(s + 1) * P], xada[:, s, k * P:(k + 1) * P],
                                            ident[:, :])
                    last.then_inc(transposed, 1)
                wait(pe, evacuated, n * OUTPUTS)
                pe.wait_ge(xT_top_ready, n * KD + KD)
                for o in range(OUTPUTS):
                    bank = pr_bank[o % 6]
                    if o >= 6:
                        pe.wait_ge(evacuated, n * OUTPUTS + o - 5)
                    passes = [(w, 0, k) for k in range(KD) for w in (0, 1)] + [(0, 1, k) for k in range(KD)]
                    for i, (wp, xp, k) in enumerate(passes):
                        if o == 0 and xp == 1:
                            pe.wait_ge(xT_low_ready, n * KD + k + 1)
                        if o < NS:
                            lhsT, rhs = xT[:, xp, k, o * P:(o + 1) * P], w_parts[2][:, wp, k, :]
                        else:
                            which, g = divmod(o - NS, KD)
                            lhsT, rhs = w_parts[which][:, wp, k, g * P:(g + 1) * P], xT[:, xp, k, :]
                        last = pe.matmul(bank[:, :], lhsT, rhs, start=(i == 0), stop=(i == len(passes) - 1))
                    last.then_inc(projected, 1)

            turns(pe, B * NC, chunk)


N_ANGLE = KD + 8 + 2 + 2 + 3 + 4
N_SILU = N_ANGLE + 1
N_VAR = 2 * NS + 1


U = 4
Q_PARTS = (0, 0, 1, 1)
K_PARTS = (0, 1, 0, 1)
HEAD_DMAS = 2 * len(Q_PARTS) + 1


def attention_phase(nc, S, B, io, q2_dram, k2_dram, v_dram, mask8_dram, ctx_dram):
    assert B == 2
    NQ = S // P
    NCK = S // BANK
    NG = NQ // U
    TILES = B * H * NQ
    GROUPS = TILES // U
    bias_tiles = io["fside"].rearrange("b h (q p) k -> (b h q) p k", p=P)
    mask_rows = mask8_dram.rearrange("(b q p) k -> b p q k", b=B, p=P)
    q_rows = q2_dram.rearrange("t (n r) k -> n t r k", r=HD)
    k_rows = k2_dram.rearrange("t (n r) k -> n t r k", r=HD)
    v_rows = v_dram.rearrange("(b c) h p v -> b h p c v", b=B)

    with ExitStack() as ctx:
        sb = lambda name, shape, dt=F32: ctx.enter_context(nc.sbuf_tensor(name, shape, dt))
        sem = lambda name: ctx.enter_context(nc.semaphore(name))
        bank = lambda name: ctx.enter_context(nc.psum_tensor(name, [P, BANK], F32))

        ident = sb("b_ident", [P, P])
        mask_diag = sb("b_mask_diag", [P, P], BF16)
        mask = [sb(f"b_mask{b}", [P, NQ, S], F8) for b in range(B)]
        qst = [sb(f"b_qst{i}", [P, S], F32R) for i in range(2)]
        kst = [sb(f"b_kst{i}", [P, S], F32R) for i in range(2)]
        vh = [sb(f"b_vh{i}", [P, NQ, VP], BF16) for i in range(2)]
        bias = [sb(f"b_bias{i}", [P, S]) for i in range(U)]
        scores = [sb(f"b_scores{i}", [P, S]) for i in range(2)]
        chunk_max = [sb(f"b_chunk_max{i}", [P, NCK]) for i in range(2)]
        row_max = [sb(f"b_row_max{i}", [P, 1]) for i in range(2)]
        probs = sb("b_probs", [P, 2, BANK])
        top = [sb(f"b_top{i}", [P, NCK, BANK], F16) for i in range(2)]
        low = [sb(f"b_low{i}", [P, NCK, BANK], BF16) for i in range(2)]
        total = sb("b_total", [P, 2, HV])
        denom = sb("b_denom", [P, 2])
        ctx_out = [sb(f"b_ctx_out{i}", [P, HD]) for i in range(U)]
        s_bank = [bank(f"b_s_bank{i}") for i in range(NCK)]
        t_bank = [bank(f"b_t_bank{i}") for i in range(2)]
        o_bank = [bank(f"b_o_bank{i}") for i in range(2)]

        zeroed, ident_ready, blank_ready = sem("b_zeroed"), sem("b_ident_ready"), sem("b_blank_ready")
        first_mask, group_mask, mask_loaded = sem("b_first_mask"), sem("b_group_mask"), sem("b_mask_loaded")
        head_loaded = [sem(f"b_head_loaded{i}") for i in range(2)]
        bias_loaded = [sem(f"b_bias_loaded{i}") for i in range(U)]
        ctx_stored = [sem(f"b_ctx_stored{i}") for i in range(U)]
        qk_done, scored = sem("b_qk_done"), sem("b_scored")
        max_done, shifted, transposed = sem("b_max_done"), sem("b_shifted"), sem("b_transposed")
        exp_done, top_done, low_done = sem("b_exp_done"), sem("b_top_done"), sem("b_low_done")
        pv_done, summed, inverted, ctx_ready = sem("b_pv_done"), sem("b_summed"), sem("b_inverted"), sem("b_ctx_ready")
        sp_gate, dve_gate = sem("b_sp_gate"), sem("b_dve_gate")

        def load_head(queue, h, b):
            row = b * H + h
            for r in range(len(Q_PARTS)):
                rows = slice(HD * r, HD * (r + 1))
                queue.dma_start(qst[b][rows, :].bitcast(F32), q_rows[row, Q_PARTS[r]]).then_inc(head_loaded[b], 16)
                queue.dma_start(kst[b][rows, :].bitcast(F32), k_rows[row, K_PARTS[r]]).then_inc(head_loaded[b], 16)
            queue.dma_start(vh[b].rearrange("p (c s) v -> p c (s v)", s=NS), v_rows[b, h]).then_inc(head_loaded[b], 16)

        block = ctx.enter_context(nc.Block())

        @block.sync
        def _(sp):
            for w in range(U):
                sp.sem_inc(ctx_stored[w], 16)
            load_head(sp, 0, 0)
            sp.dma_start(mask[0][:, 0:1, :].bitcast(BF16), mask_rows[0][:, 0:1, :]).then_inc(first_mask, 16)
            for u in range(U):
                sp.dma_start(bias[u][:, :], bias_tiles[u]).then_inc(bias_loaded[u], 16)
            sp.dma_start(mask[0][:, 1:U, :].bitcast(BF16), mask_rows[0][:, 1:U, :]).then_inc(group_mask, 16)
            sp.dma_start(mask[0][:, U:, :].bitcast(BF16), mask_rows[0][:, U:, :]).then_inc(mask_loaded, 16)
            sp.dma_start(mask[1][:, :, :].bitcast(BF16), mask_rows[1]).then_inc(mask_loaded, 16)

            def store(t, w):
                wait_apart(sp, ctx_ready, t + 1, sp_gate)
                sp.dma_start(ctx_dram[t], ctx_out[w][:, :]).then_inc(ctx_stored[w], 16)

            def group(hd, g, rows_next, first=False):
                t0 = (hd * NG + g) * U
                for u in range(U):
                    if rows_next is not None:
                        wait_apart(sp, scored, (t0 + u + 1) * NCK, sp_gate)
                        sp.dma_start(bias[u][:, :], bias_tiles[rows_next + u]).then_inc(bias_loaded[u], 16)
                    if not first or u == U - 1:
                        store(t0 + u - 3, (u + 1) % U)

            def head(h, b, first, last):
                hd = h * B + b
                row = (b * H + h) * NQ
                h_next, b_next = (h, 1) if b == 0 else (h + 1, 0)
                row_next = None if last else (b_next * H + h_next) * NQ
                group(hd, 0, row + U if NG > 1 else row_next, first)
                if not last:
                    wait_apart(sp, qk_done, hd * (NQ * NCK) + 1, sp_gate)
                    wait_apart(sp, pv_done, hd * NQ + 1, sp_gate)
                    load_head(sp, h_next, b_next)
                if NG > 2:
                    with sp.Fori(1, NG - 1) as g:
                        group(hd, g, row + U + g * U)
                if NG > 1:
                    group(hd, NG - 1, row_next)

            head(0, 0, True, False)
            head(0, 1, False, False)
            with sp.Fori(1, H - 1) as h:
                for b in range(B):
                    head(h, b, False, False)
            head(H - 1, 0, False, False)
            head(H - 1, 1, False, True)
            for t in range(TILES - 3, TILES):
                store(t, t % U)
            for w in range(U):
                sp.wait_ge(ctx_stored[w], GROUPS * 16 + 16)

        @block.gpsimd
        def _(pool):
            make_identity(pool, ident, zeroed, ident_ready)
            pool.memset(mask_diag[:, :], 0.0).then_inc(zeroed, 1)
            pool.wait_ge(zeroed, 2)
            pool.affine_select(out=mask_diag[:, :], in_=mask_diag[:, :], compare_op=ALU.not_equal, fill=MASKED,
                               base=0, pattern=[[-1, P]], channel_multiplier=1).then_inc(ident_ready, 1)
            pool.memset(top[1][:, :, :], 0.0).then_inc(blank_ready, 1)
            pool.memset(low[1][:, :, :], 0.0).then_inc(blank_ready, 1)
            pool.memset(vh[1][:, :, :], 0.0).then_inc(blank_ready, 1)

            def tile(g, u):
                t, par = g * U + u, u % 2
                for c in range(NCK):
                    x = t * NCK + c
                    if c == 0:
                        wait(pool, pv_done, t)
                    pool.wait_ge(exp_done, x + 1)
                    pool.wait_ge(top_done, x + 1 + NCK)
                    pool.tensor_tensor(low[par][:, c, :], probs[:, c % 2, :], top[par][:, c, :], ALU.subtract
                                       ).then_inc(low_done, 1)

            pool.sem_inc(low_done, NCK)
            for u in range(U):
                tile(0, u)
            with pool.Fori(1, GROUPS) as g:
                for u in range(U):
                    tile(g, u)

        @block.vector
        def _(dve):
            dve.sem_inc(summed, 3)

            def sum_parts(t, par, w, in_group):
                dve.wait_ge(pv_done, t + 2)
                dve.tensor_reduce(total[:, par, :], o_bank[par][:, 0:VP].rearrange("p (t v) -> p v t", t=3),
                                  AX.X, ALU.add).then_inc(summed, 1)

            def invert(t, par, w, in_group):
                dve.wait_ge(summed, t + 4)
                dve.reciprocal(denom[:, par:par + 1], total[:, par, HD:HV]).then_inc(inverted, 1)

            def normalise(t, par, w, in_group):
                dve.wait_ge(ctx_stored[w], in_group * 16 + 16)
                dve.wait_ge(inverted, t + 1)
                dve.tensor_scalar(ctx_out[w][:, :], total[:, par, 0:HD], denom[:, par:par + 1], None,
                                  ALU.mult).then_inc(ctx_ready, 1)

            def tile(g, u, first):
                t = g * U + u
                par = u % 2
                before = None
                if u == U - 1:
                    before = (t - 3, 0, 0, g)
                elif not first:
                    before = (t - 3, (u + 1) % 2, u + 1, g - 1)
                if not (first and u < 2):
                    dve.wait_ge(transposed, (t - 1) * NCK)
                dve.wait_ge(bias_loaded[u], g * 16 + 16)
                if before is not None:
                    sum_parts(*before)
                for c in range(NCK):
                    cols = slice(c * BANK, (c + 1) * BANK)
                    wait_apart(dve, qk_done, t * NCK + c + 1, dve_gate)
                    dve.tensor_tensor_reduce(scores[par][:, cols], s_bank[c][:, :], bias[u][:, cols], 1.0, -3.0e38,
                                             ALU.add, ALU.max, chunk_max[par][:, c:c + 1]).then_inc(scored, 1)
                if before is not None:
                    invert(*before)
                dve.wait_ge(scored, (t + 1) * NCK)
                dve.tensor_reduce(row_max[par][:, :], chunk_max[par][:, :], AX.X, ALU.max).then_inc(max_done, 1)
                if before is not None:
                    normalise(*before)
                dve.wait_ge(max_done, t + 1)
                for c in range(NCK):
                    cols = slice(c * BANK, (c + 1) * BANK)
                    dve.tensor_scalar(scores[par][:, cols], scores[par][:, cols], row_max[par][:, 0:1], None,
                                      ALU.subtract).then_inc(shifted, 1)

            for u in range(U):
                tile(0, u, True)
            with dve.Fori(1, GROUPS) as g:
                for u in range(U):
                    tile(g, u, False)
            for t in range(TILES - 3, TILES):
                for step in (sum_parts, invert, normalise):
                    step(t, t % 2, t % U, t // U)

        @block.scalar
        def _(act):
            act.sem_inc(top_done, NCK)

            def tile(g, u):
                t, par = g * U + u, u % 2
                for c in range(NCK):
                    x = t * NCK + c
                    if c == 0:
                        wait(act, pv_done, t)
                    act.wait_ge(transposed, x + 1)
                    act.wait_ge(low_done, x - 1 + NCK)
                    act.activation(probs[:, c % 2, :], t_bank[c % 2][:, :], ACT.Exp).then_inc(exp_done, 1)
                    act.activation(top[par][:, c, :], t_bank[c % 2][:, :], ACT.Exp).then_inc(top_done, 1)

            for u in range(U):
                tile(0, u)
            with act.Fori(1, GROUPS) as g:
                for u in range(U):
                    tile(g, u)

        @block.tensor
        def _(pe):
            def qk(t, b, q, c):
                pe.matmul(s_bank[c][:, :], qst[b][:, bass.ts(q, P)], kst[b][:, bass.ts(c, BANK)],
                          start=True, stop=False)
                pe.matmul(s_bank[c][:, :], mask_diag[:, :], mask[b][:, q, bass.ts(c, BANK)], start=False, stop=True
                          ).then_inc(qk_done, 1)

            def turn(t, par, c):
                pe.wait_ge(shifted, t * NCK + c + 1)
                pe.wait_ge(top_done, t * NCK + c - 1 + NCK)
                for i in range(BANK // P):
                    last = pe.transpose(t_bank[c % 2][:, i * P:(i + 1) * P],
                                        scores[par][:, c * BANK + i * P:c * BANK + (i + 1) * P], ident[:, :])
                last.then_inc(transposed, 1)

            def pv(t_next, b, par, c):
                if c == 0:
                    pe.wait_ge(summed, t_next + 1)
                pe.wait_ge(top_done, t_next * NCK + c + 1)
                pe.wait_ge(low_done, t_next * NCK + c + 1)
                for i in range(BANK // P):
                    k = c * (BANK // P) + i
                    tops = (top[par][:, c, i * P:(i + 1) * P], VP)
                    lows = (low[par][:, c, i * P:(i + 1) * P], 2 * HV)
                    for j, (lhsT, width) in enumerate((tops, lows) if k == 0 else (lows, tops)):
                        last = pe.matmul(o_bank[par][:, 0:width], lhsT, vh[b][:, k, 0:width],
                                         start=(k == 0 and j == 0), stop=(k == NQ - 1 and j == 1))
                if c == NCK - 1:
                    last.then_inc(pv_done, 1)

            def tile(h, b, g, u, last):
                t = ((h * B + b) * NG + g) * U + u
                crosses = g == NG - 1 and u == U - 1
                b_next, q_next = (1 - b, 0) if crosses else (b, g * U + u + 1)
                b_before = 1 - b if g == 0 and u == 0 else b

                def score(c):
                    if last and crosses:
                        return
                    if crosses and c == 0:
                        pe.wait_ge(head_loaded[b_next], (h + 1 + b) * (16 * HEAD_DMAS))
                    if (b, g, u, c) == (0, 0, 0, 0):
                        pe.wait_ge(group_mask, 16)
                    if u == U - 1 and c == 0:
                        pe.wait_ge(mask_loaded, 32)
                    pe.wait_ge(scored, t * NCK + c + 1)
                    qk(t + 1, b_next, q_next, c)

                scores_left, contexts_left = list(range(NCK)), list(range(NCK))
                for c in range(NCK):
                    turn(t, u % 2, c)
                    for _ in range(2):
                        if scores_left:
                            score(scores_left.pop(0))
                        elif contexts_left:
                            pv(t, b_before, 1 - u % 2, contexts_left.pop(0))
                for c in contexts_left:
                    pv(t, b_before, 1 - u % 2, c)

            def head(h, b, last):
                for g in range(NG):
                    for u in range(U):
                        tile(h, b, g, u, last)

            pe.wait_ge(ident_ready, 2)
            pe.wait_ge(blank_ready, 3)
            pe.wait_ge(head_loaded[0], 16 * HEAD_DMAS)
            pe.wait_ge(first_mask, 16)
            for c in range(NCK):
                qk(0, 0, 0, c)
            with pe.Fori(0, H - 1) as h:
                for b in range(B):
                    head(h, b, False)
            head(H - 1, 0, False)
            head(H - 1, 1, True)
            for c in range(NCK):
                pv(TILES, 1, (TILES - 1) % 2, c)


def batch_turns(engine, B, NC, body):
    for b in range(B):
        first, last = b * NC, (b + 1) * NC - 1
        if b == 0 and NC > 1:
            body(0, 0, 0)
            first = 1
        if last > first:
            with engine.Fori(first, last) as n:
                body(n, b, b)
        body(last, b, b + 1 if b + 1 < B else None)


class Norm:

    N_VAR = 2 * NS + 1
    SIZE = N_VAR + 1 + NS

    def __init__(self, sb, sem, name):
        self.stats = sb(name + "_stats", [P, NS, 6])
        self.moments = sb(name + "_moments", [P, NS, 2])
        self.var = sb(name + "_var", [P, NS])
        self.dev = sb(name + "_dev", [P, NS])
        self.rstd = sb(name + "_rstd", [P, NS])
        self.done, self.dev_done, self.gate = sem(name + "_done"), sem(name + "_dev_done"), sem(name + "_gate")

    def statistics(self, dve, s, row):
        dve.bn_stats(self.stats[:, s, :], row).then_inc(self.done, 1)

    def rows(self, dve, n, out, x):
        base = n * self.SIZE
        wait_apart(dve, self.done, base + NS, self.gate)
        for s in range(NS):
            dve.bn_aggr(self.moments[:, s, :], self.stats[:, s, :]).then_inc(self.done, 1)
        dve.wait_ge(self.done, base + 2 * NS)
        dve.tensor_scalar(self.var[:, :], self.moments[:, :, 1], EPS, None, ALU.add).then_inc(self.done, 1)
        dve.wait_ge(self.dev_done, n + 1)
        dve.reciprocal(self.rstd[:, :], self.dev[:, :]).then_inc(self.done, 1)
        dve.wait_ge(self.done, base + self.N_VAR + 1)
        for s in range(NS):
            dve.tensor_scalar(out[:, s, :], x[:, s, :], self.moments[:, s, 0:1], self.rstd[:, s:s + 1],
                              ALU.subtract, ALU.mult).then_inc(self.done, 1)

    def deviations(self, act, n):
        act.wait_ge(self.done, n * self.SIZE + self.N_VAR)
        act.activation(self.dev[:, :], self.var[:, :], ACT.Sqrt).then_inc(self.dev_done, 1)


def feed_forward_phase(nc, S, B, io, xada_dram, ctx_dram, x2_dram):
    NC = S // CH
    N = B * NC
    ctx_tiles = ctx_dram.rearrange("(h b c s) p d -> b c s p h d", b=B, h=H, s=NS)
    xada_tiles = xada_dram.rearrange("(n s p) d -> n p s d", s=NS, p=P)
    x2_tiles = x2_dram.rearrange("(n s p) d -> n p s d", s=NS, p=P)

    with ExitStack() as ctx:
        sb = lambda name, shape, dt=F32: ctx.enter_context(nc.sbuf_tensor(name, shape, dt))
        sem = lambda name: ctx.enter_context(nc.semaphore(name))

        ident = sb("c_ident", [P, P])
        cols = sb("c_cols", [P, N_COLUMNS])
        b1_sig = sb("c_b1_sig", [P, KF])
        bo_row = sb("c_bo_row", [P, D])
        b2_row = sb("c_b2_row", [P, D])
        wo = sb("c_wo", [P, KD, D])
        w1 = sb("c_w1", [P, 2, KD, FF], F32R)
        w2 = sb("c_w2", [P, KF, D])
        ctx_in = sb("c_ctx_in", [P, NS, D])
        xada = sb("c_xada", [P, NS, D])
        x1 = sb("c_x1", [P, NS, D])
        x1b = sb("c_x1b", [P, NS, D])
        x2 = x1b
        h = sb("c_h", [P, NS, D])
        ctxT = h
        hT = sb("c_hT", [P, 2, KD, CH], F32R)
        sig = sb("c_sig", [P, 2, CH])
        ff = sb("c_ff", [P, KF, CH])
        t_bank = [ctx.enter_context(nc.psum_tensor(f"c_t_bank{i}", [P, BANK], F32)) for i in range(2)]
        y_bank = [ctx.enter_context(nc.psum_tensor(f"c_y_bank{i}", [P, BANK], F32)) for i in range(NS)]
        f_bank = [ctx.enter_context(nc.psum_tensor(f"c_f_bank{i}", [P, BANK], F32)) for i in range(2)]
        norm = Norm(sb, sem, "c_norm")
        w1_rows = [ff[:, k * (KF // KD):(k + 1) * (KF // KD), :].rearrange("p f n -> p (f n)") for k in range(KD)]

        params_in, wo_in, w2_in = sem("c_params_in"), sem("c_wo_in"), sem("c_w2_in")
        w1_in = [sem(f"c_w1_in{k}") for k in range(KD)]
        w1_top_ready, w1_low_ready = sem("c_w1_top_ready"), sem("c_w1_low_ready")
        zeroed, ident_ready, b1_ready = sem("c_zeroed"), sem("c_ident_ready"), sem("c_b1_ready")
        ctx_loaded, xada_loaded, x2_stored = sem("c_ctx_loaded"), sem("c_xada_loaded"), sem("c_x2_stored")
        ctx_turned, ctxT_ready = sem("c_ctx_turned"), sem("c_ctxT_ready")
        bo_added, wo_done, x1_ready, x1b_ready = (sem("c_bo_added"), sem("c_wo_done"), sem("c_x1_ready"),
                                                  sem("c_x1b_ready"))
        h_turned, h_copied, hT_top_ready, hT_ready = (sem("c_h_turned"), sem("c_h_copied"), sem("c_hT_top_ready"),
                                                      sem("c_hT_ready"))
        w1_done, sig_ready, ff_ready = sem("c_w1_done"), sem("c_sig_ready"), sem("c_ff_ready")
        w2_done, x2_ready = sem("c_w2_done"), sem("c_x2_ready")
        sp_gate = sem("c_sp_gate")

        block = ctx.enter_context(nc.Block())

        @block.sync
        def _(sp):
            def load_ctx(b, c):
                for s in range(NS):
                    sp.dma_start(ctx_in[:, s, :].rearrange("p (h d) -> p h d", h=H), ctx_tiles[b, c, s]
                                 ).then_inc(ctx_loaded, 16)

            def load_xada(n):
                sp.dma_start(xada[:, :, :], xada_tiles[n]).then_inc(xada_loaded, 16)

            def store_x2(n):
                wait_apart(sp, x2_ready, n * NS + NS, sp_gate)
                sp.dma_start(x2_tiles[n], x2[:, :, :]).then_inc(x2_stored, 16)

            sp.sem_inc(x2_stored, 16)
            sp.dma_start(cols[:, :], io["cols"]).then_inc(params_in, 16)
            load_ctx(0, 0)
            sp.dma_start(wo[:, :, :], io["Wo"].rearrange("(k p) n -> p k n", p=P)).then_inc(wo_in, 16)
            load_xada(0)
            for row, name in ((bo_row, "bo"), (b2_row, "b2")):
                sp.dma_start(row[:, :], io[name].rearrange("(a n) -> a n", a=1).to_broadcast([P, D])
                             ).then_inc(params_in, 16)
            for k in range(KD):
                sp.dma_start(w1_rows[k], io["W1"].rearrange("(k p) n -> p k n", p=P)[:, k, :]).then_inc(w1_in[k], 16)
            sp.dma_start(w2[:, :, :], io["W2"].rearrange("(k p) n -> p k n", p=P)).then_inc(w2_in, 16)

            def ahead(n, b_next, c_next):
                wait_apart(sp, ctx_turned, n * KD + KD, sp_gate)
                load_ctx(b_next, c_next)
                wait_apart(sp, x1_ready, n * NS + NS, sp_gate)
                load_xada(n + 1)

            ahead(0, 0, 1) if NC > 1 else ahead(0, 1, 0) if B > 1 else None
            for b in range(B):
                first = 0 if b else 1
                if NC - 1 > first:
                    with sp.Fori(first, NC - 1) as c:
                        n = c + b * NC
                        ahead(n, b, c + 1)
                        store_x2(n - 1)
                if (b or NC > 1) and b + 1 < B:
                    ahead((b + 1) * NC - 1, b + 1, 0)
                    store_x2((b + 1) * NC - 2)
            if N > 1:
                store_x2(N - 2)
            store_x2(N - 1)
            sp.wait_ge(x2_stored, N * 16 + 16)

        @block.gpsimd
        def _(pool):
            make_identity(pool, ident, zeroed, ident_ready)
            pool.wait_ge(params_in, 16 * 3)

            def turn(n, first, last):
                pool.wait_ge(xada_loaded, n * 16 + 16)
                for s in range(NS):
                    pool.tensor_tensor(xada[:, s, :], xada[:, s, :], bo_row[:, :], ALU.add).then_inc(bo_added, 1)
                pool.wait_ge(x1_ready, n * NS + NS)
                pool.wait_ge(x2_stored, n * 16 + 16)
                for s in range(NS):
                    pool.tensor_tensor(x1b[:, s, :], x1[:, s, :], b2_row[:, :], ALU.add).then_inc(x1b_ready, 1)

            turns(pool, N, turn)

        @block.vector
        def _(dve):
            dve.wait_ge(params_in, 16 * 3)
            at, k = COLUMNS["b1"]
            dve.tensor_scalar(b1_sig[:, :], cols[:, at:at + k], 1.702, None, ALU.mult).then_inc(b1_ready, 1)

            def second_residual(n):
                for s in range(NS):
                    dve.wait_ge(w2_done, n * NS + s + 1)
                    dve.wait_ge(x1b_ready, n * NS + s + 1)
                    dve.tensor_tensor(x2[:, s, :], y_bank[s][:, :], x1b[:, s, :], ALU.add).then_inc(x2_ready, 1)

            def turn(n, first, last):
                if not first:
                    dve.wait_ge(x1b_ready, n * NS)
                for s in range(NS):
                    dve.wait_ge(wo_done, n * NS + s + 1)
                    dve.wait_ge(bo_added, n * NS + s + 1)
                    dve.tensor_tensor(x1[:, s, :], y_bank[s][:, :], xada[:, s, :], ALU.add).then_inc(x1_ready, 1)
                    dve.wait_ge(x1_ready, n * NS + s + 1)
                    norm.statistics(dve, s, x1[:, s, :])
                wait(dve, h_turned, n * KD)
                norm.rows(dve, n, h, x1)
                if first:
                    for k in range(KD):
                        dve.wait_ge(w1_top_ready, k + 1)
                        dve.tensor_tensor(w1[:, 1, k, :], w1_rows[k], w1[:, 0, k, :], ALU.subtract
                                          ).then_inc(w1_low_ready, 1)
                else:
                    second_residual(n - 1)
                for k in range(KD):
                    dve.wait_ge(h_copied, n * KD + k + 1)
                    dve.wait_ge(hT_top_ready, n * KD + k + 1)
                    dve.tensor_tensor(hT[:, 1, k, :], sig[:, k % 2, :], hT[:, 0, k, :], ALU.subtract
                                      ).then_inc(hT_ready, 1)
                for f in range(KF):
                    dve.wait_ge(sig_ready, n * KF + f + 1)
                    dve.scalar_tensor_tensor(out=ff[:, f, :], in0=f_bank[f % 2][:, :], scalar=column(cols, "b1", f),
                                             in1=sig[:, f % 2, :], op0=ALU.add, op1=ALU.mult).then_inc(ff_ready, 1)

            turns(dve, N, turn)
            second_residual(N - 1)

        @block.scalar
        def _(act):
            act.wait_ge(b1_ready, 1)

            def turn(n, first, last):
                for k in range(KD):
                    act.wait_ge(ctx_turned, n * KD + k + 1)
                    act.activation(ctxT[:, k, :], t_bank[k % 2][:, :], ACT.Identity, bias=column(cols, "bv", k)
                                   ).then_inc(ctxT_ready, 1)
                norm.deviations(act, n)
                if first:
                    for k in range(KD):
                        act.wait_ge(w1_in[k], 16)
                        act.activation(w1[:, 0, k, :], w1_rows[k], ACT.Copy).then_inc(w1_top_ready, 1)
                for k in range(KD):
                    act.wait_ge(h_turned, n * KD + k + 1)
                    if k >= 2:
                        act.wait_ge(hT_ready, n * KD + k - 1)
                    else:
                        wait(act, ff_ready, n * KF)
                    act.activation(sig[:, k % 2, :], t_bank[k % 2][:, :], ACT.Identity,
                                   bias=column(cols, "beta2", k), scale=column(cols, "g2", k)).then_inc(h_copied, 1)
                    act.activation(hT[:, 0, k, :], t_bank[k % 2][:, :], ACT.Identity,
                                   bias=column(cols, "beta2", k), scale=column(cols, "g2", k)
                                   ).then_inc(hT_top_ready, 1)
                for f in range(KF):
                    act.wait_ge(w1_done, n * KF + f + 1)
                    if f >= 2:
                        act.wait_ge(ff_ready, n * KF + f - 1)
                    else:
                        act.wait_ge(hT_ready, n * KD + KD)
                    act.activation(sig[:, f % 2, :], f_bank[f % 2][:, :], ACT.Sigmoid, bias=b1_sig[:, f:f + 1],
                                   scale=1.702).then_inc(sig_ready, 1)

            turns(act, N, turn)

        @block.tensor
        def _(pe):
            pe.wait_ge(ident_ready, 1)

            def transposes(n, src, turned, ready):
                for k in range(KD):
                    if k >= 2:
                        pe.wait_ge(ready, n * KD + k - 1)
                    for s in range(NS):
                        last = pe.transpose(t_bank[k % 2][:, s * P:(s + 1) * P], src[:, s, k * P:(k + 1) * P],
                                            ident[:, :])
                    last.then_inc(turned, 1)
                pe.wait_ge(ready, n * KD + KD)

            def second_product(n):
                pe.wait_ge(ff_ready, n * KF + KF)
                for s in range(NS):
                    pe.wait_ge(x1_ready, (n + 1) * NS + s + 1 if not isinstance(n, int) or n < N - 1 else N * NS)
                    for k in range(KF):
                        last = pe.matmul(y_bank[s][:, :], ff[:, k, s * P:(s + 1) * P], w2[:, k, :],
                                         start=(k == 0), stop=(k == KF - 1))
                    last.then_inc(w2_done, 1)

            def turn(n, first, last):
                pe.wait_ge(ctx_loaded, (n + 1) * (16 * NS))
                transposes(n, ctx_in, ctx_turned, ctxT_ready)
                if first:
                    pe.wait_ge(wo_in, 16)
                for s in range(NS):
                    if not first:
                        pe.wait_ge(x1b_ready, n * NS)
                    for k in range(KD):
                        out = pe.matmul(y_bank[s][:, :], ctxT[:, k, s * P:(s + 1) * P], wo[:, k, :],
                                        start=(k == 0), stop=(k == KD - 1))
                    out.then_inc(wo_done, 1)
                if not first:
                    second_product(n - 1)
                pe.wait_ge(norm.done, (n + 1) * Norm.SIZE)
                transposes(n, h, h_turned, hT_top_ready)
                if first:
                    pe.wait_ge(w1_low_ready, KD)
                    pe.wait_ge(w2_in, 16)
                for f in range(KF):
                    wait(pe, ff_ready, n * KF + f - 1 if f >= 2 else n * KF)
                    passes = [(wp, 0, k) for k in range(KD) for wp in (0, 1)] + [(0, 1, k) for k in range(KD)]
                    for i, (wp, hp, k) in enumerate(passes):
                        if f == 0 and hp == 1:
                            pe.wait_ge(hT_ready, n * KD + k + 1)
                        out = pe.matmul(f_bank[f % 2][:, :], w1[:, wp, k, f * P:(f + 1) * P], hT[:, hp, k, :],
                                        start=(i == 0), stop=(i == len(passes) - 1))
                    out.then_inc(w1_done, 1)

            turns(pe, N, turn)
            second_product(N - 1)


def adapter_phase(nc, S, B, io, x2_dram, out):
    NC = S // CH
    N = B * NC
    x2_tiles = x2_dram.rearrange("(n s p) d -> n p s d", s=NS, p=P)
    out_tiles = out.rearrange("b (c s p) d -> (b c) p s d", s=NS, p=P)
    K1 = 2 * KD

    with ExitStack() as ctx:
        sb = lambda name, shape, dt=F32: ctx.enter_context(nc.sbuf_tensor(name, shape, dt))
        sem = lambda name: ctx.enter_context(nc.semaphore(name))

        ident = sb("d_ident", [P, P])
        cols = sb("d_cols", [P, N_COLUMNS])
        ids_i = sb("d_ids_i", [P, 2, B], I32)
        ids = sb("d_ids", [P, 2, B])
        number = sb("d_number", [P, EXPERTS])
        number_i = sb("d_number_i", [P, EXPERTS], I32)
        clipped = sb("d_clipped", [P, B])
        valid = sb("d_valid", [P, 4, B])
        onehot = sb("d_onehot", [P, B, EXPERTS])
        case = sb("d_case", [P, 3, B])
        not_sr = sb("d_not_sr", [P, B])
        angle = sb("d_angle", [P, 4, 2, 2, B])
        turned = sb("d_turned", [P, 2, 2, B])
        minus_sin = sb("d_minus_sin", [P, 2, B])
        vecs = sb("d_vecs", [P, 2, EXPERTS])
        picked = sb("d_picked", [P, EXPERTS])
        sums = sb("d_sums", [P, 2])
        expert_bias = sb("d_expert_bias", [P, B])
        expertT = [sb(f"d_expertT{b}", [P, AD]) for b in range(B)]
        downT = sb("d_downT", [P, KD, AD])
        upT = sb("d_upT", [P, D])
        up_b = sb("d_up_b", [P, D])
        ln1 = sb("d_ln1", [P, 2, D])
        ln3 = sb("d_ln3", [P, 2, D])
        rot = [sb(f"d_rot{b}", [P, 3, D]) for b in range(B)]
        w_first = [sb(f"d_w_first{b}", [P, KD, 2 * D]) for b in range(B)]
        w_mid = sb("d_w_mid", [P, K1, D])
        w_last = [sb(f"d_w_last{b}", [P, KD, D]) for b in range(B)]
        b_first = sb("d_b_first", [P, B, K1])
        b_last = [sb(f"d_b_last{b}", [P, D]) for b in range(B)]

        x2 = sb("d_x2", [P, NS, D])
        x2T = sb("d_x2T", [P, KD, CH])
        hid = sb("d_hid", [P, CH])
        hid2 = sb("d_hid2", [P, CH])
        x3 = sb("d_x3", [P, NS, D])
        x4 = sb("d_x4", [P, NS, D])
        swapped = sb("d_swapped", [P, D])
        x4b = sb("d_x4b", [P, NS, D])
        x4T = sb("d_x4T", [P, KD, CH])
        h1 = sb("d_h1", [P, K1, CH])
        g2_kept = sb("d_g2_kept", [P, 4, CH])
        g2, kept = g2_kept[:, 0:2, :], g2_kept[:, 2:4, :]
        h2 = sb("d_h2", [P, KD, CH])
        y = sb("d_y", [P, NS, D])
        staged = [h1[:, KD * i:KD * (i + 1), :] for i in range(2)] + [h2[:, :, :], g2_kept[:, :, :]]
        experts = y[:, :, :].rearrange("p s (e o) -> p (s e) o", o=AD)
        t_bank = [ctx.enter_context(nc.psum_tensor(f"d_t_bank{i}", [P, BANK], F32)) for i in range(2)]
        y_bank = [ctx.enter_context(nc.psum_tensor(f"d_y_bank{i}", [P, BANK], F32)) for i in range(NS)]
        w_bank = [ctx.enter_context(nc.psum_tensor(f"d_w_bank{i}", [P, BANK], F32)) for i in range(2)]
        norm1, norm3 = Norm(sb, sem, "d_norm1"), Norm(sb, sem, "d_norm3")

        params_in, experts_in, up_in = sem("d_params_in"), sem("d_experts_in"), sem("d_up_in")
        first_in, last_in = sem("d_first_in"), sem("d_last_in")
        fixed_in, mid_in, rows_in = sem("d_fixed_in"), sem("d_mid_in"), sem("d_rows_in")
        x2_loaded, y_stored = sem("d_x2_loaded"), sem("d_y_stored")
        zeroed, ident_ready, numbered = sem("d_zeroed"), sem("d_ident_ready"), sem("d_numbered")
        prep, turned_done = sem("d_prep"), sem("d_turned_done")
        x2_turned, x2T_ready, up_b_added = sem("d_x2_turned"), sem("d_x2T_ready"), sem("d_up_b_added")
        down_done, hid_ready, expert_done, hid2_ready = (sem("d_down_done"), sem("d_hid_ready"),
                                                         sem("d_expert_done"), sem("d_hid2_ready"))
        up_done, x3_ready = sem("d_up_done"), sem("d_x3_ready")
        swap_done, rot_done, x4_ready, x4b_ready = (sem("d_swap_done"), sem("d_rot_done"), sem("d_x4_ready"),
                                                    sem("d_x4b_ready"))
        x4_turned, x4T_ready = sem("d_x4_turned"), sem("d_x4T_ready")
        first_done, h1_ready, mid_done, g2_ready = (sem("d_first_done"), sem("d_h1_ready"), sem("d_mid_done"),
                                                    sem("d_g2_ready"))
        kept_ready, h2_ready, last_done = sem("d_kept_ready"), sem("d_h2_ready"), sem("d_last_done")
        y_sum, y_scaled, y_ready = sem("d_y_sum"), sem("d_y_scaled"), sem("d_y_ready")
        sp_gate = sem("d_sp_gate")

        block = ctx.enter_context(nc.Block())

        @block.sync
        def _(sp):
            row = lambda name: io[name].rearrange("(a n) -> a n", a=1)
            tiled = lambda name: io[name].rearrange("(k p) n -> p k n", p=P)
            sp.dma_start(x2[:, :, :], x2_tiles[0]).then_inc(x2_loaded, 16)
            sp.dma_start(downT[:, :, :], tiled("down_WT")).then_inc(fixed_in, 16)
            sp.dma_start(cols[:, :], io["cols"]).then_inc(params_in, 16)
            for i, name in enumerate(("domain", "condition")):
                sp.dma_start(ids_i[:, i, :], row(name).to_broadcast([P, B])).then_inc(params_in, 16)
            for i, name in enumerate(("theta", "phi")):
                for quarter in range(2):
                    sp.dma_start(angle[:, 0, quarter, i, :], row(name).to_broadcast([P, B])).then_inc(params_in, 16)
            sp.dma_start(vecs[:, 0, :], io["expert_bT"]).then_inc(params_in, 16)
            sp.dma_start(vecs[:, 1, :], io["domain_embT"]).then_inc(params_in, 16)
            sp.dma_start(experts, io["expert_WT"]).then_inc(experts_in, 16)
            sp.dma_start(upT[:, :], io["up_WT"]).then_inc(up_in, 16)
            for i, name in enumerate(("ln1_gamma", "ln1_beta")):
                sp.dma_start(ln1[:, i, :], row(name).to_broadcast([P, D])).then_inc(rows_in, 16)
            sp.dma_start(up_b[:, :], row("up_b").to_broadcast([P, D])).then_inc(rows_in, 16)
            sp.dma_start(w_first[0][:, :, :], tiled("w1_sr")).then_inc(first_in, 16)
            for i, name in enumerate(("w1_nr", "w1_tsr")):
                sp.dma_start(staged[i], tiled(name)).then_inc(first_in, 16)
            sp.dma_start(w_last[0][:, :, :], tiled("w3_sr")).then_inc(last_in, 16)
            for i, name in enumerate(("w2_nr", "w2_tsr")):
                sp.dma_start(staged[2 + i], tiled(name)).then_inc(last_in, 16)
            for i, name in enumerate(("b3_sr", "b2_nr", "b2_tsr")):
                sp.dma_start(x4b[:, i, :], row(name).to_broadcast([P, D])).then_inc(last_in, 16)
            for i, name in enumerate(("ln3_gamma", "ln3_beta")):
                sp.dma_start(ln3[:, i, :], row(name).to_broadcast([P, D])).then_inc(last_in, 16)
            sp.dma_start(w_mid[:, :, :], tiled("w2_sr")).then_inc(mid_in, 16)

            def load(n):
                wait_apart(sp, x3_ready, n * NS, sp_gate)
                sp.dma_start(x2[:, :, :], x2_tiles[n]).then_inc(x2_loaded, 16)

            def store(n):
                wait_apart(sp, y_ready, n * NS + NS, sp_gate)
                sp.dma_start(out_tiles[n], y[:, :, :]).then_inc(y_stored, 16)

            if N > 1:
                load(1)
            if N > 2:
                with sp.Fori(0, N - 2) as n:
                    load(n + 2)
                    store(n)
            for n in range(max(0, N - 2), N):
                store(n)
            sp.wait_ge(y_stored, 16 * N)

        @block.gpsimd
        def _(pool):
            make_identity(pool, ident, zeroed, ident_ready)
            pool.iota(number_i[:, :], pattern=[[1, EXPERTS]], base=0, channel_multiplier=0).then_inc(numbered, 1)
            pool.wait_ge(rows_in, 16 * 3)

            def residual_bias(n):
                pool.wait_ge(x2_loaded, n * 16 + 16)
                pool.wait_ge(x2_turned, n * KD + KD)
                for s in range(NS):
                    pool.tensor_tensor(x2[:, s, :], x2[:, s, :], up_b[:, :], ALU.add).then_inc(up_b_added, 1)

            def rotation(n, b):
                for s in range(NS):
                    pool.wait_ge(norm1.done, n * Norm.SIZE + Norm.N_VAR + 1 + s + 1)
                    if s:
                        pool.wait_ge(x4_ready, n * NS + s)
                    else:
                        wait(pool, x4_ready, n * NS)
                    pairs = lambda ap: ap.rearrange("p (g u) -> p g u", u=2)
                    for u in range(2):
                        pool.tensor_tensor(pairs(swapped[:, :])[:, :, u], pairs(x3[:, s, :])[:, :, 1 - u],
                                           pairs(rot[b][:, 1, :])[:, :, u], ALU.mult).then_inc(swap_done, 1)

            def last_bias(n, b):
                if isinstance(n, int) and n == 0:
                    pool.wait_ge(prep, N_PREP)
                wait(pool, y_sum, n * NS)
                pool.wait_ge(x4_ready, n * NS + NS)
                for s in range(NS):
                    pool.tensor_tensor(x4b[:, s, :], x4[:, s, :], b_last[b][:, :], ALU.add).then_inc(x4b_ready, 1)

            residual_bias(0)
            pool.wait_ge(prep, N_ROTATION)
            rotation(0, 0)

            def chunk(n, b, b_next):
                last_bias(n, b)
                if b_next is not None:
                    residual_bias(n + 1)
                    rotation(n + 1, b_next)

            batch_turns(pool, B, NC, chunk)

        @block.vector
        def _(dve):
            st = Steps(prep)
            done = lambda: dve.wait_ge(prep, st.n)
            dve.wait_ge(params_in, 16 * 9)
            st.mark(dve.tensor_scalar(angle[:, 1, :, :, :], angle[:, 0, :, :, :], 1.0 / (2 * math.pi), ROUND,
                                      ALU.mult, ALU.add))
            done()
            st.mark(dve.tensor_scalar(angle[:, 2, :, :, :], angle[:, 1, :, :, :], ROUND, None, ALU.subtract))
            for part in (TWO_PI_1, TWO_PI_2, TWO_PI_3):
                done()
                st.mark(dve.scalar_tensor_tensor(out=angle[:, 0, :, :, :], in0=angle[:, 2, :, :, :], scalar=-part,
                                                 in1=angle[:, 0, :, :, :], op0=ALU.mult, op1=ALU.add))
            done()
            st.mark(dve.tensor_scalar(angle[:, 0, 1, :, :], angle[:, 0, 1, :, :], math.pi / 2, None, ALU.add))
            done()
            st.mark(dve.tensor_scalar(angle[:, 1, 1, :, :], angle[:, 0, 1, :, :], math.pi, -2 * math.pi,
                                      ALU.is_gt, ALU.mult))
            done()
            st.mark(dve.tensor_tensor(angle[:, 0, 1, :, :], angle[:, 0, 1, :, :], angle[:, 1, 1, :, :], ALU.add))
            done()
            k = st.mark(dve.tensor_scalar(angle[:, 3, :, :, :], angle[:, 0, :, :, :], -PI_INSIDE, PI_INSIDE,
                                          ALU.max, ALU.min))
            assert k == N_TURN
            dve.wait_ge(numbered, 1)
            st.mark(dve.tensor_copy(number[:, :], number_i[:, :]))
            st.mark(dve.tensor_copy(ids[:, :, :], ids_i[:, :, :]))
            done()
            st.mark(dve.tensor_scalar(clipped[:, :], ids[:, 0, :], 0.0, EXPERTS - 1.0, ALU.max, ALU.min))
            for i in range(3):
                st.mark(dve.tensor_scalar(case[:, i, :], ids[:, 1, :], float(i), None, ALU.is_equal))
            done()
            st.mark(dve.tensor_tensor(valid[:, 0, :], clipped[:, :], ids[:, 0, :], ALU.is_equal))
            st.mark(dve.tensor_scalar(not_sr[:, :], case[:, 2, :], -1.0, 1.0, ALU.mult, ALU.add))
            done()
            st.mark(dve.tensor_scalar(valid[:, 1, :], valid[:, 0, :], -1.0, 1.0, ALU.mult, ALU.add))
            for b in range(B):
                st.mark(dve.tensor_scalar(onehot[:, b, :], number[:, :], clipped[:, b:b + 1], None, ALU.is_equal))
            def expert(b):
                done()
                st.mark(dve.tensor_scalar(expertT[b][:, :], experts[:, 0, :], onehot[:, b, 0:1], None, ALU.mult))
                for e in range(1, EXPERTS):
                    done()
                    st.mark(dve.scalar_tensor_tensor(out=expertT[b][:, :], in0=experts[:, e, :],
                                                     scalar=onehot[:, b, e:e + 1], in1=expertT[b][:, :],
                                                     op0=ALU.mult, op1=ALU.add))
                done()
                st.mark(dve.tensor_scalar(expertT[b][:, :], expertT[b][:, :], valid[:, 0, b:b + 1], None, ALU.mult))
                done()
                st.mark(dve.scalar_tensor_tensor(out=expertT[b][:, :], in0=ident[:, :], scalar=valid[:, 1, b:b + 1],
                                                 in1=expertT[b][:, :], op0=ALU.mult, op1=ALU.add))
                for i in range(2):
                    done()
                    st.mark(dve.tensor_tensor(picked[:, :], vecs[:, i, :], onehot[:, b, :], ALU.mult))
                    done()
                    st.mark(dve.tensor_reduce(sums[:, i:i + 1], picked[:, :], AX.X, ALU.add))
                done()
                st.mark(dve.scalar_tensor_tensor(out=expert_bias[:, b:b + 1], in0=sums[:, 0:1],
                                                 scalar=valid[:, 0, b:b + 1], in1=sums[:, 1:2],
                                                 op0=ALU.mult, op1=ALU.add))

            quads = lambda ap: ap.rearrange("p (g t u) -> p g t u", t=2, u=2)

            def turned_gain(b):
                for t in range(2):
                    cos, sin, neg = turned[:, 1, t, b:b + 1], turned[:, 0, t, b:b + 1], minus_sin[:, t, b:b + 1]
                    st.mark(dve.tensor_scalar(quads(rot[b][:, 0, :])[:, :, t, :], quads(ln1[:, 0, :])[:, :, t, :],
                                              cos, None, ALU.mult))
                    st.mark(dve.tensor_scalar(quads(rot[b][:, 2, :])[:, :, t, :], quads(ln1[:, 1, :])[:, :, t, :],
                                              cos, None, ALU.mult))
                    done()
                    for u, factor in ((0, sin), (1, neg)):
                        st.mark(dve.tensor_scalar(quads(rot[b][:, 1, :])[:, :, t, u],
                                                  quads(ln1[:, 0, :])[:, :, t, 1 - u], factor, None, ALU.mult))
                        st.mark(dve.scalar_tensor_tensor(out=quads(rot[b][:, 2, :])[:, :, t, u],
                                                         in0=quads(ln1[:, 1, :])[:, :, t, 1 - u], scalar=factor,
                                                         in1=quads(rot[b][:, 2, :])[:, :, t, u],
                                                         op0=ALU.mult, op1=ALU.add))

            def choose(made):
                for b in reversed(range(B)):
                    pick = lambda i: case[:, i, b:b + 1]
                    done()
                    for whole, out, _, _ in made:
                        st.mark(dve.tensor_scalar(out[b], whole, pick(2), None, ALU.mult))
                    for i in range(2):
                        done()
                        for _, out, part, two in made:
                            st.mark(dve.scalar_tensor_tensor(out=part(out[b]), in0=two[i], scalar=pick(i),
                                                             in1=part(out[b]), op0=ALU.mult, op1=ALU.add))

            whole = lambda ap: ap
            at = {name: slice(COLUMNS[name][0], COLUMNS[name][0] + COLUMNS[name][1])
                  for name in ("b1_sr", "b1_nr", "b1_tsr")}
            dve.wait_ge(experts_in, 16)
            dve.wait_ge(ident_ready, 1)
            expert(0)
            assert st.n == N_EXPERT, st.n
            dve.wait_ge(rows_in, 16 * 3)
            dve.wait_ge(turned_done, 1)
            st.mark(dve.tensor_scalar(minus_sin[:, :, :], turned[:, 0, :, :], -1.0, None, ALU.mult))
            done()
            turned_gain(0)
            assert st.n == N_ROTATION, st.n

            def adapter_rows(n, b):
                wait(dve, x4_turned, n * KD)
                wait(dve, x4b_ready, n * NS)
                for s in range(NS):
                    dve.wait_ge(up_done, n * NS + s + 1)
                    dve.wait_ge(up_b_added, n * NS + s + 1)
                    dve.tensor_tensor(x3[:, s, :], y_bank[s][:, :], x2[:, s, :], ALU.add).then_inc(x3_ready, 1)
                    dve.wait_ge(x3_ready, n * NS + s + 1)
                    norm1.statistics(dve, s, x3[:, s, :])
                norm1.rows(dve, n, x3, x3)
                for s in range(NS):
                    r = (n * NS + s) * 2
                    dve.wait_ge(norm1.done, n * Norm.SIZE + Norm.N_VAR + 2 + s)
                    dve.tensor_tensor(x4[:, s, :], x3[:, s, :], rot[b][:, 0, :], ALU.mult).then_inc(rot_done, 1)
                    dve.wait_ge(rot_done, r + 1)
                    dve.tensor_tensor(x4[:, s, :], x4[:, s, :], rot[b][:, 2, :], ALU.add).then_inc(rot_done, 1)
                    dve.wait_ge(rot_done, r + 2)
                    dve.wait_ge(swap_done, r + 2)
                    dve.tensor_tensor(x4[:, s, :], x4[:, s, :], swapped[:, :], ALU.add).then_inc(x4_ready, 1)

            def middle(n, b):
                for k in range(KD):
                    i = n * KD + k
                    dve.wait_ge(h1_ready, n * K1 + k + 1)
                    if k >= 2:
                        dve.wait_ge(h2_ready, i - 1)
                    dve.tensor_scalar(kept[:, k % 2, :], h1[:, k, :], not_sr[:, b:b + 1], None, ALU.mult
                                      ).then_inc(kept_ready, 1)
                    dve.wait_ge(g2_ready, i + 1)
                    dve.wait_ge(kept_ready, i + 1)
                    dve.scalar_tensor_tensor(out=h2[:, k, :], in0=g2[:, k % 2, :], scalar=case[:, 2, b:b + 1],
                                             in1=kept[:, k % 2, :], op0=ALU.mult, op1=ALU.add).then_inc(h2_ready, 1)

            def result(n):
                wait(dve, y_stored, n * 16)
                for s in range(NS):
                    dve.wait_ge(last_done, n * NS + s + 1)
                    dve.wait_ge(x4b_ready, n * NS + s + 1)
                    dve.tensor_tensor(y[:, s, :], y_bank[s][:, :], x4b[:, s, :], ALU.add).then_inc(y_sum, 1)
                    dve.wait_ge(y_sum, n * NS + s + 1)
                    norm3.statistics(dve, s, y[:, s, :])
                norm3.rows(dve, n, y, y)
                for s in range(NS):
                    dve.wait_ge(norm3.done, n * Norm.SIZE + Norm.N_VAR + 2 + s)
                    dve.tensor_tensor(y[:, s, :], y[:, s, :], ln3[:, 0, :], ALU.mult).then_inc(y_scaled, 1)
                    dve.wait_ge(y_scaled, n * NS + s + 1)
                    dve.tensor_tensor(y[:, s, :], y[:, s, :], ln3[:, 1, :], ALU.add).then_inc(y_ready, 1)

            adapter_rows(0, 0)
            dve.wait_ge(first_in, 16 * 3)
            choose(((w_first[0][:, :, :], [w[:, :, :] for w in w_first], lambda ap: ap[:, :, 0:D], staged[0:2]),
                    (cols[:, at["b1_sr"]], [b_first[:, b, :] for b in range(B)], lambda ap: ap[:, 0:KD],
                     (cols[:, at["b1_nr"]], cols[:, at["b1_tsr"]]))))
            assert st.n == N_FIRST, st.n
            dve.wait_ge(last_in, 16 * 8)
            choose(((w_last[0][:, :, :], [w[:, :, :] for w in w_last], whole, staged[2:4]),
                    (x4b[:, 0, :], [w[:, :] for w in b_last], whole, (x4b[:, 1, :], x4b[:, 2, :]))))
            for b in range(1, B):
                expert(b)
                turned_gain(b)
            done()
            assert st.n == N_PREP, st.n

            def chunk(n, b, b_next):
                if b_next is not None:
                    adapter_rows(n + 1, b_next)
                middle(n, b)
                result(n)

            batch_turns(dve, B, NC, chunk)

        @block.scalar
        def _(act):
            act.wait_ge(prep, N_TURN)
            act.activation(turned[:, :, :, :], angle[:, 3, :, :, :], ACT.Sin).then_inc(turned_done, 1)

            def copy_turned(n, dst, turned_sem, ready):
                for k in range(KD):
                    act.wait_ge(turned_sem, n * KD + k + 1)
                    act.activation(dst[:, k, :], t_bank[k % 2][:, :], ACT.Copy).then_inc(ready, 1)

            def adapter_down(n):
                copy_turned(n, x2T, x2_turned, x2T_ready)
                act.wait_ge(down_done, n + 1)
                act.activation(hid[:, :], w_bank[0][:, :], ACT.Gelu, bias=column(cols, "down_b", 0)
                               ).then_inc(hid_ready, 1)

            def adapter_expert(n, b):
                act.wait_ge(expert_done, n + 1)
                act.activation(hid2[:, :], w_bank[1][:, :], ACT.Identity, bias=expert_bias[:, b:b + 1]
                               ).then_inc(hid2_ready, 1)

            def first_layer(n, b):
                wait(act, h2_ready, n * KD)
                for j in range(K1):
                    act.wait_ge(first_done, n * K1 + j + 1)
                    act.activation(h1[:, j, :], w_bank[j % 2][:, :], ACT.Gelu, bias=b_first[:, b, j:j + 1]
                                   ).then_inc(h1_ready, 1)

            def middle_layer(n):
                if isinstance(n, int) and n == 0:
                    act.wait_ge(prep, N_PREP)
                for j in range(KD):
                    act.wait_ge(mid_done, n * KD + j + 1)
                    if j >= 2:
                        act.wait_ge(h2_ready, n * KD + j - 1)
                    act.activation(g2[:, j % 2, :], w_bank[j % 2][:, :], ACT.Gelu, bias=column(cols, "b2_sr", j)
                                   ).then_inc(g2_ready, 1)

            def chunk(n, b, b_next):
                ahead = b_next is not None
                if ahead:
                    adapter_down(n + 1)
                first_layer(n, b)
                if ahead:
                    adapter_expert(n + 1, b_next)
                    norm1.deviations(act, n + 1)
                middle_layer(n)
                if ahead:
                    copy_turned(n + 1, x4T, x4_turned, x4T_ready)
                norm3.deviations(act, n)

            act.wait_ge(params_in, 16 * 9)
            adapter_down(0)
            act.wait_ge(prep, N_EXPERT)
            adapter_expert(0, 0)
            norm1.deviations(act, 0)
            copy_turned(0, x4T, x4_turned, x4T_ready)
            batch_turns(act, B, NC, chunk)

        @block.tensor
        def _(pe):
            pe.wait_ge(ident_ready, 1)
            pe.wait_ge(fixed_in, 16)

            def transposes(n, src, turned_sem, ready):
                for k in range(KD):
                    if k >= 2:
                        pe.wait_ge(ready, n * KD + k - 1)
                    for s in range(NS):
                        out = pe.transpose(t_bank[k % 2][:, s * P:(s + 1) * P], src[:, s, k * P:(k + 1) * P],
                                           ident[:, :])
                    out.then_inc(turned_sem, 1)
                pe.wait_ge(ready, n * KD + KD)

            def adapter_down(n):
                pe.wait_ge(x2_loaded, n * 16 + 16)
                transposes(n, x2, x2_turned, x2T_ready)
                wait(pe, g2_ready, (n - 1) * KD)
                for k in range(KD):
                    out = pe.matmul(w_bank[0][:, :], downT[:, k, :], x2T[:, k, :], start=(k == 0), stop=(k == KD - 1))
                out.then_inc(down_done, 1)
                pe.wait_ge(hid_ready, n + 1)

            def adapter_expert(n, b):
                wait(pe, h1_ready, n * K1)
                pe.matmul(w_bank[1][:, :], expertT[b][:, :], hid[:, :], start=True, stop=True).then_inc(expert_done, 1)

            def adapter_up(n):
                pe.wait_ge(hid2_ready, n + 1)
                wait(pe, y_sum, (n - 1) * NS)
                for s in range(NS):
                    pe.matmul(y_bank[s][:, :], hid2[:, s * P:(s + 1) * P], upT[:, :], start=True, stop=True
                              ).then_inc(up_done, 1)

            def first_layer(n, b):
                for j in range(K1):
                    if j >= 2:
                        pe.wait_ge(h1_ready, n * K1 + j - 1)
                    else:
                        wait(pe, g2_ready, n * KD)
                    for k in range(KD):
                        out = pe.matmul(w_bank[j % 2][:, :], w_first[b][:, k, j * P:(j + 1) * P], x4T[:, k, :],
                                        start=(k == 0), stop=(k == KD - 1))
                    out.then_inc(first_done, 1)

            def middle_layer(n, ahead):
                for j in range(KD):
                    if j >= 2:
                        pe.wait_ge(g2_ready, n * KD + j - 1)
                    else:
                        pe.wait_ge(h1_ready, n * K1 + K1)
                    if j == 1 and ahead:
                        pe.wait_ge(hid2_ready, n + 2)
                    for k in range(K1):
                        out = pe.matmul(w_bank[j % 2][:, :], w_mid[:, k, j * P:(j + 1) * P], h1[:, k, :],
                                        start=(k == 0), stop=(k == K1 - 1))
                    out.then_inc(mid_done, 1)

            def last_layer(n, b, ahead):
                pe.wait_ge(h2_ready, n * KD + KD)
                for s in range(NS):
                    pe.wait_ge(x3_ready, (n + 1) * NS + s + 1 if ahead else (n + 1) * NS)
                    for k in range(KD):
                        out = pe.matmul(y_bank[s][:, :], h2[:, k, s * P:(s + 1) * P], w_last[b][:, k, :],
                                        start=(k == 0), stop=(k == KD - 1))
                    out.then_inc(last_done, 1)

            def chunk(n, b, b_next):
                ahead = b_next is not None
                first = isinstance(n, int) and n == 0
                if ahead:
                    adapter_down(n + 1)
                if first:
                    pe.wait_ge(prep, N_FIRST)
                first_layer(n, b)
                if ahead:
                    adapter_expert(n + 1, b_next)
                    adapter_up(n + 1)
                if first:
                    pe.wait_ge(mid_in, 16)
                middle_layer(n, ahead)
                if first:
                    pe.wait_ge(prep, N_PREP)
                last_layer(n, b, ahead)
                if ahead:
                    pe.wait_ge(x4_ready, (n + 2) * NS)
                    transposes(n + 1, x4, x4_turned, x4T_ready)

            adapter_down(0)
            pe.wait_ge(prep, N_EXPERT)
            adapter_expert(0, 0)
            pe.wait_ge(up_in, 16)
            adapter_up(0)
            pe.wait_ge(x4_ready, NS)
            transposes(0, x4, x4_turned, x4T_ready)
            batch_turns(pe, B, NC, chunk)


N_TURN = 9
N_EXPERT = N_TURN + 11 + 23
N_ROTATION = N_EXPERT + 1 + 12
N_FIRST = N_ROTATION + 2 * 6
N_PREP = N_FIRST + 2 * 6 + 35


def frequencies():
    half = D // 2
    f = np.exp(np.arange(half, dtype=np.float32) * np.float32(-math.log(10000.0) / (half - 1)))
    return np.concatenate([f, f]).reshape(KD, P).T


def block_program(nc, S, B, io, out):
    scratch = lambda name, shape, dt=F32: nc.dram_tensor(name, shape, dt, kind="Internal").ap()
    xada = scratch("xada", (B * S, D))
    q2 = scratch("q2", (2, B * D, S), F32)
    k2 = scratch("k2", (2, B * D, S), F32)
    v = scratch("v", (B * S // CH, H, P, NS * VP), BF16)
    mask8 = scratch("mask8", (B * S, S // 2), BF16)
    context = scratch("context", (B * H * (S // P), P, HD))
    x2 = scratch("x2", (B * S, D))
    project_phase(nc, S, B, io, xada, q2, k2, v, mask8)
    attention_phase(nc, S, B, io, q2, k2, v, mask8, context)
    feed_forward_phase(nc, S, B, io, xada, context, x2)
    adapter_phase(nc, S, B, io, x2, out)


_NAMES = {
    "x": "x", "fside": "fside_Bx16xSxS_0", "mask": "mask_Bx1xSxS_bk0", "timestep": "itok_B_34_63",
    "domain": "itok_B_0_15", "condition": "itok_B_0_2", "theta": "condB_theta", "phi": "condB_phi",
    "W_ada": "L0_cond_W_ada", "Wq": "L0_cond_Wq", "Wk": "L0_cond_Wk", "Wv": "L0_cond_Wv", "Wo": "L0_cond_Wo",
    "W1": "L0_cond_W1", "W2": "L0_cond_W2", "bo": "L0_cond_bo", "b2": "L0_cond_b2", "up_b": "L1_cond_up_b",
    "ln1_gamma": "L1_cond_ln_gamma", "ln1_beta": "L1_cond_ln_beta", "ln3_gamma": "L3_cond_gamma",
    "ln3_beta": "L3_cond_beta", "w1_nr": "L3_cond_w1_nr", "w2_nr": "L3_cond_w2_nr", "w1_tsr": "L3_cond_w1_tsr",
    "w2_tsr": "L3_cond_w2_tsr", "w1_sr": "L3_cond_w1_sr", "w2_sr": "L3_cond_w2_sr", "w3_sr": "L3_cond_w3_sr",
    "b2_nr": "L3_cond_b2_nr", "b2_tsr": "L3_cond_b2_tsr", "b3_sr": "L3_cond_b3_sr",
}
_COLUMN_NAMES = {
    "b_ada": "L0_cond_b_ada", "bq": "L0_cond_bq", "bk": "L0_cond_bk", "bv": "L0_cond_bv", "b1": "L0_cond_b1",
    "g2": "L0_cond_g2", "beta2": "L0_cond_beta2", "down_b": "L1_cond_down_b", "b1_sr": "L3_cond_b1_sr",
    "b2_sr": "L3_cond_b2_sr", "b1_nr": "L3_cond_b1_nr", "b1_tsr": "L3_cond_b1_tsr",
}


def kernel(**inputs):
    import numpy as _np
    import concourse.bacc as _bacc
    from concourse import mybir as _mybir
    from concourse.bass_utils import run_bass_kernel_spmd as _run

    nc = _bacc.Bacc("TRN2", target_bir_lowering=False, num_devices=1)
    arrays, io = {}, {}

    def give(name, a):
        a = _np.ascontiguousarray(a)
        arrays[f"in_{name}"] = a
        io[name] = nc.dram_tensor(f"in_{name}", a.shape, _mybir.dt.from_np(a.dtype), kind="ExternalInput").ap()

    array = lambda name: _np.asarray(inputs[name])
    for name, given in _NAMES.items():
        give(name, array(given))
    give("cols", _np.concatenate([array(_COLUMN_NAMES[c]).reshape(-1, P).T for c in COLUMNS], axis=1))
    give("freqs", frequencies())
    give("down_WT", array("L1_cond_down_W").T)
    give("up_WT", array("L1_cond_up_W").T)
    give("expert_WT", array("L1_cond_expert_W").transpose(2, 0, 1))
    give("expert_bT", array("L1_cond_expert_b").T)
    give("domain_embT", array("L1_cond_domain_emb").T)
    B, S, _ = inputs["x"].shape
    out = nc.dram_tensor("out_0", (B, S, D), _mybir.dt.float32, kind="ExternalOutput").ap()
    block_program(nc, S, B, io, out)
    r = _run(nc, [arrays], core_ids=[0])
    return r.results[0]["out_0"]
```
